# Optimizing a Trainium2 kernel written in Bass

```python
import numpy as np
import jax
import jax.numpy as jnp

def _softmax(x, axis=-1):
    return jax.nn.softmax(x, axis=axis)

def _gelu(x):
    return jax.nn.gelu(x, approximate=True)

def _silu(x):
    return jax.nn.silu(x)

def _sigmoid(x):
    return jax.nn.sigmoid(x)

def _layernorm(x, axis=-1, eps=1e-05):
    m = jnp.mean(x, axis=axis, keepdims=True)
    v = jnp.var(x, axis=axis, keepdims=True)
    return (x - m) / jnp.sqrt(v + eps)

def _scatter_add(tgt, idx, src, axis=0):
    return tgt.at[idx].add(src)

def _segment_sum(src, seg, n):
    return jax.ops.segment_sum(src, seg, n)
kernel_name = 'mk_gps_d2_gnn_r8_5d4e6e'

def setup_inputs(seed: int=0):
    np.random.seed(seed)
    _w = jnp.asarray

    def _rec_inputs():
        import jax
        import jax.numpy as jnp
        _gk = jax.random.key(seed)
        x = 7.22e-05 + 1 * jax.random.normal(jax.random.fold_in(_gk, 1), (2048, 512), jnp.float32)
        src = jax.random.randint(jax.random.fold_in(_gk, 2), (32768,), 0, 2048, jnp.int32)
        dst = jnp.minimum((2048 * jax.random.uniform(jax.random.fold_in(_gk, 3), (32768,)) ** 2.0).astype(jnp.int32), 16383)
        _o = jnp.argsort(dst, stable=True)
        src = src[_o]
        dst = dst[_o]
        edge_attr_16 = -0.000585658 + 0.999949 * jax.random.normal(jax.random.fold_in(_gk, 12), (32768, 16), jnp.float32)
        return (x, src, dst, edge_attr_16)
    x, src, dst, edge_attr_16 = _rec_inputs()

    def _L0_gnn_setup():
        import jax, jax.numpy as jnp
        import numpy as np
        B = 32
        N = 512
        HID = 512
        H = 8
        E = 32768
        ED = 16
        key = jax.random.key(seed)
        ks = jax.random.split(key, 12)
        x = jax.random.normal(ks[0], (B * N, HID), jnp.float32)
        batch = jnp.repeat(jnp.arange(B, dtype=jnp.int64), N)
        g = jax.random.randint(ks[1], (E,), 0, B)
        src = g * N + jax.random.randint(ks[2], (E,), 0, N)
        dst = g * N + jax.random.randint(ks[3], (E,), 0, N)
        edge_index = jnp.stack([src, dst]).astype(jnp.int64)
        edge_attr = jax.random.normal(ks[4], (E, ED), jnp.float32)
        s = 1.0 / np.sqrt(HID).astype(np.float32)
        Wq = jax.random.normal(ks[5], (HID, HID), jnp.float32) * s
        Wk = jax.random.normal(ks[6], (HID, HID), jnp.float32) * s
        Wv = jax.random.normal(ks[7], (HID, HID), jnp.float32) * s
        Wo = jax.random.normal(ks[8], (HID, HID), jnp.float32) * s
        We = jax.random.normal(ks[9], (ED, H), jnp.float32) * (1.0 / np.sqrt(ED).astype(np.float32))
        bq = jnp.zeros((HID,), jnp.float32)
        bk = jnp.zeros((HID,), jnp.float32)
        bv = jnp.zeros((HID,), jnp.float32)
        bo = jnp.zeros((HID,), jnp.float32)
        be = jnp.zeros((H,), jnp.float32)
        return dict(x=x, batch=batch, edge_index=edge_index, edge_attr=edge_attr, Wq=Wq, bq=bq, Wk=Wk, bk=bk, Wv=Wv, bv=bv, Wo=Wo, bo=bo, We=We, be=be, num_graphs=B)
    _L0_gnn_all = _L0_gnn_setup()
    _L0_gnn_in = {k: v for k, v in _L0_gnn_all.items() if k in ('Wq', 'bq', 'Wk', 'bk', 'Wv', 'bv', 'Wo', 'bo', 'We', 'be')}
    del _L0_gnn_all

    def _L0_mix_setup():
        import jax, jax.numpy as jnp
        import numpy as np
        HEADS = 8
        DIM_HEAD = 64
        DIM = 512
        INNER = HEADS * DIM_HEAD
        SCALE = DIM_HEAD ** (-0.5)

        def _feature_map(t):
            return jax.nn.elu(t) + 1.0
        key = jax.random.key(seed)
        k1, k2, k3, k4 = jax.random.split(key, 4)
        b, n = (8, 512)
        x = jax.random.normal(k1, (b, n, DIM), dtype=jnp.float32)
        w_qkv = jax.random.normal(k2, (INNER * 3, DIM), dtype=jnp.float32) * DIM ** (-0.5)
        w_out = jax.random.normal(k3, (DIM, INNER), dtype=jnp.float32) * INNER ** (-0.5)
        b_out = jax.random.normal(k4, (DIM,), dtype=jnp.float32) * 0.01
        return {'x': x, 'w_qkv': w_qkv, 'w_out': w_out, 'b_out': b_out}
    _L0_mix_all = _L0_mix_setup()
    _L0_mix_in = {k: v for k, v in _L0_mix_all.items() if k in ('w_qkv', 'w_out', 'b_out')}
    del _L0_mix_all

    def _L0_ffn_setup():
        import jax, jax.numpy as jnp
        import numpy as np
        B, S, D, H, E = (4, 256, 512, 1024, 8)
        key = jax.random.key(seed)
        ks = jax.random.split(key, 4)
        x = jax.random.normal(ks[0], (B, S, D), jnp.float32)
        Wr = jax.random.normal(ks[1], (E, D), jnp.float32) * 0.02
        br = jnp.zeros((E,), jnp.float32)
        W1 = jax.random.normal(ks[2], (E, D, H), jnp.float32) * 0.02
        b1 = jnp.zeros((E, H), jnp.float32)
        W2 = jax.random.normal(ks[3], (E, H, D), jnp.float32) * 0.02
        b2 = jnp.zeros((E, D), jnp.float32)
        return {'x': x, 'Wr': Wr, 'br': br, 'W1': W1, 'b1': b1, 'W2': W2, 'b2': b2}
    _L0_ffn_all = _L0_ffn_setup()
    _L0_ffn_in = {k: v for k, v in _L0_ffn_all.items() if k in ('Wr', 'br', 'W1', 'b1', 'W2', 'b2')}
    del _L0_ffn_all

    def _L1_gnn_setup():
        import jax, jax.numpy as jnp
        import numpy as np
        N_NODES = 1250
        IN_FEAT = 512
        OUT_FEAT = 512
        N_EDGES = 20000
        key = jax.random.key(seed)
        kx, kw, ks, kd = jax.random.split(key, 4)
        x = jax.random.normal(kx, (N_NODES, IN_FEAT), dtype=jnp.float32)
        fan_in, fan_out = (2 * IN_FEAT, OUT_FEAT)
        limit = float(np.sqrt(6.0 / (fan_in + fan_out)))
        w = jax.random.uniform(kw, (OUT_FEAT, 2 * IN_FEAT), dtype=jnp.float32, minval=-limit, maxval=limit)
        src = jax.random.randint(ks, (N_EDGES,), 0, N_NODES, dtype=jnp.int32)
        dst = jax.random.randint(kd, (N_EDGES,), 0, N_NODES, dtype=jnp.int32)
        edge_index = jnp.stack([src, dst], axis=0)
        return {'x': x, 'w': w, 'edge_index': edge_index}
    _L1_gnn_all = _L1_gnn_setup()
    _L1_gnn_in = {k: v for k, v in _L1_gnn_all.items() if k in ('w',)}
    del _L1_gnn_all

    def _L1_mix_setup():
        import jax, jax.numpy as jnp
        import numpy as np
        EPS = 1e-06
        H = 8
        DH = 64
        LN_EPS = 1e-05

        def _layernorm(x, g, b):
            m = jnp.mean(x, axis=-1, keepdims=True)
            v = jnp.mean(jnp.square(x - m), axis=-1, keepdims=True)
            return (x - m) / jnp.sqrt(v + LN_EPS) * g + b

        def _flow_attention(x, Wq, bq, Wk, bk, Wv, bv, Wo, bo):
            B, L, D = x.shape
            S = L
            q = jax.nn.sigmoid((x @ Wq + bq).reshape(B, L, H, DH).transpose(0, 2, 1, 3))
            k = jax.nn.sigmoid((x @ Wk + bk).reshape(B, S, H, DH).transpose(0, 2, 1, 3))
            v = (x @ Wv + bv).reshape(B, S, H, DH).transpose(0, 2, 1, 3)
            sink_incoming = 1.0 / jnp.einsum('nhld,nhd->nhl', q + EPS, k.sum(axis=2) + EPS)
            source_outgoing = 1.0 / jnp.einsum('nhld,nhd->nhl', k + EPS, q.sum(axis=2) + EPS)
            conserved_sink = jnp.einsum('nhld,nhd->nhl', q + EPS, (k * source_outgoing[..., None]).sum(axis=2) + EPS)
            conserved_source = jnp.einsum('nhld,nhd->nhl', k + EPS, (q * sink_incoming[..., None]).sum(axis=2) + EPS)
            conserved_source = jnp.clip(conserved_source, -1.0, 1.0)
            sink_allocation = jax.nn.sigmoid(conserved_sink * (float(L) / float(S)))
            source_competition = jax.nn.softmax(conserved_source, axis=-1) * float(S)
            kv = jnp.einsum('nhld,nhlm->nhdm', k, v * source_competition[..., None])
            o = jnp.einsum('nhld,nhdm->nhlm', q * sink_incoming[..., None], kv)
            o = o * sink_allocation[..., None]
            o = o.transpose(0, 2, 1, 3).reshape(B, L, D)
            return o @ Wo + bo
        key = jax.random.key(seed)
        ks = jax.random.split(key, 16)
        B, L, D, F = (2, 2048, 512, 256)
        s = 0.02
        inp = {'x': jax.random.normal(ks[0], (B, L, D), dtype=jnp.float32), 'Wq': jax.random.normal(ks[1], (D, D), dtype=jnp.float32) * s, 'bq': jnp.zeros((D,), jnp.float32), 'Wk': jax.random.normal(ks[2], (D, D), dtype=jnp.float32) * s, 'bk': jnp.zeros((D,), jnp.float32), 'Wv': jax.random.normal(ks[3], (D, D), dtype=jnp.float32) * s, 'bv': jnp.zeros((D,), jnp.float32), 'Wo': jax.random.normal(ks[4], (D, D), dtype=jnp.float32) * s, 'bo': jnp.zeros((D,), jnp.float32), 'W1': jax.random.normal(ks[5], (D, F), dtype=jnp.float32) * s, 'b1': jnp.zeros((F,), jnp.float32), 'W2': jax.random.normal(ks[6], (F, D), dtype=jnp.float32) * s, 'b2': jnp.zeros((D,), jnp.float32), 'g1': jnp.ones((D,), jnp.float32), 'be1': jnp.zeros((D,), jnp.float32), 'g2': jnp.ones((D,), jnp.float32), 'be2': jnp.zeros((D,), jnp.float32)}
        return inp
    _L1_mix_all = _L1_mix_setup()
    _L1_mix_in = {k: v for k, v in _L1_mix_all.items() if k in ('Wq', 'bq', 'Wk', 'bk', 'Wv', 'bv', 'Wo', 'bo', 'W1', 'b1', 'W2', 'b2', 'g1', 'be1', 'g2', 'be2')}
    del _L1_mix_all

    def _L1_ffn_setup():
        import jax, jax.numpy as jnp
        import numpy as np
        B, S, D, F, E, NS, K = (2, 256, 512, 256, 8, 2, 2)
        key = jax.random.key(seed)
        ks = jax.random.split(key, 6)
        scale = 0.02

        def p(k, shape):
            return jax.random.normal(k, shape, jnp.float32) * scale
        return {'x': jax.random.normal(ks[0], (B, S, D), jnp.float32), 'gate_w': p(ks[1], (E, D)), 'gate_b': jnp.zeros((E,), jnp.float32), 'sw1': p(ks[2], (NS, F, D)), 'sb1': jnp.zeros((NS, F), jnp.float32), 'sw2': p(ks[3], (NS, D, F)), 'sb2': jnp.zeros((NS, D), jnp.float32), 'rw1': p(ks[4], (E, F, D)), 'rb1': jnp.zeros((E, F), jnp.float32), 'rw2': p(ks[5], (E, D, F)), 'rb2': jnp.zeros((E, D), jnp.float32)}
    _L1_ffn_all = _L1_ffn_setup()
    _L1_ffn_in = {k: v for k, v in _L1_ffn_all.items() if k in ('gate_w', 'gate_b', 'sw1', 'sb1', 'sw2', 'sb2', 'rw1', 'rb1', 'rw2', 'rb2')}
    del _L1_ffn_all
    return {'x': x, 'src': src, 'dst': dst, 'edge_attr_16': edge_attr_16, 'L0_gnn_Wq': _L0_gnn_in['Wq'], 'L0_gnn_bq': _L0_gnn_in['bq'], 'L0_gnn_Wk': _L0_gnn_in['Wk'], 'L0_gnn_bk': _L0_gnn_in['bk'], 'L0_gnn_Wv': _L0_gnn_in['Wv'], 'L0_gnn_bv': _L0_gnn_in['bv'], 'L0_gnn_Wo': _L0_gnn_in['Wo'], 'L0_gnn_bo': _L0_gnn_in['bo'], 'L0_gnn_We': _L0_gnn_in['We'], 'L0_gnn_be': _L0_gnn_in['be'], 'L0_mix_w_qkv': _L0_mix_in['w_qkv'], 'L0_mix_w_out': _L0_mix_in['w_out'], 'L0_mix_b_out': _L0_mix_in['b_out'], 'L0_ffn_Wr': _L0_ffn_in['Wr'], 'L0_ffn_br': _L0_ffn_in['br'], 'L0_ffn_W1': _L0_ffn_in['W1'], 'L0_ffn_b1': _L0_ffn_in['b1'], 'L0_ffn_W2': _L0_ffn_in['W2'], 'L0_ffn_b2': _L0_ffn_in['b2'], 'L1_gnn_w': _L1_gnn_in['w'], 'L1_mix_Wq': _L1_mix_in['Wq'], 'L1_mix_bq': _L1_mix_in['bq'], 'L1_mix_Wk': _L1_mix_in['Wk'], 'L1_mix_bk': _L1_mix_in['bk'], 'L1_mix_Wv': _L1_mix_in['Wv'], 'L1_mix_bv': _L1_mix_in['bv'], 'L1_mix_Wo': _L1_mix_in['Wo'], 'L1_mix_bo': _L1_mix_in['bo'], 'L1_mix_W1': _L1_mix_in['W1'], 'L1_mix_b1': _L1_mix_in['b1'], 'L1_mix_W2': _L1_mix_in['W2'], 'L1_mix_b2': _L1_mix_in['b2'], 'L1_mix_g1': _L1_mix_in['g1'], 'L1_mix_be1': _L1_mix_in['be1'], 'L1_mix_g2': _L1_mix_in['g2'], 'L1_mix_be2': _L1_mix_in['be2'], 'L1_ffn_gate_w': _L1_ffn_in['gate_w'], 'L1_ffn_gate_b': _L1_ffn_in['gate_b'], 'L1_ffn_sw1': _L1_ffn_in['sw1'], 'L1_ffn_sb1': _L1_ffn_in['sb1'], 'L1_ffn_sw2': _L1_ffn_in['sw2'], 'L1_ffn_sb2': _L1_ffn_in['sb2'], 'L1_ffn_rw1': _L1_ffn_in['rw1'], 'L1_ffn_rb1': _L1_ffn_in['rb1'], 'L1_ffn_rw2': _L1_ffn_in['rw2'], 'L1_ffn_rb2': _L1_ffn_in['rb2']}

def reference(x, src, dst, edge_attr_16, L0_gnn_Wq, L0_gnn_bq, L0_gnn_Wk, L0_gnn_bk, L0_gnn_Wv, L0_gnn_bv, L0_gnn_Wo, L0_gnn_bo, L0_gnn_We, L0_gnn_be, L0_mix_w_qkv, L0_mix_w_out, L0_mix_b_out, L0_ffn_Wr, L0_ffn_br, L0_ffn_W1, L0_ffn_b1, L0_ffn_W2, L0_ffn_b2, L1_gnn_w, L1_mix_Wq, L1_mix_bq, L1_mix_Wk, L1_mix_bk, L1_mix_Wv, L1_mix_bv, L1_mix_Wo, L1_mix_bo, L1_mix_W1, L1_mix_b1, L1_mix_W2, L1_mix_b2, L1_mix_g1, L1_mix_be1, L1_mix_g2, L1_mix_be2, L1_ffn_gate_w, L1_ffn_gate_b, L1_ffn_sw1, L1_ffn_sb1, L1_ffn_sw2, L1_ffn_sb2, L1_ffn_rw1, L1_ffn_rb1, L1_ffn_rw2, L1_ffn_rb2):
    import jax
    import jax.numpy as jnp

    def _L0_gnn_ref(x, batch, edge_index, edge_attr, Wq, bq, Wk, bk, Wv, bv, Wo, bo, We, be, num_graphs):
        import jax, jax.numpy as jnp
        import numpy as np
        B = 32
        N = 512
        HID = 512
        H = 8
        E = 32768
        ED = 16
        n_total, hid = x.shape
        n = n_total // num_graphs
        hd = hid // H
        scale = 1.0 / jnp.sqrt(jnp.asarray(hd, x.dtype))
        q = (x @ Wq + bq).reshape(num_graphs, n, H, hd)
        k = (x @ Wk + bk).reshape(num_graphs, n, H, hd)
        v = (x @ Wv + bv).reshape(num_graphs, n, H, hd)
        attn = jnp.einsum('bnhd,bmhd->bnmh', q, k) * scale
        eb = edge_attr @ We + be
        b_idx = edge_index[0] // n
        loc_src = edge_index[0] % n
        loc_dst = edge_index[1] % n
        attn = attn.at[b_idx, loc_src, loc_dst].add(eb)
        attn = jax.nn.softmax(attn, axis=2)
        out = jnp.einsum('bnmh,bmhd->bnhd', attn, v).reshape(n_total, hid)
        return out @ Wo + bo

    def _L0_mix_ref(x, w_qkv, w_out, b_out):
        import jax, jax.numpy as jnp
        import numpy as np
        HEADS = 8
        DIM_HEAD = 64
        DIM = 512
        INNER = HEADS * DIM_HEAD
        SCALE = DIM_HEAD ** (-0.5)

        def _feature_map(t):
            return jax.nn.elu(t) + 1.0
        b, n, _ = x.shape
        h, d = (HEADS, DIM_HEAD)
        qkv = x @ w_qkv.T
        q, k, v = jnp.split(qkv, 3, axis=-1)
        reshape = lambda t: t.reshape(b, n, h, d).transpose(0, 2, 1, 3)
        q, k, v = (reshape(q), reshape(k), reshape(v))
        q = _feature_map(q * SCALE)
        k = _feature_map(k)
        k_cumsum = k.sum(axis=2)
        context = jnp.einsum('bhnd,bhne->bhde', k, v)
        out = jnp.einsum('bhnd,bhde->bhne', q, context)
        denom = jnp.einsum('bhnd,bhd->bhn', q, k_cumsum)[..., None] + 1e-08
        out = out / denom
        out = out.transpose(0, 2, 1, 3).reshape(b, n, h * d)
        return out @ w_out.T + b_out

    def _L0_ffn_ref(x, Wr, br, W1, b1, W2, b2):
        import jax, jax.numpy as jnp
        import numpy as np
        B, S, D, H, E = (4, 256, 512, 1024, 8)
        b, s, d = x.shape
        n = b * s
        e = Wr.shape[0]
        xf = x.reshape(n, d)
        logits = xf @ Wr.T + br
        probs = jax.nn.softmax(logits, axis=-1)
        top2_prob, top2_idx = jax.lax.top_k(probs, 2)
        comb = jnp.zeros((n, e), x.dtype).at[jnp.arange(n)[:, None], top2_idx].add(top2_prob)
        h = jax.nn.gelu(jnp.einsum('nd,edh->enh', xf, W1) + b1[:, None, :], approximate=False)
        o = jnp.einsum('enh,ehd->end', h, W2) + b2[:, None, :]
        y = jnp.einsum('ne,end->nd', comb, o)
        return y.reshape(b, s, d)

    def _L1_gnn_ref(x, w, edge_index):
        import jax, jax.numpy as jnp
        import numpy as np
        N_NODES = 1250
        IN_FEAT = 512
        OUT_FEAT = 512
        N_EDGES = 20000
        src, dst = (edge_index[0], edge_index[1])
        msgs = x[src]
        summed = jax.ops.segment_sum(msgs, dst, num_segments=x.shape[0])
        deg = jax.ops.segment_sum(jnp.ones_like(dst, dtype=x.dtype), dst, num_segments=x.shape[0])
        neighbor_mean = summed / jnp.maximum(deg, 1.0)[:, None]
        message = jnp.concatenate([x, neighbor_mean], axis=-1)
        weighted = jnp.einsum('of,nf->no', w, message)
        return jax.nn.relu(weighted)

    def _L1_mix_ref(x, Wq, bq, Wk, bk, Wv, bv, Wo, bo, W1, b1, W2, b2, g1, be1, g2, be2):
        import jax, jax.numpy as jnp
        import numpy as np
        EPS = 1e-06
        H = 8
        DH = 64
        LN_EPS = 1e-05

        def _layernorm(x, g, b):
            m = jnp.mean(x, axis=-1, keepdims=True)
            v = jnp.mean(jnp.square(x - m), axis=-1, keepdims=True)
            return (x - m) / jnp.sqrt(v + LN_EPS) * g + b

        def _flow_attention(x, Wq, bq, Wk, bk, Wv, bv, Wo, bo):
            B, L, D = x.shape
            S = L
            q = jax.nn.sigmoid((x @ Wq + bq).reshape(B, L, H, DH).transpose(0, 2, 1, 3))
            k = jax.nn.sigmoid((x @ Wk + bk).reshape(B, S, H, DH).transpose(0, 2, 1, 3))
            v = (x @ Wv + bv).reshape(B, S, H, DH).transpose(0, 2, 1, 3)
            sink_incoming = 1.0 / jnp.einsum('nhld,nhd->nhl', q + EPS, k.sum(axis=2) + EPS)
            source_outgoing = 1.0 / jnp.einsum('nhld,nhd->nhl', k + EPS, q.sum(axis=2) + EPS)
            conserved_sink = jnp.einsum('nhld,nhd->nhl', q + EPS, (k * source_outgoing[..., None]).sum(axis=2) + EPS)
            conserved_source = jnp.einsum('nhld,nhd->nhl', k + EPS, (q * sink_incoming[..., None]).sum(axis=2) + EPS)
            conserved_source = jnp.clip(conserved_source, -1.0, 1.0)
            sink_allocation = jax.nn.sigmoid(conserved_sink * (float(L) / float(S)))
            source_competition = jax.nn.softmax(conserved_source, axis=-1) * float(S)
            kv = jnp.einsum('nhld,nhlm->nhdm', k, v * source_competition[..., None])
            o = jnp.einsum('nhld,nhdm->nhlm', q * sink_incoming[..., None], kv)
            o = o * sink_allocation[..., None]
            o = o.transpose(0, 2, 1, 3).reshape(B, L, D)
            return o @ Wo + bo
        sa = _flow_attention(_layernorm(x, g1, be1), Wq, bq, Wk, bk, Wv, bv, Wo, bo)[0]
        x = x + sa
        h = _layernorm(x, g2, be2)
        h = jax.nn.gelu(h @ W1 + b1, approximate=False) @ W2 + b2
        return x + h

    def _L1_ffn_ref(x, gate_w, gate_b, sw1, sb1, sw2, sb2, rw1, rb1, rw2, rb2):
        import jax, jax.numpy as jnp
        import numpy as np
        B, S, D, F, E, NS, K = (2, 256, 512, 256, 8, 2, 2)
        b, s, d = x.shape
        t = x.reshape(-1, d)
        T = t.shape[0]
        hs = jax.nn.gelu(jnp.einsum('td,nfd->ntf', t, sw1) + sb1[:, None, :], approximate=False)
        shared = jnp.einsum('ntf,ndf->td', hs, sw2) + sb2.sum(axis=0)
        logits = t @ gate_w.T + gate_b
        probs = jax.nn.softmax(logits, axis=-1)
        top_v, top_i = jax.lax.top_k(probs, K)
        cw = jnp.zeros_like(probs).at[jnp.arange(T)[:, None], top_i].add(top_v)
        hr = jax.nn.gelu(jnp.einsum('td,efd->etf', t, rw1) + rb1[:, None, :], approximate=False)
        oe = jnp.einsum('etf,edf->etd', hr, rw2) + rb2[:, None, :]
        routed = jnp.einsum('etd,te->td', oe, cw)
        return (shared + routed).reshape(b, s, d)
    edge_index = jnp.stack([src, dst])
    batch0 = jnp.zeros((2048,), jnp.int32)
    xn = _layernorm(x, axis=-1)
    x = x + _L0_gnn_ref(xn, batch0, edge_index, edge_attr_16, L0_gnn_Wq, L0_gnn_bq, L0_gnn_Wk, L0_gnn_bk, L0_gnn_Wv, L0_gnn_bv, L0_gnn_Wo, L0_gnn_bo, L0_gnn_We, L0_gnn_be, 32) + _L0_mix_ref(xn[None], L0_mix_w_qkv, L0_mix_w_out, L0_mix_b_out)[0]
    x = x + _L0_ffn_ref(_layernorm(x, axis=-1)[None], L0_ffn_Wr, L0_ffn_br, L0_ffn_W1, L0_ffn_b1, L0_ffn_W2, L0_ffn_b2)[0]
    xn = _layernorm(x, axis=-1)
    x = x + _L1_gnn_ref(xn, L1_gnn_w, edge_index) + _L1_mix_ref(xn[None], L1_mix_Wq, L1_mix_bq, L1_mix_Wk, L1_mix_bk, L1_mix_Wv, L1_mix_bv, L1_mix_Wo, L1_mix_bo, L1_mix_W1, L1_mix_b1, L1_mix_W2, L1_mix_b2, L1_mix_g1, L1_mix_be1, L1_mix_g2, L1_mix_be2)[0]
    x = x + _L1_ffn_ref(_layernorm(x, axis=-1)[None], L1_ffn_gate_w, L1_ffn_gate_b, L1_ffn_sw1, L1_ffn_sb1, L1_ffn_sw2, L1_ffn_sb2, L1_ffn_rw1, L1_ffn_rb1, L1_ffn_rw2, L1_ffn_rb2)[0]
    return x

_drawn_inputs = setup_inputs


def setup_inputs(seed=0):
    import zlib

    import numpy as np

    out = dict(_drawn_inputs(seed))
    spreads = {'L0_gnn_bq': (0.0, 0.374),
     'L0_gnn_bk': (0.0, 0.8),
     'L0_gnn_bv': (0.0, 0.1),
     'L0_gnn_bo': (0.0, 0.1),
     'L0_gnn_be': (0.0, 0.549),
     'L0_ffn_br': (0.0, 0.267),
     'L0_ffn_b1': (0.0, 0.745),
     'L0_ffn_b2': (0.0, 0.275),
     'L1_mix_bq': (0.0, 0.8),
     'L1_mix_bk': (0.0, 0.8),
     'L1_mix_bv': (0.0, 0.491),
     'L1_mix_bo': (0.0, 0.1),
     'L1_mix_b1': (0.0, 0.8),
     'L1_mix_b2': (0.0, 0.1),
     'L1_mix_g1': (1.0, 0.6),
     'L1_mix_be1': (0.0, 0.8),
     'L1_mix_g2': (1.0, 0.6),
     'L1_mix_be2': (0.0, 0.8),
     'L1_ffn_gate_b': (0.0, 0.8),
     'L1_ffn_sb1': (0.0, 0.662),
     'L1_ffn_sb2': (0.0, 0.1),
     'L1_ffn_rb1': (0.0, 0.8),
     'L1_ffn_rb2': (0.0, 0.61)}
    factors = {'L0_mix_b_out': 5.744,
     'L1_mix_Wq': 8.0,
     'L1_mix_Wk': 8.0,
     'L1_mix_Wv': 4.316,
     'L1_mix_Wo': 2.794,
     'L1_ffn_gate_w': 3.824,
     'L1_ffn_rw1': 5.362,
     'L1_ffn_rw2': 5.006}
    for name, (base, spread) in spreads.items():
        noise = np.random.default_rng([zlib.crc32(name.encode()), seed]).standard_normal(out[name].shape)
        drawn = base * np.exp(spread * noise) if base else spread * noise
        out[name] = jnp.asarray(drawn.astype(out[name].dtype))
    for name, factor in factors.items():
        out[name] = (out[name] * factor).astype(out[name].dtype)
    return out
```

```python
from contextlib import ExitStack

import concourse.bass as bass
from concourse import mybir

F32 = mybir.dt.float32
BF16 = mybir.dt.bfloat16
I32 = mybir.dt.int32
U32 = mybir.dt.uint32
U16 = mybir.dt.uint16
ALU = mybir.AluOpType
ACT = mybir.ActivationFunctionType
AX = mybir.AxisListType

P = 128
N_TOK = 2048
D = 512
DC = D // P
NT = N_TOK // P
BLK = 256
NB = N_TOK // BLK
HEADS = 8
DH = D // HEADS
PAIRS = HEADS // 2
GRAPH = 64
E_EDGES = 32768
EJ = E_EDGES // P
ED = 16
LN_EPS = 1e-5
FLOW_EPS = 1e-6

BUCKETS = NT * 4
GROUP = 256
NG = 192
NCH = 2 * NG
REC = 16
ACOLS = (N_TOK // GRAPH) * 16
BCOLS = 16 * HEADS

EXPERTS = 8
TOPK = 2
SLOT_TILE = 256
NST = (N_TOK * TOPK) // SLOT_TILE + EXPERTS - 1
SLOTS = NST * SLOT_TILE


class Step:

    def __init__(self, eng, sem, t, k):
        self.eng, self.sem, self.base, self.k, self.n = eng, sem, t * k, k, 0

    def did(self, ins):
        ins.then_inc(self.sem, 1)
        self.n += 1
        assert self.n <= self.k

    def wait(self):
        self.eng.wait_ge(self.sem, self.base + self.n)

    def do(self, ins):
        self.did(ins)
        self.wait()


def loop(eng, n, body, unroll=2, peel=0):
    full = (n - peel) // unroll
    with eng.Fori(0, full) as i:
        for u in range(unroll):
            body(i * unroll + u, u)
    for t in range(full * unroll, n):
        body(t, t % unroll)


LEAD = 1


def lead(eng, sem, k=1):
    eng.sem_inc(sem, LEAD * k)


def done(t, k=1):
    return (t + 1 + LEAD) * k


def reuse(t, k=1):
    return (t - 1 + LEAD) * k


def gate(eng, sem, value, passed):
    eng.wait_ge(sem, value)
    eng.sem_inc(passed, 1)


def is_last(t, n):
    return isinstance(t, int) and t == n - 1


class Phase:

    def __init__(self, nc, name):
        self.nc, self.name, self.ctx = nc, name, ExitStack()
        self.used = []

    def __enter__(self):
        self.ctx.__enter__()
        return self

    def __exit__(self, *a):
        self.ctx.__exit__(*a)
        if a[0] is None:
            self.nc.clear_and_free_semaphores(self.used)
            self.nc.all_engine_barrier()

    def sb(self, name, shape, dt=F32):
        return self.ctx.enter_context(self.nc.sbuf_tensor(f"{self.name}_{name}", shape, dt))

    def ps(self, name, shape, dt=F32):
        return self.ctx.enter_context(self.nc.psum_tensor(f"{self.name}_{name}", shape, dt))

    def sem(self, name):
        self.used.append(self.nc.alloc_semaphore(name=f"{self.name}_{name}"))
        return self.used[-1]

    def sems(self, *names):
        return [self.sem(n) for n in names]

    def block(self):
        return self.ctx.enter_context(self.nc.Block())


def constants(nc, G, x):
    with Phase(nc, "const") as ph:
        raw, made, mask_zero, x_in = ph.sems("raw", "made", "mask_zero", "x_in")
        block = ph.block()

        @block.sync
        def _(sp):
            sp.dma_start(G.X[:, :, :], x.rearrange("(t p) d -> p t d", p=P)).then_inc(x_in, 16)
            sp.wait_ge(x_in, 16)

        @block.vector
        def _(dve):
            dve.memset(G.headmask[:, :], 0.0).then_inc(mask_zero, 1)
            dve.wait_ge(mask_zero, 1)
            dve.memset(G.headmask[0:DH, 0:DH], 1.0)
            dve.memset(G.headmask[DH:P, DH:P], 1.0)

        @block.gpsimd
        def _(pool):
            pool.memset(G.ident[:, :], 0.0).then_inc(raw, 1)
            pool.memset(G.upper[:, :], 1.0).then_inc(raw, 1)
            pool.memset(G.ones[:, :], 1.0).then_inc(raw, 1)
            pool.memset(G.minus_half[:, :], -0.5).then_inc(raw, 1)
            pool.wait_ge(raw, 4)
            pool.affine_select(out=G.ident[:, :], in_=G.ident[:, :], compare_op=ALU.not_equal, fill=1.0, base=0,
                               pattern=[[-1, P]], channel_multiplier=1).then_inc(made, 1)
            pool.affine_select(out=G.upper[:, :], in_=G.upper[:, :], compare_op=ALU.is_gt, fill=0.0, base=0,
                               pattern=[[1, P]], channel_multiplier=-1).then_inc(made, 1)
            pool.iota(G.iota512[:, :], pattern=[[1, ACOLS]], base=0, channel_multiplier=0,
                      allow_small_or_imprecise_dtypes=True).then_inc(made, 1)
            pool.iota(G.iota16x8[:, :, :], pattern=[[1, 16], [0, HEADS]], base=0, channel_multiplier=0,
                      allow_small_or_imprecise_dtypes=True).then_inc(made, 1)
            pool.iota(G.part[:, :], pattern=[[0, 1]], base=0, channel_multiplier=1,
                      allow_small_or_imprecise_dtypes=True).then_inc(made, 1)
            pool.wait_ge(made, 5)


def head_rows(nc, G):
    with Phase(nc, "heads") as ph:
        sel_zero, sel_ready, rep_done, rep_ready = ph.sems("sel_zero", "sel_ready", "rep_done", "rep_ready")
        psR = ph.ps("psR", [HEADS, DC, P])
        block = ph.block()

        @block.vector
        def _(dve):
            dve.memset(G.sel[:, :, :], 0.0).then_inc(sel_zero, 1)
            dve.wait_ge(sel_zero, 1)
            for h in range(HEADS):
                dve.memset(G.sel[DH * (h % 2):DH * (h % 2 + 1), h // 2, h:h + 1], 1.0).then_inc(sel_ready, 1)
            dve.wait_ge(rep_done, 1)
            dve.tensor_copy(G.rep[:, :, :], psR[:, :, :]).then_inc(rep_ready, 1)

        @block.tensor
        def _(pe):
            pe.wait_ge(sel_ready, HEADS)
            for c in range(DC):
                mm = pe.transpose(psR[:, c], G.sel[:, c], G.ident[:, :])
            mm.then_inc(rep_done, 1)


def ln_stats_buffers(ph):
    s = type("LnStats", (), {})()
    s.bn = ph.sb("ln_bn", [P, NT, 6])
    s.mean = ph.sb("ln_mean", [P, NT])
    s.diff = ph.sb("ln_diff", [P, NT])
    s.m2 = ph.sb("ln_m2", [P, NT])
    s.var = ph.sb("ln_var", [P, NT])
    s.rstd = ph.sb("ln_rstd", [P, NT])
    s.shift = ph.sb("ln_shift", [P, NT])
    s.part_done, s.var_ready, s.rstd_ready, s.ready = ph.sems("ln_part", "ln_var", "ln_rstd", "ln_ready")
    return s


def ln_stats_vector(dve, s, X):
    st = Step(dve, s.part_done, 0, 99)
    for t in range(NT):
        st.did(dve.bn_stats(s.bn[:, t, :], X[:, t, :]))
    st.wait()
    ln_finish_vector(dve, s, s.bn, st)


def ln_finish_vector(dve, s, bn, st):
    st.did(dve.tensor_tensor(s.mean[:, :], bn[:, :, 1], bn[:, :, 4], ALU.add))
    st.did(dve.tensor_tensor(s.diff[:, :], bn[:, :, 1], bn[:, :, 4], ALU.subtract))
    st.did(dve.tensor_tensor(s.m2[:, :], bn[:, :, 2], bn[:, :, 5], ALU.add))
    st.wait()
    st.did(dve.tensor_scalar(s.mean[:, :], s.mean[:, :], 0.5, None, ALU.mult))
    st.did(dve.tensor_tensor(s.diff[:, :], s.diff[:, :], s.diff[:, :], ALU.mult))
    st.did(dve.tensor_scalar(s.m2[:, :], s.m2[:, :], 1.0 / D, LN_EPS, ALU.mult, ALU.add))
    st.wait()
    dve.scalar_tensor_tensor(out=s.var[:, :], in0=s.diff[:, :], scalar=0.25, in1=s.m2[:, :],
                             op0=ALU.mult, op1=ALU.add).then_inc(s.var_ready, 1)
    dve.wait_ge(s.rstd_ready, 1)
    dve.scalar_tensor_tensor(out=s.shift[:, :], in0=s.mean[:, :], scalar=-1.0, in1=s.rstd[:, :],
                             op0=ALU.mult, op1=ALU.mult).then_inc(s.ready, 1)
    dve.wait_ge(s.ready, 1)


def ln_stats_pool(pool, s, G):
    pool.wait_ge(s.var_ready, 1)
    pool.tensor_tensor(s.rstd[:, :], s.var[:, :], G.minus_half[:, :], ALU.pow).then_inc(s.rstd_ready, 1)


def token_tile(X, t):
    return X[:, bass.ds(t, 1), :].rearrange("p a d -> p (a d)")


def col(ap2d, t):
    return ap2d[:, bass.ds(t, 1)]


def bucket_starts(ph, nb, group, n_groups, past):
    s = type("Buckets", (), {})()
    s.nb, s.group, s.n_groups = nb, group, n_groups
    s.count = ph.sb("count", [P, nb])
    s.before = ph.sb("before", [P, nb])
    s.total = ph.sb("total", [P, nb], I32)
    s.padded = ph.sb("padded", [P, nb])
    s.end = ph.sb("end", [P, nb])
    s.first = ph.sb("first", [P, nb])
    s.group_at = ph.sb("group_at", [P, n_groups])
    s.past = past
    s.bucket = ph.sb("bucket", [P, n_groups])
    s.ps = ph.ps("ps_count", [P, 2, nb])
    s.counted, s.summed, s.step, s.numbered = ph.sems("counted", "summed", "bucket_step", "numbered")
    return s


def bucket_starts_pool(pool, s):
    pool.iota(s.group_at[:, :], pattern=[[s.group, s.n_groups]], base=0, channel_multiplier=0,
              allow_small_or_imprecise_dtypes=True).then_inc(s.numbered, 1)


def bucket_starts_tensor(pe, s, G, n_counts):
    pe.wait_ge(s.counted, n_counts)
    pe.matmul(s.ps[:, 0], G.upper[:, :], s.count[:, :], start=True, stop=True)
    pe.matmul(s.ps[:, 1], G.ones[:, :], s.count[:, :], start=True, stop=True).then_inc(s.summed, 1)


def bucket_starts_vector(dve, s):
    st = Step(dve, s.step, 0, 16)
    shift = s.group.bit_length() - 1
    dve.wait_ge(s.summed, 1)
    st.did(dve.tensor_scalar(s.total[:, :], s.ps[:, 1], float(s.group - 1), None, ALU.add))
    st.do(dve.tensor_copy(s.before[:, :], s.ps[:, 0]))
    st.do(dve.tensor_scalar(s.total[:, :], s.total[:, :], shift, shift, ALU.logical_shift_right,
                            ALU.logical_shift_left))
    st.do(dve.tensor_copy(s.padded[:, :], s.total[:, :]))
    st.do(dve.tensor_tensor_scan(s.end[:, :], s.padded[:, :], s.padded[:, :], 0.0, ALU.add, ALU.bypass))
    st.do(dve.tensor_tensor(s.first[:, :], s.end[:, :], s.padded[:, :], ALU.subtract))
    st.did(dve.scalar_tensor_tensor(out=s.first[:, :], in0=s.first[:, :], scalar=-1.0, in1=s.before[:, :],
                                    op0=ALU.add, op1=ALU.add))
    dve.wait_ge(s.numbered, 1)
    st.do(dve.tensor_tensor(s.past[:, :, :], s.group_at[:, :].unsqueeze(2).to_broadcast([P, s.n_groups, s.nb]),
                            s.end[:, :].unsqueeze(1).to_broadcast([P, s.n_groups, s.nb]), ALU.is_ge))
    st.do(dve.tensor_reduce(s.bucket[:, :], s.past[:, :, :], AX.X, ALU.add))
    st.do(dve.tensor_scalar(s.bucket[:, :], s.bucket[:, :], float(s.nb - 1), None, ALU.min))


def sort_edges(nc, G, w):
    with Phase(nc, "sort") as ph:
        src = ph.sb("src", [P, EJ], I32)
        dst = ph.sb("dst", [P, EJ], I32)
        attr = ph.sb("attr", [P, EJ * ED])
        we = ph.sb("we", [P, 8 * HEADS])
        be = ph.sb("be", [P, HEADS])
        attrT = ph.sb("attrT", [P, 2, 4, P])
        rec = ph.sb("rec", [P, EJ, REC])
        ka = ph.sb("ka", [P, EJ], I32)
        kb = ph.sb("kb", [P, EJ], I32)
        key = ph.sb("key", [P, EJ])
        onehot = ph.sb("onehot", [P, BUCKETS, EJ], BF16)
        rank = ph.sb("rank", [P, BUCKETS, EJ])
        slot = ph.sb("slot", [P, EJ])
        place = ph.sb("place", [P, EJ], I32)
        blank = ph.sb("blank", [P, NCH * REC // 4])
        rec_now = ph.sb("rec_now", [P, 2, 8, REC])
        place_now = ph.sb("place_now", [P, 2, 8], I32)
        bs = bucket_starts(ph, BUCKETS, GROUP, NG, rank[:, :, :].rearrange("p b j -> p (b j)")[:, 0:NG * BUCKETS].rearrange(
            "p (g b) -> p g b", b=BUCKETS))
        psA = ph.ps("psA", [P, 2, 4, P])
        psE = ph.ps("psE", [P, 2, 64, HEADS])
        (e_in, a_in, w_in, we_zero, blank_ready, blanked, key_step, ranked, weighed, slotted,
         a_done, a_ready, e_done, rec_ready, rec_copied, passed, out0, out1) = ph.sems(
            "e_in", "a_in", "w_in", "we_zero", "blank_ready", "blanked", "key_step", "ranked", "weighed", "slotted",
            "a_done", "a_ready", "e_done", "rec_ready", "rec_copied", "passed", "out0", "out1")
        scattered = [out0, out1]
        block = ph.block()
        n_batches = EJ // 64
        n_sets = EJ // 8

        @block.sync
        def _(sp):
            sp.dma_start(src[:, :], w["src"].rearrange("(p j) -> p j", p=P)).then_inc(e_in, 16)
            sp.dma_start(dst[:, :], w["dst"].rearrange("(p j) -> p j", p=P)).then_inc(e_in, 16)
            sp.dma_start(attr[:, :], w["edge_attr"].rearrange("(p j) f -> p (j f)", p=P)).then_inc(a_in, 16)
            sp.dma_start(be[:, :], w["be"].partition_broadcast(P)).then_inc(w_in, 16)
            sp.wait_ge(we_zero, 1)
            for k in range(8):
                sp.dma_start(we[k * ED:(k + 1) * ED, k * HEADS:(k + 1) * HEADS], w["We"]).then_inc(w_in, 16)
            sp.wait_ge(blank_ready, 1)
            for k in range(4):
                n = NCH * REC // 4
                sp.dma_start(G.rec_dram.rearrange("(p c) r -> p (c r)", p=P)[:, k * n:(k + 1) * n],
                             blank[:, :]).then_inc(blanked, 16)

        @block.gpsimd
        def _(pool):
            pool.memset(we[:, :], 0.0).then_inc(we_zero, 1)
            pool.memset(blank[:, :], -1.0).then_inc(blank_ready, 1)
            bucket_starts_pool(pool, bs)
            pool.wait_ge(blanked, 64)

            def scatter(n, u):
                gate(pool, rec_copied, done(n, 2), passed)
                for k in range(8):
                    pool.indirect_dma_start(
                        out=G.rec_dram, out_offset=bass.IndirectOffsetOnAxis(ap=place_now[:, u, k:k + 1], axis=0),
                        in_=rec_now[:, u, k], in_offset=None).then_inc(scattered[u], 16)
            loop(pool, n_sets, scatter)
            for u in range(2):
                pool.wait_ge(scattered[u], 8 * 16 * n_sets // 2)

        @block.vector
        def _(dve):
            st = Step(dve, key_step, 0, 16)
            dve.wait_ge(e_in, 32)
            st.did(dve.tensor_scalar(ka[:, :], src[:, :], 7, 2, ALU.logical_shift_right, ALU.logical_shift_left))
            st.do(dve.tensor_scalar(kb[:, :], dst[:, :], 4, 3, ALU.logical_shift_right, ALU.bitwise_and))
            st.do(dve.tensor_tensor(key[:, :], ka[:, :], kb[:, :], ALU.add))
            st.do(dve.tensor_scalar(ka[:, :], dst[:, :], 6, 4, ALU.logical_shift_right, ALU.logical_shift_left))
            st.do(dve.tensor_scalar(kb[:, :], dst[:, :], 15, None, ALU.bitwise_and))
            st.did(dve.tensor_tensor(rec[:, :, 9], ka[:, :], kb[:, :], ALU.add))
            st.do(dve.tensor_copy(rec[:, :, 10], kb[:, :]))
            st.do(dve.tensor_scalar(src[:, :], src[:, :], P - 1, None, ALU.bitwise_and))
            st.did(dve.tensor_copy(rec[:, :, 8], src[:, :]))
            st.do(dve.memset(rec[:, :, 11:REC], 0.0))

            def member(b, u):
                dve.tensor_scalar(onehot[:, bass.ds(b, 1), :].rearrange("p a j -> p (a j)"), key[:, :],
                                  col(G.iota512, b), 0.0, ALU.is_equal, ALU.add,
                                  accum_out=col(bs.count, b)).then_inc(bs.counted, 1)
            loop(dve, BUCKETS, member)
            for n in range(n_batches):
                dve.wait_ge(e_done, 2 * n + 2)
                dve.tensor_tensor(rec[:, n * 64:(n + 1) * 64, 0:HEADS], psE[:, n % 2],
                                  be[:, :].unsqueeze(1).to_broadcast([P, 64, HEADS]), ALU.add).then_inc(rec_ready, 1)
            bucket_starts_vector(dve, bs)

            def number(b, u):
                hot = onehot[:, bass.ds(b, 1), :].rearrange("p a j -> p (a j)")
                dve.tensor_tensor_scan(rank[:, bass.ds(b, 1), :].rearrange("p a j -> p (a j)"), hot, hot,
                                       col(bs.first, b), ALU.add, ALU.bypass).then_inc(ranked, 1)
            loop(dve, BUCKETS, number)
            dve.wait_ge(ranked, BUCKETS)
            dve.tensor_tensor(rank[:, :, :], rank[:, :, :], onehot[:, :, :], ALU.mult).then_inc(weighed, 1)
            dve.wait_ge(weighed, 1)
            sl = Step(dve, slotted, 0, 8)
            sl.do(dve.tensor_reduce(slot[:, :], rank[:, :, :].rearrange("p b j -> p j b"), AX.X, ALU.add))
            sl.do(dve.tensor_copy(ka[:, :], slot[:, :]))
            sl.did(dve.tensor_scalar(kb[:, :], ka[:, :], 7, None, ALU.logical_shift_right))
            sl.do(dve.tensor_scalar(ka[:, :], ka[:, :], P - 1, None, ALU.bitwise_and))
            sl.did(dve.scalar_tensor_tensor(out=place[:, :], in0=ka[:, :], scalar=float(NCH), in1=kb[:, :],
                                            op0=ALU.mult, op1=ALU.add))
            sl.did(dve.tensor_copy(G.edge_bucket[:, :], bs.bucket[:, :]))

        @block.scalar
        def _(act):
            for n in range(2 * n_batches):
                act.wait_ge(a_done, n + 1)
                if n >= 2:
                    act.wait_ge(e_done, n - 1)
                act.activation(attrT[:, n % 2], psA[:, n % 2], ACT.Copy).then_inc(a_ready, 1)
            act.wait_ge(slotted, 6)
            act.wait_ge(rec_ready, n_batches)
            act.wait_ge(key_step, 10)
            lead(act, rec_copied, 2)

            def copy(n, u):
                act.wait_ge(scattered[u], (n - u) * 64)
                act.activation(place_now[:, u], place[:, bass.ds(n * 8, 8)], ACT.Copy).then_inc(rec_copied, 1)
                act.activation(rec_now[:, u], rec[:, bass.ds(n * 8, 8), :], ACT.Copy).then_inc(rec_copied, 1)
            loop(act, n_sets, copy)

        @block.tensor
        def _(pe):
            pe.wait_ge(a_in, 16)
            pe.wait_ge(w_in, 16 * 9)
            for n in range(2 * n_batches):
                if n >= 2:
                    pe.wait_ge(a_ready, n - 1)
                for k in range(4):
                    g = 4 * n + k
                    mm = pe.transpose(psA[:, n % 2, k], attr[:, g * P:(g + 1) * P], G.ident[:, :])
                mm.then_inc(a_done, 1)
                pe.wait_ge(a_ready, n + 1)
                if n >= 4 and n % 2 == 0:
                    pe.wait_ge(rec_ready, n // 2 - 1)
                for k in range(4):
                    g = 4 * (n % 2) + k
                    mm = pe.matmul(psE[:, (n // 2) % 2, g * 8:(g + 1) * 8].rearrange("p j h -> p (j h)"),
                                   attrT[:, n % 2, k], we[:, :], start=True, stop=True)
                mm.then_inc(e_done, 1)
            bucket_starts_tensor(pe, bs, G, BUCKETS)


def build_graph(nc, G):
    with Phase(nc, "graph") as ph:
        rec = ph.sb("rec", [P, NCH, REC])
        adj = ph.sb("adj", [P, BUCKETS * ACOLS], U16)
        far = ph.sb("far", [P, 2, P])
        row = ph.sb("row", [P, 2, 2, P])
        row16 = ph.sb("row16", [P, 2, 2, P], BF16)
        cols = ph.sb("cols", [P, 2, 2, ACOLS], BF16)
        bias = ph.sb("bias", [P, 2, 2, 16, HEADS])
        psA = [ph.ps(f"psA{u}", [P, ACOLS]) for u in range(2)]
        psB = [ph.ps(f"psB{u}", [P, D]) for u in range(2)]
        (rec_in, bias_zero, adj_zero, far_ready, row_ready, cols_ready, g_done, adj_added, bias_added,
         adj_out) = ph.sems("rec_in", "bias_zero", "adj_zero", "far_ready", "row_ready", "cols_ready", "g_done",
                            "adj_added", "bias_added", "adj_out")
        block = ph.block()

        @block.sync
        def _(sp):
            sp.dma_start(rec[:, :, :], G.rec_dram.rearrange("(p c) r -> p c r", p=P)).then_inc(rec_in, 16)
            sp.wait_ge(adj_added, NG)
            sp.dma_start(G.adj_dram, adj[:, :]).then_inc(adj_out, 16)
            sp.wait_ge(adj_out, 16)

        @block.gpsimd
        def _(pool):
            pool.memset(adj[:, :].bitcast(U32), 0).then_inc(adj_zero, 1)
            pool.memset(G.BIAS[:, :], 0.0).then_inc(bias_zero, 1)

        @block.scalar
        def _(act):
            act.wait_ge(rec_in, 16)
            lead(act, row_ready, 2)

            def rows(g, u):
                act.wait_ge(row_ready, reuse(g + 1, 2))
                for k in range(2):
                    act.activation(far[:, k], G.iota512[:, 0:P], ACT.Abs, scale=-1.0,
                                   bias=rec[:, bass.ds(g * 2 + k, 1), :].rearrange("p a r -> p (a r)")[:, 8:9]
                                   ).then_inc(far_ready, 1)
                act.wait_ge(far_ready, g * 2 + 2)
                act.wait_ge(g_done, reuse(g))
                act.activation(row[:, u], far[:, :, :], ACT.Relu, scale=-1.0, bias=1.0).then_inc(row_ready, 1)
                act.activation(row16[:, u], far[:, :, :], ACT.Relu, scale=-1.0, bias=1.0).then_inc(row_ready, 1)
            loop(act, NG, rows)

        @block.vector
        def _(dve):
            dve.wait_ge(rec_in, 16)
            dve.wait_ge(adj_zero, 1)
            dve.wait_ge(bias_zero, 1)

            def columns(g, u):
                dve.wait_ge(g_done, reuse(g))
                for k in range(2):
                    r = rec[:, bass.ds(g * 2 + k, 1), :].rearrange("p a r -> p (a r)")
                    dve.tensor_scalar(cols[:, u, k], G.iota512[:, :], r[:, 9:10], None,
                                      ALU.is_equal).then_inc(cols_ready, 1)
                    dve.scalar_tensor_tensor(out=bias[:, u, k], in0=G.iota16x8[:, :, :], scalar=r[:, 10:11],
                                             in1=r[:, 0:HEADS].unsqueeze(1).to_broadcast([P, 16, HEADS]),
                                             op0=ALU.is_equal, op1=ALU.mult).then_inc(cols_ready, 1)

            def add(g, u):
                b = dve.value_load(G.edge_bucket[0:1, bass.ds(g, 1)], min_val=0, max_val=BUCKETS - 1)
                dve.wait_ge(g_done, done(g))
                a = adj[:, bass.ds(b * ACOLS, ACOLS)]
                dve.wait_ge(adj_added, g)
                dve.tensor_tensor(a, a, psA[u][:, :], ALU.add).then_inc(adj_added, 1)
                a = G.BIAS[:, bass.ds(b * BCOLS, BCOLS)]
                dve.wait_ge(bias_added, g + LEAD)
                dve.tensor_tensor(a, a, psB[u][:, 0:BCOLS], ALU.add).then_inc(bias_added, 1)

            def body(g, u):
                if not is_last(g, NG):
                    columns(g + 1, 1 - u)
                add(g, u)
            lead(dve, bias_added)
            columns(0, 0)
            loop(dve, NG, body, peel=2)

        @block.tensor
        def _(pe):
            lead(pe, g_done)

            def body(g, u):
                pe.wait_ge(cols_ready, g * 4 + 4)
                pe.wait_ge(row_ready, done(g, 2))
                pe.wait_ge(bias_added, reuse(g))
                for k in range(2):
                    pe.matmul(psA[u][:, :], row16[:, u, k], cols[:, u, k], start=(k == 0), stop=(k == 1))
                for k in range(2):
                    mm = pe.matmul(psB[u][:, 0:BCOLS], row[:, u, k], bias[:, u, k].rearrange("p r h -> p (r h)"),
                                   start=(k == 0), stop=(k == 1))
                mm.then_inc(g_done, 1)
            loop(pe, NG, body)


def linear_attention_scan(nc, G, w):
    scale = DH ** -0.5
    with Phase(nc, "lin") as ph:
        wq, wk, wv, wo = (ph.sb(n, [P, DC, D]) for n in ("wq", "wk", "wv", "wo"))
        ln = ln_stats_buffers(ph)
        xn = ph.sb("xn", [P, 2, 2, D])
        xnT = ph.sb("xnT", [P, 2, DC, BLK])
        eq = ph.sb("eq", [P, DC, BLK])
        rq = ph.sb("rq", [P, DC, BLK])
        ek = ph.sb("ek", [P, D])
        rk = ph.sb("rk", [P, D])
        kf = ph.sb("kf", [P, 2, D])
        vf = ph.sb("vf", [P, 2, D])
        ctxT = ph.sb("ctxT", [P, PAIRS, P])
        ksum = ph.sb("ksum", [P, PAIRS])
        kmask = ph.sb("kmask", [P, PAIRS, P])
        den = ph.sb("den", [P, 2, D])
        psT = ph.ps("psT", [P, DC, BLK])
        psQ = ph.ps("psQ", [P, DC, BLK])
        psK = ph.ps("psK", [P, D])
        psV = ph.ps("psV", [P, D])
        psC = ph.ps("psC", [P, PAIRS, P])
        psS = ph.ps("psS", [P, PAIRS, 2])
        w_in, w_free = ph.sems("w_in", "w_free")
        xn_ready, t_done, xnT_ready = ph.sems("xn_ready", "t_done", "xnT_ready")
        q_done, q_exp, q_relu, q_ready = ph.sems("q_done", "q_exp", "q_relu", "q_ready")
        k_done, k_exp, k_relu, k_ready = ph.sems("k_done", "k_exp", "k_relu", "k_ready")
        v_done, v_ready, ctx_done = ph.sems("v_done", "v_ready", "ctx_done")
        ctx_zero, ctx_ready, kmask_ready, m_done, m_ready = ph.sems("ctx_zero", "ctx_ready", "kmask_ready", "m_done",
                                                                    "m_ready")
        d_done, d_eps, d_rec, d_used = ph.sems("d_done", "d_eps", "d_rec", "d_used")
        spill = ph.sems("spill0", "spill1")
        block = ph.block()
        n_cols = N_TOK // D

        @block.sync
        def _(sp):
            for dst, src in ((wq, w["mix_wq"]), (wk, w["mix_wk"]), (wv, w["mix_wv"]), (wo, w["mix_wo"])):
                sp.dma_start(dst[:, :, :], src.rearrange("(c p) n -> p c n", p=P)).then_inc(w_in, 16)

            def body(b, u):
                sp.wait_ge(xnT_ready, b + 1)
                sp.dma_start(G.xnT_dram[:, bass.ds(b * DC * BLK, DC * BLK)],
                             xnT[:, u].rearrange("p c n -> p (c n)")).then_inc(spill[u], 16)
            loop(sp, NB, body)
            for u in range(2):
                sp.wait_ge(spill[u], 16 * NB // 2)

        @block.gpsimd
        def _(pool):
            ln_stats_pool(pool, ln, G)
            pool.memset(ctxT[:, :, :], 0.0).then_inc(ctx_zero, 1)

        @block.vector
        def _(dve):
            ln_stats_vector(dve, ln, G.X)

            def norm_block(b, u):
                dve.wait_ge(t_done, reuse(b))
                for j in range(2):
                    t = b * 2 + j
                    dve.tensor_scalar(xn[:, u, j], token_tile(G.X, t), col(ln.rstd, t), col(ln.shift, t),
                                      ALU.mult, ALU.add).then_inc(xn_ready, 1)

            def body(b, u):
                if not is_last(b, NB):
                    norm_block(b + 1, 1 - u)
                dve.wait_ge(q_exp, b + 1)
                dve.tensor_scalar(rq[:, :, :], psQ[:, :, :], 0.0, scale, ALU.max, ALU.mult).then_inc(q_relu, 1)
                dve.wait_ge(q_relu, b + 1)
                dve.scalar_tensor_tensor(out=G.Q[:, :, bass.ds(b * BLK, BLK)], in0=eq[:, :, :], scalar=1.0,
                                         in1=rq[:, :, :], op0=ALU.min, op1=ALU.add).then_inc(q_ready, 1)
                for j in range(2):
                    t = b * 2 + j
                    dve.wait_ge(k_exp, t + 1)
                    dve.tensor_scalar(rk[:, :], psK[:, :], 0.0, None, ALU.max).then_inc(k_relu, 1)
                    dve.wait_ge(k_relu, t + 1)
                    dve.wait_ge(ctx_done, reuse(t))
                    dve.scalar_tensor_tensor(out=kf[:, j], in0=ek[:, :], scalar=1.0, in1=rk[:, :],
                                             op0=ALU.min, op1=ALU.add).then_inc(k_ready, 1)
            norm_block(0, 0)
            loop(dve, NB, body, peel=1)
            dve.wait_ge(ctx_done, done(NT - 1))
            dve.wait_ge(ctx_zero, 1)
            dve.tensor_copy(ctxT[0:DH, :, 0:DH], psC[0:DH, :, 0:DH]).then_inc(ctx_ready, 1)
            dve.tensor_copy(ctxT[DH:P, :, DH:P], psC[DH:P, :, DH:P]).then_inc(ctx_ready, 1)
            dve.tensor_copy(ksum[:, :], psS[:, :, 0]).then_inc(ctx_ready, 1)
            dve.wait_ge(ctx_ready, 3)
            for c in range(PAIRS):
                dve.tensor_scalar(kmask[:, c], G.headmask[:, :], ksum[:, c:c + 1], None,
                                  ALU.mult).then_inc(kmask_ready, 1)

            def divide(n, u):
                for c in range(DC):
                    s = n * DC + c
                    r = c % 2
                    q = G.Q[:, c, bass.ds(n * D, D)]
                    dve.wait_ge(d_done, s + 1)
                    dve.wait_ge(d_used, reuse(s))
                    dve.tensor_scalar(den[:, r], (psK, psV)[r][:, :], 1e-8, None, ALU.add).then_inc(d_eps, 1)
                    dve.wait_ge(d_eps, s + 1)
                    dve.reciprocal(den[:, r], den[:, r]).then_inc(d_rec, 1)
                    dve.wait_ge(d_rec, s + 1)
                    dve.tensor_tensor(q, q, den[:, r], ALU.mult).then_inc(d_used, 1)
            lead(dve, d_used)
            loop(dve, n_cols, divide, 1)

        @block.scalar
        def _(act):
            def body(b, u):
                act.wait_ge(t_done, done(b))
                act.wait_ge(v_done, reuse(b, 2))
                act.wait_ge(spill[u], (b - u) * 8)
                act.activation(xnT[:, u], psT[:, :, :], ACT.Copy).then_inc(xnT_ready, 1)
                act.wait_ge(q_done, b + 1)
                act.wait_ge(q_ready, b)
                act.activation(eq[:, :, :], psQ[:, :, :], ACT.Exp, scale=scale).then_inc(q_exp, 1)
                for j in range(2):
                    t = b * 2 + j
                    act.wait_ge(k_done, t + 1)
                    act.wait_ge(k_ready, t)
                    act.activation(ek[:, :], psK[:, :], ACT.Exp).then_inc(k_exp, 1)
                    act.wait_ge(v_done, t + 3)
                    act.wait_ge(ctx_done, reuse(t))
                    act.activation(vf[:, j], psV[:, :], ACT.Copy).then_inc(v_ready, 1)
            loop(act, NB, body)
            for c in range(PAIRS):
                act.wait_ge(m_done, c + 1)
                act.activation(G.M[:, c], psQ[:, 2 * (c % 2):2 * (c % 2) + 2].rearrange("p c n -> p (c n)"),
                               ACT.Copy).then_inc(m_ready, 1)

        @block.tensor
        def _(pe):
            lead(pe, t_done)
            lead(pe, v_done, 2)
            lead(pe, ctx_done)

            def context(t, j):
                pe.wait_ge(k_ready, t + 1)
                pe.wait_ge(v_ready, t + 1)
                for c in range(PAIRS):
                    first = isinstance(t, int) and t == 0 and c == 0
                    pe.matmul(psC[:, c], vf[:, j, c * P:(c + 1) * P], kf[:, j, c * P:(c + 1) * P],
                              start=first, stop=is_last(t, NT), skip_group_check=True)
                for c in range(PAIRS):
                    first = isinstance(t, int) and t == 0 and c == 0
                    mm = pe.matmul(psS[:, c], kf[:, j, c * P:(c + 1) * P], G.ones[:, 0:2],
                                   start=first, stop=is_last(t, NT), skip_group_check=True)
                mm.then_inc(ctx_done, 1)

            def body(b, u):
                pe.wait_ge(xn_ready, b * 2 + 2)
                pe.wait_ge(xnT_ready, b)
                for c in range(DC):
                    for j in range(2):
                        mm = pe.transpose(psT[:, c, j * P:(j + 1) * P], xn[:, u, j, c * P:(c + 1) * P], G.ident[:, :])
                mm.then_inc(t_done, 1)
                pe.wait_ge(xnT_ready, b + 1)
                pe.wait_ge(q_ready, b)
                for c in range(DC):
                    for d in range(DC):
                        mm = pe.matmul(psQ[:, c], wq[:, d, c * P:(c + 1) * P], xnT[:, u, d], start=(d == 0),
                                       stop=(d == DC - 1))
                mm.then_inc(q_done, 1)
                for j in range(2):
                    t = b * 2 + j
                    for ps, wt, free, sem in ((psK, wk, k_ready, k_done), (psV, wv, v_ready, v_done)):
                        pe.wait_ge(free, t)
                        for d in range(DC):
                            mm = pe.matmul(ps[:, :], xnT[:, u, d, j * P:(j + 1) * P], wt[:, d], start=(d == 0),
                                           stop=(d == DC - 1))
                        mm.then_inc(sem, 1)
                for j in range(2):
                    context(b * 2 + j, j)
            pe.wait_ge(w_in, 64)
            body(0, 0)
            body(1, 1)
            with pe.Fori(1, NB // 2 - 1) as i:
                for u in range(2):
                    body(i * 2 + u, u)
            body(NB - 2, 0)
            body(NB - 1, 1)
            pe.wait_ge(ctx_ready, 3)
            for c in range(PAIRS):
                if c == 0:
                    pe.wait_ge(q_ready, NB)
                if c >= 2:
                    pe.wait_ge(m_ready, c - 1)
                pe.matmul(psQ[:, 2 * (c % 2):2 * (c % 2) + 2].rearrange("p c n -> p (c n)"), ctxT[:, c], wo[:, c],
                          start=True, stop=True).then_inc(m_done, 1)
            pe.wait_ge(kmask_ready, PAIRS)

            def denominators(n, u):
                for c in range(DC):
                    s = n * DC + c
                    pe.wait_ge(d_used, reuse(s))
                    pe.matmul((psK, psV)[c % 2][:, :], kmask[:, c], G.Q[:, c, bass.ds(n * D, D)], start=True,
                              stop=True).then_inc(d_done, 1)
            loop(pe, n_cols, denominators, 1)


def graph_attention(nc, G, w):
    VW = DH + 2
    with Phase(nc, "attn") as ph:
        wq, wk, wv, wo = (ph.sb(n, [P, DC, D]) for n in ("wq", "wk", "wv", "wo"))
        bq, bk = (ph.sb(n, [P, DC]) for n in ("bq", "bk"))
        bv, bo, bsum = (ph.sb(n, [P, D]) for n in ("bv", "bo", "bsum"))
        xnT = ph.sb("xnT", [P, 2, DC, BLK])
        mq = ph.sb("mq", [P, 2, DC, BLK])
        qT = ph.sb("qT", [P, 2, DC, BLK])
        kT = ph.sb("kT", [P, 2, DC, BLK])
        v = ph.sb("v", [P, 2, HEADS, VW])
        s = ph.sb("s", [P, 2, HEADS, GRAPH])
        top = ph.sb("top", [P, 2, HEADS])
        prob = ph.sb("prob", [P, 2, HEADS, P])
        probT = ph.sb("probT", [P, 2, 4, P])
        rsum = ph.sb("rsum", [P, HEADS])
        o = ph.sb("o", [P, HEADS, DH])
        oT = ph.sb("oT", [P, DC, P])
        y = ph.sb("y", [P, D])
        psQ = ph.ps("psQ", [P, DC, BLK])
        psV = ph.ps("psV", [P, D])
        psS = ph.ps("psS", [P, 2, D])
        psP = ph.ps("psP", [P, 4, P])
        psO = ph.ps("psO", [P, 2, D])
        names = ("w_in bsum_ready prob_zero v_ones x_in0 x_in1 mq_ready passed_pool passed_pe q_done q_ready v_done "
                 "v_ready s_done s_biased top_ready s_ready p_ready t_done pT_ready o_done rsum_ready o_ready oT_done "
                 "oT_ready y_done y_ready x_ready").split()
        S = dict(zip(names, ph.sems(*names)))
        S = type("Sems", (), S)
        x_in = [S.x_in0, S.x_in1]
        block = ph.block()

        @block.sync
        def _(sp):
            for dst, name in ((wq, "Wq"), (wk, "Wk"), (wv, "Wv"), (wo, "Wo")):
                sp.dma_start(dst[:, :, :], w[name].rearrange("(c p) n -> p c n", p=P)).then_inc(S.w_in, 16)
            for dst, name in ((bq, "bq"), (bk, "bk")):
                sp.dma_start(dst[:, :], w[name]).then_inc(S.w_in, 16)
            for dst, name in ((bv, "bv"), (bo, "bo"), (bsum, "b_out")):
                sp.dma_start(dst[:, :], w[name].partition_broadcast(P)).then_inc(S.w_in, 16)

            def body(b, u):
                sp.wait_ge(S.v_done, reuse(b, 2))
                sp.dma_start(xnT[:, u].rearrange("p c n -> p (c n)"),
                             G.xnT_dram[:, bass.ds(b * DC * BLK, DC * BLK)]).then_inc(x_in[u], 16)
            loop(sp, NB, body)

        @block.gpsimd
        def _(pool):
            pool.memset(prob[:, :, :, :], 0.0).then_inc(S.prob_zero, 1)
            pool.memset(v[:, :, :, DH:VW], 1.0).then_inc(S.v_ones, 1)

            def body(b, u):
                gate(pool, S.y_done, reuse(b, 2), S.passed_pool)
                pool.tensor_copy(mq[:, u], G.Q[:, :, bass.ds(b * BLK, BLK)]).then_inc(S.mq_ready, 1)
            loop(pool, NB, body)

        @block.vector
        def _(dve):
            dve.wait_ge(S.w_in, 16 * 9)
            dve.tensor_tensor(bsum[:, :], bsum[:, :], bo[:, :], ALU.add).then_inc(S.bsum_ready, 1)
            dve.wait_ge(S.bsum_ready, 1)
            dve.wait_ge(S.v_ones, 1)

            def front(t, j):
                dve.wait_ge(S.v_done, t + 1 + 2 * LEAD)
                dve.wait_ge(S.o_done, reuse(t))
                dve.tensor_tensor(v[:, j, :, 0:DH], psV[:, :].rearrange("p (h d) -> p h d", h=HEADS),
                                  bv[:, :].rearrange("p (h d) -> p h d", h=HEADS), ALU.add).then_inc(S.v_ready, 1)
                dve.wait_ge(S.s_done, t + 1)
                dve.wait_ge(S.p_ready, reuse(t, 2))
                bias = G.BIAS[:, bass.ds(t * GRAPH * HEADS, GRAPH * HEADS)].rearrange(
                    "p (m h r) -> p r h m", m=GRAPH, r=2)
                heads = s[:, j].rearrange("p (h r) m -> p r h m", r=2)
                for r in range(2):
                    dve.scalar_tensor_tensor(out=heads[:, r], in0=psS[:, r, 0:4 * GRAPH].rearrange(
                        "p (h m) -> p h m", h=4), scalar=DH ** -0.5, in1=bias[:, r], op0=ALU.mult,
                        op1=ALU.add).then_inc(S.s_biased, 1)
                dve.wait_ge(S.s_biased, t * 2 + 2)
                dve.tensor_reduce(top[:, j], s[:, j], AX.X, ALU.max).then_inc(S.top_ready, 1)
                dve.wait_ge(S.top_ready, t + 1)
                dve.tensor_tensor(s[:, j], s[:, j], top[:, j].unsqueeze(2).to_broadcast([P, HEADS, GRAPH]),
                                  ALU.subtract).then_inc(S.s_ready, 1)

            def back(t, j):
                sums = psO[:, :, 0:4 * VW].rearrange("p r (h d) -> p r h d", h=4)
                dve.wait_ge(S.o_done, done(t))
                dve.reciprocal(rsum[:, :].rearrange("p (r h) -> p r h", r=2), sums[:, :, :, DH]).then_inc(S.rsum_ready, 1)
                dve.wait_ge(S.rsum_ready, t + 1)
                dve.wait_ge(S.oT_done, t)
                for r in range(2):
                    dve.tensor_tensor(o[:, 4 * r:4 * r + 4], sums[:, r, :, 0:DH],
                                      rsum[:, 4 * r:4 * r + 4].unsqueeze(2).to_broadcast([P, 4, DH]),
                                      ALU.mult).then_inc(S.o_ready, 1)
                dve.wait_ge(S.y_done, t + 1 + 2 * LEAD)
                dve.wait_ge(S.x_ready, t)
                dve.tensor_tensor(y[:, :], psV[:, :], bsum[:, :], ALU.add).then_inc(S.y_ready, 1)
                dve.wait_ge(S.y_ready, t + 1)
                dve.tensor_tensor(token_tile(G.X, t), token_tile(G.X, t), y[:, :], ALU.add).then_inc(S.x_ready, 1)

            def body(b, u):
                front(b * 2 + 1, 1)
                back(b * 2, 0)
                if not is_last(b, NB):
                    front(b * 2 + 2, 0)
                back(b * 2 + 1, 1)
            front(0, 0)
            loop(dve, NB, body, peel=1)

        @block.scalar
        def _(act):
            act.wait_ge(S.w_in, 16 * 9)
            act.wait_ge(S.prob_zero, 1)
            lead(act, S.p_ready, 2)

            def project(b, u):
                for k, (dst, bias) in enumerate(((qT, bq), (kT, bk))):
                    act.wait_ge(S.q_done, b * 2 + k + 1)
                    for c in range(DC):
                        act.activation(dst[:, u, c], psQ[:, c], ACT.Identity, bias=bias[:, c:c + 1],
                                       ).then_inc(S.q_ready, 1)

            def exponentials(t, j):
                act.wait_ge(S.s_ready, t + 1)
                act.wait_ge(S.t_done, t * 2)
                for g in range(2):
                    h = slice(g * GRAPH, (g + 1) * GRAPH)
                    act.activation(prob[h, j, :, h], s[h, j], ACT.Exp).then_inc(S.p_ready, 1)

            def transposed(t, j):
                for r in range(2):
                    act.wait_ge(S.t_done, t * 2 + r + 1)
                    if r == 0:
                        act.wait_ge(S.o_done, t + LEAD)
                    act.activation(probT[:, r], psP[:, :, :], ACT.Copy).then_inc(S.pT_ready, 1)

            def output(t, j):
                act.wait_ge(S.oT_done, t + 1)
                act.wait_ge(S.y_done, t + 2 * LEAD)
                act.activation(oT[:, :, :], psP[:, :, :], ACT.Copy).then_inc(S.oT_ready, 1)

            def body(b, u):
                transposed(b * 2, 0)
                exponentials(b * 2 + 1, 1)
                output(b * 2, 0)
                if not is_last(b, NB):
                    project(b + 1, 1 - u)
                transposed(b * 2 + 1, 1)
                if not is_last(b, NB):
                    exponentials(b * 2 + 2, 0)
                output(b * 2 + 1, 1)
            project(0, 0)
            exponentials(0, 0)
            loop(act, NB, body, peel=1)

        @block.tensor
        def _(pe):
            pe.wait_ge(S.w_in, 16 * 9)
            lead(pe, S.v_done, 2)
            lead(pe, S.o_done)
            lead(pe, S.y_done, 2)

            def project(b, u):
                pe.wait_ge(x_in[u], (b - u) * 8 + 16)
                for k, wt in enumerate((wq, wk)):
                    pe.wait_ge(S.q_ready, (b * 2 + k) * DC)
                    for c in range(DC):
                        for d in range(DC):
                            mm = pe.matmul(psQ[:, c], wt[:, d, c * P:(c + 1) * P], xnT[:, u, d], start=(d == 0),
                                           stop=(d == DC - 1))
                    mm.then_inc(S.q_done, 1)

            def front(t, u, j):
                pe.wait_ge(S.v_ready, t)
                if not (isinstance(t, int) and t == 0):
                    pe.wait_ge(S.y_ready, t - 1)
                for d in range(DC):
                    mm = pe.matmul(psV[:, :], xnT[:, u, d, j * P:(j + 1) * P], wv[:, d], start=(d == 0),
                                   stop=(d == DC - 1))
                mm.then_inc(S.v_done, 1)
                if j == 0:
                    pe.wait_ge(S.q_ready, (t + 2) * DC)
                gate(pe, S.s_biased, t * 2, S.passed_pe)
                for h in range(HEADS):
                    r = slice((h % 2) * DH, (h % 2 + 1) * DH)
                    for g in range(2):
                        n = slice(j * P + g * GRAPH, j * P + (g + 1) * GRAPH)
                        mm = pe.matmul(psS[g * GRAPH:(g + 1) * GRAPH, h % 2, (h // 2) * GRAPH:(h // 2 + 1) * GRAPH],
                                       qT[r, u, h // 2, n], kT[r, u, h // 2, n], start=True, stop=True)
                mm.then_inc(S.s_done, 1)

            def back(t, b, u, j):
                pe.wait_ge(S.p_ready, (t + 1 + LEAD) * 2)
                for r in range(2):
                    pe.wait_ge(*((S.oT_ready, t) if r == 0 else (S.pT_ready, t * 2 + 1)))
                    for h in range(4):
                        mm = pe.transpose(psP[:, h], prob[:, j, 4 * r + h], G.ident[:, :])
                    mm.then_inc(S.t_done, 1)
                pe.wait_ge(S.v_ready, t + 1)
                pe.wait_ge(S.o_ready, t * 2)
                for r in range(2):
                    pe.wait_ge(S.pT_ready, t * 2 + r + 1)
                    for h in range(4):
                        mm = pe.matmul(psO[:, r, h * VW:(h + 1) * VW], probT[:, r, h], v[:, j, 4 * r + h],
                                       start=True, stop=True)
                mm.then_inc(S.o_done, 1)
                pe.wait_ge(S.o_ready, t * 2 + 2)
                for c in range(DC):
                    mm = pe.transpose(psP[:, c], o[:, 2 * c:2 * c + 2].rearrange("p h d -> p (h d)"), G.ident[:, :])
                mm.then_inc(S.oT_done, 1)
                if is_last(t, NT):
                    pe.wait_ge(S.y_ready, t)
                else:
                    pe.wait_ge(S.v_ready, t + 2)
                if j == 0:
                    pe.wait_ge(S.mq_ready, b + 1)
                for c in range(DC):
                    pe.matmul(psV[:, :], mq[:, u, c, j * P:(j + 1) * P], G.M[:, c], start=(c == 0), stop=False)
                pe.wait_ge(S.oT_ready, t + 1)
                for c in range(DC):
                    mm = pe.matmul(psV[:, :], oT[:, c], wo[:, c], start=False, stop=(c == DC - 1))
                mm.then_inc(S.y_done, 1)

            def body(b, u):
                front(b * 2 + 1, u, 1)
                back(b * 2, b, u, 0)
                if not is_last(b, NB):
                    project(b + 1, 1 - u)
                    front(b * 2 + 2, 1 - u, 0)
                back(b * 2 + 1, b, u, 1)
            project(0, 0)
            front(0, 0, 0)
            loop(pe, NB, body, peel=1)


def route(nc, G, w, pre, shared):
    FS = 4
    with Phase(nc, f"route{pre}") as ph:
        wr = ph.sb("wr", [P, DC, EXPERTS])
        br = ph.sb("br", [P, EXPERTS])
        ln = ln_stats_buffers(ph)
        hn = ph.sb("hn", [P, 2, 2, D])
        H = ph.sb("H", [P, NT, D])
        hT = ph.sb("hT", [P, 2, DC, BLK])
        L = ph.sb("L", [P, NT, EXPERTS])
        small = [ph.sb(f"small{i}", [P, NT]) for i in range(3)]
        pv = ph.sb("pv", [P, NT, 8])
        pidx = ph.sb("pidx", [P, NT, 8], U32)
        which = ph.sb("which", [P, NT, TOPK])
        onehot = ph.sb("onehot", [P, EXPERTS, TOPK * NT])
        rank = ph.sb("rank", [P, EXPERTS, TOPK * NT])
        part1 = ph.sb("part1", [P, NT, EXPERTS])
        slot = ph.sb("slot", [P, TOPK * NT])
        bs = bucket_starts(ph, EXPERTS, SLOT_TILE, NST, ph.sb("past", [P, NST, EXPERTS]))
        psT = ph.ps("psT", [P, DC, BLK])
        psL = ph.ps("psL", [P, 2, EXPERTS])
        names = ("w_in passed_pe passed_pool kept h_ready t_done hT_ready l_done l_ready step exps_ready count_step slotted scattered "
                 "hid_done hid_ready y_done y_ready x_ready srow_ready").split()
        S = type("Sems", (), dict(zip(names, ph.sems(*names))))
        n_w = 2
        if shared:
            w1 = ph.sb("w1", [P, DC, FS * P])
            w2 = ph.sb("w2", [P, FS, D])
            b1 = ph.sb("b1", [P, FS])
            brow = ph.sb("brow", [P, 2, D])
            srow = ph.sb("srow", [P, D])
            hid = ph.sb("hid", [P, 2, FS, BLK])
            y = ph.sb("y", [P, D])
            psH = [ph.ps(f"psH{i}", [P, D]) for i in range(2)]
            psY = ph.ps("psY", [P, D])
            n_w = 7
        block = ph.block()

        @block.sync
        def _(sp):
            sp.dma_start(wr[:, :, :], w[pre + "Wr"].rearrange("(c p) n -> p c n", p=P)).then_inc(S.w_in, 16)
            sp.dma_start(br[:, :], w[pre + "br"].partition_broadcast(P)).then_inc(S.w_in, 16)
            if shared:
                sp.dma_start(w1[:, :, :], w["sw1"].rearrange("(c p) n -> p c n", p=P)).then_inc(S.w_in, 16)
                sp.dma_start(w2[:, :, :], w["sw2"].rearrange("(c p) n -> p c n", p=P)).then_inc(S.w_in, 16)
                sp.dma_start(b1[:, :], w["sb1"]).then_inc(S.w_in, 16)
                for n in range(2):
                    sp.dma_start(brow[:, n], w["sb2"][n].partition_broadcast(P)).then_inc(S.w_in, 16)

        @block.gpsimd
        def _(pool):
            ln_stats_pool(pool, ln, G)
            bucket_starts_pool(pool, bs)
            lead(pool, S.kept)

            def keep(b, u):
                gate(pool, S.h_ready, b * 2 + 2, S.passed_pool)
                pool.tensor_copy(H[:, bass.ds(b * 2, 2), :], hn[:, u]).then_inc(S.kept, 1)
            loop(pool, NB, keep)
            pool.wait_ge(S.kept, done(NB - 1))
            pool.wait_ge(S.slotted, 5)
            for k in range(TOPK):
                for t in range(NT):
                    n = k * NT + t
                    pool.indirect_dma_start(
                        out=G.xs_dram, out_offset=bass.IndirectOffsetOnAxis(ap=G.place[:, n:n + 1], axis=0),
                        in_=H[:, t], in_offset=None).then_inc(S.scattered, 16)
            pool.wait_ge(S.scattered, 16 * TOPK * NT)

        @block.vector
        def _(dve):
            ln_stats_vector(dve, ln, G.X)
            dve.wait_ge(S.w_in, 16 * n_w)
            if shared:
                dve.tensor_tensor(srow[:, :], brow[:, 0], brow[:, 1], ALU.add).then_inc(S.srow_ready, 1)
                dve.wait_ge(S.srow_ready, 1)

            def norm_block(b, u):
                dve.wait_ge(S.t_done, reuse(b))
                dve.wait_ge(S.kept, reuse(b))
                for j in range(2):
                    t = b * 2 + j
                    dve.tensor_scalar(hn[:, u, j], token_tile(G.X, t), col(ln.rstd, t), col(ln.shift, t),
                                      ALU.mult, ALU.add).then_inc(S.h_ready, 1)

            def body(b, u):
                if not is_last(b, NB):
                    norm_block(b + 1, 1 - u)
                dve.wait_ge(S.l_done, b + 1)
                dve.tensor_tensor(L[:, bass.ds(b * 2, 2), :], psL[:, :, :],
                                  br[:, :].unsqueeze(1).to_broadcast([P, 2, EXPERTS]), ALU.add).then_inc(S.l_ready, 1)
                if shared:
                    for j in range(2):
                        t = b * 2 + j
                        dve.wait_ge(S.y_done, t + 1 + 2 * LEAD)
                        dve.wait_ge(S.x_ready, t)
                        dve.tensor_tensor(y[:, :], psY[:, :], srow[:, :], ALU.add).then_inc(S.y_ready, 1)
                        dve.wait_ge(S.y_ready, t + 1)
                        dve.tensor_tensor(token_tile(G.X, t), token_tile(G.X, t), y[:, :],
                                          ALU.add).then_inc(S.x_ready, 1)
            norm_block(0, 0)
            loop(dve, NB, body, peel=1)
            st = Step(dve, S.step, 0, 64)

            def spread(a):
                return a[:, :].unsqueeze(2).to_broadcast([P, NT, EXPERTS])
            dve.wait_ge(S.l_ready, NB)
            st.do(dve.tensor_reduce(small[0][:, :], L[:, :, :], AX.X, ALU.max))
            st.do(dve.tensor_tensor(L[:, :, :], L[:, :, :], spread(small[0]), ALU.subtract))
            dve.wait_ge(S.exps_ready, 1)
            st.do(dve.tensor_reduce(small[1][:, :], L[:, :, :], AX.X, ALU.add))
            st.do(dve.reciprocal(small[2][:, :], small[1][:, :]))
            st.do(dve.tensor_tensor(L[:, :, :], L[:, :, :], spread(small[2]), ALU.mult))
            for t in range(NT):
                st.did(dve.max(pv[:, t], L[:, t]))
            st.wait()
            for t in range(NT):
                st.did(dve.max_index(pidx[:, t], pv[:, t], L[:, t]))
            st.wait()
            st.did(dve.tensor_copy(which[:, :, :], pidx[:, :, 0:TOPK]))
            st.do(dve.tensor_copy(G.gate[:, :, :], pv[:, :, 0:TOPK]))
            for k in range(TOPK):
                st.did(dve.tensor_tensor(
                    onehot[:, :, k * NT:(k + 1) * NT], G.iota512[:, 0:EXPERTS].unsqueeze(2).to_broadcast([P, EXPERTS, NT]),
                    which[:, :, k].unsqueeze(1).to_broadcast([P, EXPERTS, NT]), ALU.is_equal))
            st.wait()
            dve.tensor_reduce(bs.count[:, :], onehot[:, :, :], AX.X, ALU.add).then_inc(bs.counted, 1)
            for k, dst in enumerate((G.comb, part1)):
                st.did(dve.tensor_tensor(dst[:, :, :], onehot[:, :, k * NT:(k + 1) * NT].rearrange("p e t -> p t e"),
                                         G.gate[:, :, k].unsqueeze(2).to_broadcast([P, NT, EXPERTS]), ALU.mult))
            st.wait()
            st.do(dve.tensor_tensor(G.comb[:, :, :], G.comb[:, :, :], part1[:, :, :], ALU.add))
            bucket_starts_vector(dve, bs)
            for e in range(EXPERTS):
                st.did(dve.tensor_tensor_scan(rank[:, e], onehot[:, e], onehot[:, e], bs.first[:, e:e + 1], ALU.add,
                                              ALU.bypass))
            st.wait()
            sl = Step(dve, S.slotted, 0, 8)
            sl.do(dve.tensor_tensor(rank[:, :, :], rank[:, :, :], onehot[:, :, :], ALU.mult))
            sl.do(dve.tensor_reduce(slot[:, :], rank[:, :, :].rearrange("p e n -> p n e"), AX.X, ALU.add))
            sl.did(dve.tensor_copy(G.place[:, :], slot[:, :]))
            sl.do(dve.tensor_scalar(bs.bucket[:, :], bs.bucket[:, :], float(P), None, ALU.mult))
            sl.did(dve.tensor_scalar(G.wrow[:, :], bs.bucket[:, :], G.part[:, 0:1], None, ALU.add))

        @block.scalar
        def _(act):
            act.wait_ge(S.w_in, 16 * n_w)

            lead(act, S.hid_ready)

            def body(b, u):
                act.wait_ge(S.t_done, done(b))
                act.activation(hT[:, u], psT[:, :, :], ACT.Copy).then_inc(S.hT_ready, 1)
                if shared:
                    for f in range(FS):
                        n = b * FS + f
                        act.wait_ge(S.hid_done, n + 1)
                        if f == 0:
                            act.wait_ge(S.y_done, reuse(b, 2))
                        act.activation(hid[:, u, f], psH[f % 2][:, 0:BLK], ACT.Gelu,
                                       bias=b1[:, f:f + 1]).then_inc(S.hid_ready, 1)
            loop(act, NB, body)
            act.wait_ge(S.step, 2)
            act.activation(L[:, :, :], L[:, :, :], ACT.Exp).then_inc(S.exps_ready, 1)

        @block.tensor
        def _(pe):
            pe.wait_ge(S.w_in, 16 * n_w)
            lead(pe, S.t_done)
            lead(pe, S.y_done, 2)

            def transposes(b, u):
                pe.wait_ge(S.h_ready, b * 2 + 2)
                pe.wait_ge(S.hT_ready, b)
                for c in range(DC):
                    for j in range(2):
                        mm = pe.transpose(psT[:, c, j * P:(j + 1) * P], hn[:, u, j, c * P:(c + 1) * P], G.ident[:, :])
                mm.then_inc(S.t_done, 1)

            def body(b, u):
                pe.wait_ge(S.hT_ready, b + 1)
                gate(pe, S.l_ready, b, S.passed_pe)
                for j in range(2):
                    for c in range(DC):
                        mm = pe.matmul(psL[:, j], hT[:, u, c, j * P:(j + 1) * P], wr[:, c], start=(c == 0),
                                       stop=(c == DC - 1))
                mm.then_inc(S.l_done, 1)
                if shared:
                    for f in range(FS):
                        pe.wait_ge(S.hid_ready, b * FS + f - 1 + LEAD)
                        for c in range(DC):
                            mm = pe.matmul(psH[f % 2][:, 0:BLK], w1[:, c, f * P:(f + 1) * P], hT[:, u, c],
                                           start=(c == 0), stop=(c == DC - 1))
                        mm.then_inc(S.hid_done, 1)
                if not is_last(b, NB):
                    transposes(b + 1, 1 - u)
                if shared:
                    pe.wait_ge(S.hid_ready, b * FS + FS + LEAD)
                    for j in range(2):
                        pe.wait_ge(S.y_ready, b * 2 + j)
                        for f in range(FS):
                            mm = pe.matmul(psY[:, :], hid[:, u, f, j * P:(j + 1) * P], w2[:, f], start=(f == 0),
                                           stop=(f == FS - 1))
                        mm.then_inc(S.y_done, 1)
            transposes(0, 0)
            loop(pe, NB, body, peel=1)
            bucket_starts_tensor(pe, bs, G, 1)


def experts(nc, G, w, pre, F):
    FC = F // P
    RING = 4
    with Phase(nc, f"experts{pre}") as ph:
        w1 = ph.sb("w1", [P, 2, DC * F])
        w2 = ph.sb("w2", [P, 2, FC * D])
        b1 = ph.sb("b1", [P, 2, FC])
        rows = ph.sb("rows", [P, 2], I32)
        xs = ph.sb("xs", [P, 2, 2, D])
        xsT = ph.sb("xsT", [P, 2, DC, BLK])
        hid = ph.sb("hid", [P, 2, FC, BLK])
        y = ph.sb("y", [P, 2, 2, D])
        psT = ph.ps("psT", [P, DC, BLK])
        psH = [ph.ps(f"psH{i}", [P, D]) for i in range(RING)]
        psY = [ph.ps(f"psY{i}", [P, D]) for i in range(2)]
        names = ("passed row_ready w_in0 w_in1 xs_in0 xs_in1 t_done xsT_ready hid_done hid_ready y_done y_ready "
                 "stored0 stored1").split()
        S = type("Sems", (), dict(zip(names, ph.sems(*names))))
        w_in, xs_in, stored = (S.w_in0, S.w_in1), (S.xs_in0, S.xs_in1), (S.stored0, S.stored1)
        block = ph.block()
        xs_dram = G.xs_dram.rearrange("(n p j) d -> p n (j d)", p=P, j=2)
        ys_dram = G.ys_dram.rearrange("(n p j) d -> p n (j d)", p=P, j=2)

        @block.gpsimd
        def _(pool):
            def load(g, u):
                gate(pool, S.y_done, reuse(g, 2), S.passed)
                pool.tensor_copy(rows[:, u:u + 1], col(G.wrow, g)).then_inc(S.row_ready, 1)
                gate(pool, S.row_ready, g + 1, S.passed)
                for table, dst in ((w[pre + "W1"], w1), (w[pre + "W2"], w2), (w[pre + "b1"], b1)):
                    pool.indirect_dma_start(
                        out=dst[:, u], out_offset=None, in_=table,
                        in_offset=bass.IndirectOffsetOnAxis(ap=rows[:, u:u + 1], axis=0)).then_inc(w_in[u], 16)
            loop(pool, NST, load)

        @block.sync
        def _(sp):
            def load(g, u):
                sp.wait_ge(S.t_done, reuse(g))
                sp.dma_start(xs[:, u].rearrange("p j d -> p (j d)"),
                             xs_dram[:, bass.ds(g, 1), :].rearrange("p a d -> p (a d)")).then_inc(xs_in[u], 16)

            def store(g, u):
                sp.wait_ge(S.y_ready, (g + 1 + LEAD) * 2)
                sp.dma_start(ys_dram[:, bass.ds(g, 1), :].rearrange("p a d -> p (a d)"),
                             y[:, u].rearrange("p j d -> p (j d)")).then_inc(stored[u], 16)

            def body(g, u):
                if not is_last(g, NST):
                    load(g + 1, 1 - u)
                store(g, u)
            load(0, 0)
            loop(sp, NST, body, peel=1)
            for u in range(2):
                sp.wait_ge(stored[u], 16 * ((NST + 1 - u) // 2))

        @block.vector
        def _(dve):
            lead(dve, S.y_ready, 2)

            def transposed(g, u):
                dve.wait_ge(S.t_done, done(g))
                dve.tensor_copy(xsT[:, u], psT[:, :, :]).then_inc(S.xsT_ready, 1)

            def body(g, u):
                if not is_last(g, NST):
                    transposed(g + 1, 1 - u)
                dve.wait_ge(stored[u], (g - u) * 8)
                for j in range(2):
                    dve.wait_ge(S.y_done, g * 2 + j + 1 + 2 * LEAD)
                    dve.tensor_copy(y[:, u, j], psY[j][:, :]).then_inc(S.y_ready, 1)
            transposed(0, 0)
            loop(dve, NST, body, peel=1)

        @block.scalar
        def _(act):
            lead(act, S.hid_ready, RING)

            def body(g, u):
                act.wait_ge(w_in[u], (g - u) * 24 + 48)
                act.wait_ge(S.y_done, reuse(g, 2))
                for f in range(FC):
                    act.wait_ge(S.hid_done, g * FC + f + 1)
                    act.activation(hid[:, u, f], psH[(u * FC + f) % RING][:, 0:BLK], ACT.Gelu,
                                   bias=b1[:, u, f:f + 1]).then_inc(S.hid_ready, 1)
            loop(act, NST, body)

        @block.tensor
        def _(pe):
            lead(pe, S.t_done)
            lead(pe, S.y_done, 2)

            def transposes(g, u):
                pe.wait_ge(xs_in[u], (g - u) * 8 + 16)
                pe.wait_ge(S.xsT_ready, g)
                for c in range(DC):
                    for j in range(2):
                        mm = pe.transpose(psT[:, c, j * P:(j + 1) * P], xs[:, u, j, c * P:(c + 1) * P], G.ident[:, :])
                mm.then_inc(S.t_done, 1)

            def body(g, u):
                pe.wait_ge(w_in[u], (g - u) * 24 + 48)
                pe.wait_ge(S.xsT_ready, g + 1)
                for f in range(FC):
                    pe.wait_ge(S.hid_ready, g * FC + f + 1)
                    for c in range(DC):
                        mm = pe.matmul(psH[(u * FC + f) % RING][:, 0:BLK], w1[:, u, c * F + f * P:c * F + (f + 1) * P],
                                       xsT[:, u, c], start=(c == 0), stop=(c == DC - 1))
                    mm.then_inc(S.hid_done, 1)
                if not is_last(g, NST):
                    transposes(g + 1, 1 - u)
                pe.wait_ge(S.hid_ready, g * FC + FC + RING)
                for j in range(2):
                    pe.wait_ge(S.y_ready, g * 2 + j + 1)
                    for f in range(FC):
                        mm = pe.matmul(psY[j][:, :], hid[:, u, f, j * P:(j + 1) * P], w2[:, u, f * D:(f + 1) * D],
                                       start=(f == 0), stop=(f == FC - 1))
                    mm.then_inc(S.y_done, 1)
            transposes(0, 0)
            loop(pe, NST, body, peel=1)


def combine(nc, G, w, pre, out):
    with Phase(nc, f"combine{pre}") as ph:
        b2 = ph.sb("b2", [EXPERTS, D])
        place = ph.sb("place", [P, 2, TOPK], I32)
        comb = ph.sb("comb", [P, 2, EXPERTS])
        combT = ph.sb("combT", [EXPERTS, 2, P])
        y = ph.sb("y", [P, 2, TOPK, D])
        psT = ph.ps("psT", [EXPERTS, P])
        psB = [ph.ps(f"psB{i}", [P, D]) for i in range(2)]
        names = ("w_in passed place_ready y_in0 y_in1 comb_ready t_done combT_ready b_done x_biased x_first x_ready "
                 "out0 out1").split()
        S = type("Sems", (), dict(zip(names, ph.sems(*names))))
        y_in, stored = (S.y_in0, S.y_in1), (S.out0, S.out1)
        block = ph.block()

        @block.sync
        def _(sp):
            sp.dma_start(b2[:, :], w[pre + "b2"]).then_inc(S.w_in, 16)
            if out is not None:
                rows = out.rearrange("(t p) d -> p t d", p=P)

                def body(t, u):
                    sp.wait_ge(S.x_ready, done(t))
                    sp.dma_start(rows[:, bass.ds(t, 1), :].rearrange("p a d -> p (a d)"),
                                 token_tile(G.X, t)).then_inc(stored[u], 16)
                loop(sp, NT, body)
                for u in range(2):
                    sp.wait_ge(stored[u], 16 * NT // 2)

        @block.gpsimd
        def _(pool):
            lead(pool, S.place_ready)

            def body(t, u):
                gate(pool, S.x_ready, reuse(t), S.passed)
                pool.tensor_copy(place[:, u], G.place[:, :].rearrange("p (k t) -> p t k", k=TOPK)[
                    :, bass.ds(t, 1), :].rearrange("p a k -> p (a k)")).then_inc(S.place_ready, 1)
                gate(pool, S.place_ready, done(t), S.passed)
                for k in range(TOPK):
                    pool.indirect_dma_start(
                        out=y[:, u, k], out_offset=None, in_=G.ys_dram,
                        in_offset=bass.IndirectOffsetOnAxis(ap=place[:, u, k:k + 1], axis=0)).then_inc(y_in[u], 16)
            loop(pool, NT, body)

        @block.vector
        def _(dve):
            lead(dve, S.x_ready)

            def columns(t, u):
                dve.tensor_copy(comb[:, u], G.comb[:, bass.ds(t, 1), :].rearrange("p a e -> p (a e)")
                                ).then_inc(S.comb_ready, 1)

            def body(t, u):
                if not is_last(t, NT):
                    columns(t + 1, 1 - u)
                x = token_tile(G.X, t)
                gates = G.gate[:, bass.ds(t, 1), :].rearrange("p a k -> p (a k)")
                dve.wait_ge(S.b_done, t + 1)
                dve.tensor_tensor(x, x, psB[u][:, :], ALU.add).then_inc(S.x_biased, 1)
                dve.wait_ge(y_in[u], (t - u) * 16 + 32)
                dve.wait_ge(S.x_biased, t + 1)
                dve.scalar_tensor_tensor(out=x, in0=y[:, u, 0], scalar=gates[:, 0:1], in1=x, op0=ALU.mult,
                                         op1=ALU.add).then_inc(S.x_first, 1)
                dve.wait_ge(S.x_first, t + 1)
                dve.scalar_tensor_tensor(out=x, in0=y[:, u, 1], scalar=gates[:, 1:2], in1=x, op0=ALU.mult,
                                         op1=ALU.add).then_inc(S.x_ready, 1)
            columns(0, 0)
            loop(dve, NT, body, peel=2)

        @block.scalar
        def _(act):
            def body(t, u):
                act.wait_ge(S.t_done, t + 1)
                act.activation(combT[:, u], psT[:, :], ACT.Copy).then_inc(S.combT_ready, 1)
            loop(act, NT, body)

        @block.tensor
        def _(pe):
            pe.wait_ge(S.w_in, 16)

            def body(t, u):
                pe.wait_ge(S.comb_ready, t + 1)
                pe.wait_ge(S.combT_ready, t)
                pe.transpose(psT[:, :], comb[:, u], G.ident[:, :]).then_inc(S.t_done, 1)
                pe.wait_ge(S.combT_ready, t + 1)
                pe.wait_ge(S.x_ready, reuse(t))
                pe.matmul(psB[u][:, :], combT[:, u], b2[:, :], start=True, stop=True).then_inc(S.b_done, 1)
            loop(pe, NT, body)


def neighbour_products(nc, G, w):
    with Phase(nc, "nprod") as ph:
        w12 = ph.sb("w12", [P, 2, DC, D])
        ln = ln_stats_buffers(ph)
        xn = ph.sb("xn", [P, 2, 2, D])
        xnT = ph.sb("xnT", [P, 2, DC, BLK])
        psT = ph.ps("psT", [P, DC, BLK])
        psY = [[ph.ps(f"psY{k}{j}", [P, D]) for j in range(2)] for k in range(2)]
        names = "w_in adj_in xn_ready kept0 kept1 stats t_done xnT_ready y1_done y2_done y1_ready y2_ready".split()
        S = type("Sems", (), dict(zip(names, ph.sems(*names))))
        kept = (S.kept0, S.kept1)
        block = ph.block()

        @block.sync
        def _(sp):
            for k in range(2):
                sp.dma_start(w12[:, k], w["gw"][k * D:(k + 1) * D, :].rearrange("(c p) n -> p c n", p=P)
                             ).then_inc(S.w_in, 16)
            sp.dma_start(G.adj[:, :], G.adj_dram).then_inc(S.adj_in, 16)

            def keep(b, u):
                sp.wait_ge(S.xn_ready, b * 2 + 2)
                sp.dma_start(G.xn_dram[:, bass.ds(b * 2 * D, 2 * D)],
                             xn[:, u].rearrange("p j d -> p (j d)")).then_inc(kept[u], 16)
            loop(sp, NB, keep)
            for u in range(2):
                sp.wait_ge(kept[u], 16 * NB // 2)
            sp.wait_ge(S.adj_in, 16)

        @block.gpsimd
        def _(pool):
            ln_stats_pool(pool, ln, G)

        @block.vector
        def _(dve):
            ln_stats_vector(dve, ln, G.X)

            def norm_block(b, u):
                dve.wait_ge(S.t_done, reuse(b))
                dve.wait_ge(kept[u], (b - u) * 8)
                for j in range(2):
                    t = b * 2 + j
                    dve.tensor_scalar(xn[:, u, j], token_tile(G.X, t), col(ln.rstd, t), col(ln.shift, t),
                                      ALU.mult, ALU.add).then_inc(S.xn_ready, 1)
                dve.wait_ge(S.xn_ready, b * 2 + 2)
                for j in range(2):
                    dve.bn_stats(G.bn[:, bass.ds(b * 2 + j, 1), :].rearrange("p a s -> p (a s)"),
                                 xn[:, u, j]).then_inc(S.stats, 1)

            def body(b, u):
                if not is_last(b, NB):
                    norm_block(b + 1, 1 - u)
                for j in range(2):
                    t = b * 2 + j
                    dve.wait_ge(S.y2_done, t + 1)
                    dve.tensor_copy(token_tile(G.Y2, t), psY[1][j][:, :]).then_inc(S.y2_ready, 1)
            norm_block(0, 0)
            loop(dve, NB, body, peel=1)

        @block.scalar
        def _(act):
            def body(b, u):
                act.wait_ge(S.t_done, done(b))
                act.activation(xnT[:, u], psT[:, :, :], ACT.Copy).then_inc(S.xnT_ready, 1)
                for j in range(2):
                    t = b * 2 + j
                    act.wait_ge(S.y1_done, t + 1)
                    act.activation(token_tile(G.Y1, t), psY[0][j][:, :], ACT.Copy).then_inc(S.y1_ready, 1)
            loop(act, NB, body)

        @block.tensor
        def _(pe):
            pe.wait_ge(S.w_in, 32)
            lead(pe, S.t_done)

            def transposes(b, u):
                pe.wait_ge(S.xn_ready, b * 2 + 2)
                pe.wait_ge(S.xnT_ready, b)
                for c in range(DC):
                    for j in range(2):
                        mm = pe.transpose(psT[:, c, j * P:(j + 1) * P], xn[:, u, j, c * P:(c + 1) * P], G.ident[:, :])
                mm.then_inc(S.t_done, 1)

            def body(b, u):
                pe.wait_ge(S.xnT_ready, b + 1)
                for j in range(2):
                    for k, (free, sem) in enumerate(((S.y1_ready, S.y1_done), (S.y2_ready, S.y2_done))):
                        pe.wait_ge(free, b * 2)
                        for c in range(DC):
                            mm = pe.matmul(psY[k][j][:, :], xnT[:, u, c, j * P:(j + 1) * P], w12[:, k, c],
                                           start=(c == 0), stop=(c == DC - 1))
                        mm.then_inc(sem, 1)
                    if j == 0 and not is_last(b, NB):
                        transposes(b + 1, 1 - u)
            transposes(0, 0)
            loop(pe, NB, body, peel=1)


def neighbour_mean(nc, G):
    with Phase(nc, "nmean") as ph:
        counts = ph.sb("counts", [P, 2, NT, P])
        rdeg = ph.sb("rdeg", [P, 2])
        z = ph.sb("z", [P, 2, D])
        psZ = [ph.ps(f"psZ{i}", [P, D]) for i in range(2)]
        psD = [ph.ps(f"psD{i}", [P, 2]) for i in range(2)]
        names = "counts_ready z_done deg_ready rdeg_ready z_ready x_ready".split()
        S = type("Sems", (), dict(zip(names, ph.sems(*names))))
        block = ph.block()

        @block.vector
        def _(dve):
            def widen(t, u):
                dve.wait_ge(S.z_done, reuse(t))
                for g in range(2):
                    a = G.adj3[:, :, bass.ds(t * 32 + g * 16, 16)]
                    dst = counts[:, u, :, g * GRAPH:(g + 1) * GRAPH].rearrange("p s (q r) -> p s q r", q=4)
                    dve.tensor_copy(dst, a.rearrange("p (s q) r -> p s q r", q=4)).then_inc(S.counts_ready, 1)

            def body(t, u):
                if not is_last(t, NT):
                    widen(t + 1, 1 - u)
                dve.wait_ge(S.z_done, done(t))
                dve.tensor_scalar(rdeg[:, 0:1], psD[u][:, 0:1], 1.0, None, ALU.max).then_inc(S.deg_ready, 1)
                dve.wait_ge(S.deg_ready, t + 1)
                dve.reciprocal(rdeg[:, 1:2], rdeg[:, 0:1]).then_inc(S.rdeg_ready, 1)
                dve.wait_ge(S.rdeg_ready, t + 1)
                dve.scalar_tensor_tensor(out=z[:, u], in0=psZ[u][:, :], scalar=rdeg[:, 1:2], in1=token_tile(G.Y1, t),
                                         op0=ALU.mult, op1=ALU.add).then_inc(S.z_ready, 1)
                dve.wait_ge(S.z_ready, t + 1)
                dve.scalar_tensor_tensor(out=token_tile(G.X, t), in0=z[:, u], scalar=0.0, in1=token_tile(G.X, t),
                                         op0=ALU.max, op1=ALU.add).then_inc(S.x_ready, 1)
            widen(0, 0)
            loop(dve, NT, body, peel=2)

        @block.tensor
        def _(pe):
            lead(pe, S.z_done)

            def body(t, u):
                pe.wait_ge(S.counts_ready, t * 2 + 2)
                for s in range(NT):
                    pe.matmul(psZ[u][:, :], counts[:, u, s], G.Y2[:, s], start=(s == 0), stop=(s == NT - 1))
                    mm = pe.matmul(psD[u][:, :], counts[:, u, s], G.ones[:, 0:2], start=(s == 0), stop=(s == NT - 1))
                mm.then_inc(S.z_done, 1)
            loop(pe, NT, body)


def flow_projections(nc, G, w):
    with Phase(nc, "fproj") as ph:
        wq, wk, wv = (ph.sb(n, [P, DC, D]) for n in ("wq", "wk", "wv"))
        bq, bk, g1, be1 = (ph.sb(n, [P, DC]) for n in ("bq", "bk", "g1", "be1"))
        bv = ph.sb("bv", [P, D])
        ln = ln_stats_buffers(ph)
        xin = ph.sb("xin", [P, 2, 2, D])
        xn = ph.sb("xn", [P, 2, 2, D])
        xnT = ph.sb("xnT", [P, 2, DC, BLK])
        part = ph.sb("part", [P, 2, DC, NB])
        psT = ph.ps("psT", [P, DC, BLK])
        psQ = [ph.ps(f"psQ{i}", [P, DC, BLK]) for i in range(2)]
        psV = [ph.ps(f"psV{i}", [P, D]) for i in range(2)]
        names = ("w_in x_in0 x_in1 xn_ready t_done xnT_ready q_done q_ready v_done v_ready sums_ready").split()
        S = type("Sems", (), dict(zip(names, ph.sems(*names))))
        x_in = (S.x_in0, S.x_in1)
        block = ph.block()

        @block.sync
        def _(sp):
            for dst, name in ((wq, "F_Wq"), (wk, "F_Wk"), (wv, "F_Wv")):
                sp.dma_start(dst[:, :, :], w[name].rearrange("(c p) n -> p c n", p=P)).then_inc(S.w_in, 16)
            for dst, name in ((bq, "F_bq"), (bk, "F_bk"), (g1, "g1"), (be1, "be1")):
                sp.dma_start(dst[:, :], w[name]).then_inc(S.w_in, 16)
            sp.dma_start(bv[:, :], w["F_bv"].partition_broadcast(P)).then_inc(S.w_in, 16)

            def load(b, u):
                sp.wait_ge(S.xn_ready, reuse(b, 2))
                sp.dma_start(xin[:, u].rearrange("p j d -> p (j d)"),
                             G.xn_dram[:, bass.ds(b * 2 * D, 2 * D)]).then_inc(x_in[u], 16)
            loop(sp, NB, load)

        @block.gpsimd
        def _(pool):
            ln_stats_pool(pool, ln, G)

        @block.vector
        def _(dve):
            ln_finish_vector(dve, ln, G.bn, Step(dve, ln.part_done, 0, 99))
            dve.wait_ge(S.w_in, 16 * 8)
            lead(dve, S.xn_ready, 2)

            def norm_block(b, u):
                dve.wait_ge(x_in[u], (b - u) * 8 + 16)
                dve.wait_ge(S.t_done, reuse(b))
                for j in range(2):
                    t = b * 2 + j
                    dve.tensor_scalar(xn[:, u, j], xin[:, u, j], col(ln.rstd, t), col(ln.shift, t),
                                      ALU.mult, ALU.add).then_inc(S.xn_ready, 1)

            def body(b, u):
                if not is_last(b, NB):
                    norm_block(b + 1, 1 - u)
                for j in range(2):
                    t = b * 2 + j
                    dve.wait_ge(S.v_done, t + 1)
                    dve.tensor_tensor(token_tile(G.V, t), psV[j][:, :], bv[:, :], ALU.add).then_inc(S.v_ready, 1)
            norm_block(0, 0)
            loop(dve, NB, body, peel=1)
            dve.wait_ge(S.q_ready, NB * 2 * DC)
            dve.tensor_reduce(G.qksum[:, :, :], part[:, :, :, :], AX.X, ALU.add).then_inc(S.sums_ready, 1)

        @block.scalar
        def _(act):
            act.wait_ge(S.w_in, 16 * 8)

            def body(b, u):
                act.wait_ge(S.t_done, done(b))
                for c in range(DC):
                    act.activation(xnT[:, u, c], psT[:, c], ACT.Identity, bias=be1[:, c:c + 1],
                                   scale=g1[:, c:c + 1]).then_inc(S.xnT_ready, 1)
                for k, (dst, bias) in enumerate(((G.Q, bq), (G.K, bk))):
                    act.wait_ge(S.q_done, b * 2 + k + 1)
                    for c in range(DC):
                        act.activation(dst[:, c, bass.ds(b * BLK, BLK)], psQ[k][:, c], ACT.Sigmoid,
                                       bias=bias[:, c:c + 1], accum_out=part[:, k, c, bass.ds(b, 1)]
                                       ).then_inc(S.q_ready, 1)
            loop(act, NB, body)

        @block.tensor
        def _(pe):
            pe.wait_ge(S.w_in, 16 * 8)
            lead(pe, S.t_done)

            def transposes(b, u):
                pe.wait_ge(S.xn_ready, (b + 1 + LEAD) * 2)
                pe.wait_ge(S.xnT_ready, b * DC)
                for c in range(DC):
                    for j in range(2):
                        mm = pe.transpose(psT[:, c, j * P:(j + 1) * P], xn[:, u, j, c * P:(c + 1) * P], G.ident[:, :])
                mm.then_inc(S.t_done, 1)

            def body(b, u):
                pe.wait_ge(S.xnT_ready, b * DC + DC)
                for k, wt in enumerate((wq, wk)):
                    pe.wait_ge(S.q_ready, b * 2 * DC)
                    for c in range(DC):
                        for d in range(DC):
                            mm = pe.matmul(psQ[k][:, c], wt[:, d, c * P:(c + 1) * P], xnT[:, u, d],
                                           start=(d == 0), stop=(d == DC - 1))
                    mm.then_inc(S.q_done, 1)
                    if k == 0 and not is_last(b, NB):
                        transposes(b + 1, 1 - u)
                for j in range(2):
                    pe.wait_ge(S.v_ready, b * 2 + j)
                    for d in range(DC):
                        mm = pe.matmul(psV[j][:, :], xnT[:, u, d, j * P:(j + 1) * P], wv[:, d], start=(d == 0),
                                       stop=(d == DC - 1))
                    mm.then_inc(S.v_done, 1)
            transposes(0, 0)
            loop(pe, NB, body, peel=1)


def flow_scan(nc, G, w):
    NBIG = N_TOK // D
    NX = NBIG * DC
    with Phase(nc, "fscan") as ph:
        wo = ph.sb("wo", [P, DC, D])
        sums = ph.sb("sums", [P, 4, DC])
        masked = ph.sb("masked", [P, 4, DC, HEADS])
        eps = ph.sb("eps", [P, 2])
        const = ph.sb("const", [HEADS, 4])
        rows = ph.sb("rows", [HEADS, 4, N_TOK])
        part = ph.sb("part", [P, 2, NBIG, DC])
        prod = ph.sb("prod", [P, 2, D])
        junk = ph.sb("junk", [P, D])
        stat = ph.sb("stat", [HEADS, 4])
        ke = ph.sb("ke", [P, DC, D])
        kt = prod
        kv = junk[:, :].rearrange("p (c n) -> p c n", c=PAIRS)
        kvT = ke[:, 0].rearrange("p (c n) -> p c n", c=PAIRS)
        psC = ph.ps("psC", [HEADS, 4, 2])
        psR = [ph.ps(f"psR{i}", [HEADS, D]) for i in range(2)]
        psX = [ph.ps(f"psX{i}", [P, D]) for i in range(2)]
        psT = [ph.ps(f"psT{i}", [P, D]) for i in range(2)]
        psK = ph.ps("psK", [P, PAIRS, P])
        names = ("w_in eps_ready kv_zero sum_step masked_ready c_done c_ready r_done r_ready rec_ready x_done x_used "
                 "summed step sig_ready exp_ready t_done kt_ready kv_done kv_ready kvT_done kvT_ready "
                 "m_done m_ready flow_ready passed passed_dve").split()
        S = type("Sems", (), dict(zip(names, ph.sems(*names))))
        block = ph.block()
        X_of = (G.Q, G.K, G.Q, G.K)

        @block.sync
        def _(sp):
            sp.dma_start(wo[:, :, :], w["F_Wo"].rearrange("(c p) n -> p c n", p=P)).then_inc(S.w_in, 16)

        @block.gpsimd
        def _(pool):
            pool.memset(eps[:, :], FLOW_EPS).then_inc(S.eps_ready, 1)
            pool.wait_ge(S.summed, done(2 * NX - 1))
            pool.memset(junk[:, :], 0.0).then_inc(S.kv_zero, 1)

        @block.tensor
        def _(pe):
            pe.wait_ge(S.eps_ready, 1)
            lead(pe, S.kv_done)

            def head_sums(i):
                pe.wait_ge(S.masked_ready, i + 1)
                pe.wait_ge(S.c_ready, i)
                for c in range(DC):
                    mm = pe.matmul(psC[:, i], masked[:, i, c], eps[:, :], start=(c == 0), stop=(c == DC - 1))
                mm.then_inc(S.c_done, 1)

                def body(n, u):
                    pe.wait_ge(S.r_ready, reuse(n + i * NBIG))
                    for c in range(DC):
                        mm = pe.matmul(psR[u][:, :], masked[:, i, c], X_of[i][:, c, bass.ds(n * D, D)],
                                       start=(c == 0), stop=(c == DC - 1))
                    mm.then_inc(S.r_done, 1)
                loop(pe, NBIG, body)

            def spread(k, row, n):
                for c in range(DC):
                    gate(pe, S.x_used, reuse(n * DC + c + k * NX), S.passed)
                    pe.matmul(psX[c % 2][:, :], G.rep[:, c], rows[:, row, bass.ds(n * D, D)], start=True,
                              stop=True).then_inc(S.x_done, 1)
            head_sums(0)
            head_sums(1)
            for row in range(2):
                pe.wait_ge(S.rec_ready, (row + 1) * NBIG)
                loop(pe, NBIG, lambda n, u: spread(row, row, n))
            head_sums(2)
            head_sums(3)
            pe.wait_ge(S.step, STEPS)

            def context(n, u):
                spread(2, 3, n)
                pe.wait_ge(S.x_used, done(n * DC + DC - 1 + 2 * NX))
                for j in range(5):
                    t = n * 4 + j
                    if j < 4:
                        pe.wait_ge(S.kt_ready, reuse(t))
                        for c in range(DC):
                            mm = pe.transpose(psT[j % 2][:, c * P:(c + 1) * P], ke[:, c, j * P:(j + 1) * P],
                                              G.ident[:, :])
                        mm.then_inc(S.t_done, 1)
                    if j:
                        pe.wait_ge(S.kt_ready, done(t - 1))
                        for c in range(PAIRS):
                            mm = pe.matmul(psK[:, c], kt[:, (j - 1) % 2, c * P:(c + 1) * P],
                                           G.V[:, bass.ds(t - 1, 1), c * P:(c + 1) * P].rearrange("p a m -> p (a m)"),
                                           start=(isinstance(t, int) and t == 1 and c == 0),
                                           stop=is_last(t - 1, NT), skip_group_check=True)
                        mm.then_inc(S.kv_done, 1)
            for n in range(NBIG):
                context(n, n % 2)
            pe.wait_ge(S.kv_ready, 2)
            for c in range(PAIRS):
                mm = pe.transpose(psT[0][:, c * P:(c + 1) * P], kv[:, c], G.ident[:, :])
            mm.then_inc(S.kvT_done, 1)
            pe.wait_ge(S.kvT_ready, 1)
            pe.wait_ge(S.w_in, 16)
            for c in range(PAIRS):
                if c >= 2:
                    pe.wait_ge(S.m_ready, c - 1)
                pe.matmul(psX[c % 2][:, :], kvT[:, c], wo[:, c], start=True, stop=True).then_inc(S.m_done, 1)

        @block.vector
        def _(dve):
            lead(dve, S.r_ready)
            lead(dve, S.x_used)
            ss = Step(dve, S.sum_step, 0, 8)
            ss.did(dve.tensor_scalar(sums[:, 0], G.qksum[:, 1], FLOW_EPS, None, ALU.add))
            ss.do(dve.tensor_scalar(sums[:, 1], G.qksum[:, 0], FLOW_EPS, None, ALU.add))

            def mask(i):
                dve.tensor_tensor(masked[:, i], G.sel[:, :, :], sums[:, i].unsqueeze(2).to_broadcast([P, DC, HEADS]),
                                  ALU.mult).then_inc(S.masked_ready, 1)

            def take(i, invert):
                dve.wait_ge(S.c_done, i + 1)
                dve.tensor_copy(const[:, i:i + 1], psC[:, i, 0:1]).then_inc(S.c_ready, 1)
                dve.wait_ge(S.c_ready, i + 1)

                def body(n, u):
                    m = n + i * NBIG
                    r = rows[:, i, bass.ds(n * D, D)]
                    dve.wait_ge(S.r_done, m + 1)
                    dve.tensor_scalar(r, psR[u][:, :], const[:, i:i + 1], None, ALU.add).then_inc(S.r_ready, 1)
                    if invert:
                        gate(dve, S.r_ready, done(m), S.passed_dve)
                        dve.reciprocal(r, r).then_inc(S.rec_ready, 1)
                loop(dve, NBIG, body)

            def weigh(row, X):
                def body(n, u):
                    for c in range(DC):
                        m = n * DC + c + row * NX
                        dve.wait_ge(S.x_done, m + 1)
                        dve.wait_ge(S.summed, reuse(m))
                        dve.tensor_tensor(prod[:, c % 2], X[:, c, bass.ds(n * D, D)], psX[c % 2][:, :],
                                          ALU.mult).then_inc(S.x_used, 1)
                loop(dve, NBIG, body)
            mask(0)
            mask(1)
            take(0, True)
            take(1, True)
            weigh(0, G.Q)
            weigh(1, G.K)
            dve.wait_ge(S.summed, done(2 * NX - 1))
            for i, k in ((2, 1), (3, 0)):
                ss.do(dve.tensor_reduce(sums[:, i], part[:, k].rearrange("p n c -> p c n"), AX.X, ALU.add))
                ss.do(dve.tensor_scalar(sums[:, i], sums[:, i], FLOW_EPS, None, ALU.add))
                mask(i)
            take(2, False)
            take(3, False)
            st = Step(dve, S.step, 0, STEPS)
            dve.wait_ge(S.r_ready, done(4 * NBIG - 1))
            st.do(dve.tensor_scalar(rows[:, 3], rows[:, 3], -1.0, 1.0, ALU.max, ALU.min))
            st.do(dve.tensor_reduce(stat[:, 0:1], rows[:, 3], AX.X, ALU.max))
            st.do(dve.tensor_scalar(stat[:, 1:2], stat[:, 0:1], -1.0, None, ALU.mult))
            dve.wait_ge(S.exp_ready, 1)
            st.do(dve.reciprocal(stat[:, 3:4], stat[:, 2:3]))
            st.do(dve.tensor_scalar(rows[:, 3], rows[:, 3], stat[:, 3:4], float(N_TOK), ALU.mult, ALU.mult))
            dve.wait_ge(S.sig_ready, 1)
            dve.tensor_tensor(G.flow[:, :], rows[:, 0], rows[:, 2], ALU.mult).then_inc(S.flow_ready, 1)

            def compete(n, u):
                for c in range(DC):
                    m = n * DC + c + 2 * NX
                    dve.wait_ge(S.x_done, m + 1)
                    if c == 0:
                        dve.wait_ge(S.t_done, n * 4)
                    dve.tensor_tensor(ke[:, c], G.K[:, c, bass.ds(n * D, D)], psX[c % 2][:, :], ALU.mult)\
                        .then_inc(S.x_used, 1)
            loop(dve, NBIG, compete)
            dve.wait_ge(S.kv_done, done(NT - 1))
            dve.wait_ge(S.kv_zero, 1)
            for h in (slice(0, DH), slice(DH, P)):
                dve.tensor_copy(kv[h, :, h], psK[h, :, h]).then_inc(S.kv_ready, 1)

        @block.scalar
        def _(act):
            lead(act, S.summed)
            lead(act, S.kt_ready)
            for k in range(2):
                def body(n, u):
                    for c in range(DC):
                        m = n * DC + c + k * NX
                        act.wait_ge(S.x_used, done(m))
                        act.wait_ge(S.summed, m + LEAD)
                        act.activation(junk[:, :], prod[:, c % 2], ACT.Copy,
                                       accum_out=part[:, k, bass.ds(n, 1), c]).then_inc(S.summed, 1)
                loop(act, NBIG, body)
            act.wait_ge(S.r_ready, done(3 * NBIG - 1))
            act.activation(rows[:, 2], rows[:, 2], ACT.Sigmoid).then_inc(S.sig_ready, 1)
            act.wait_ge(S.step, 3)
            act.activation(rows[:, 3], rows[:, 3], ACT.Exp, bias=stat[:, 1:2],
                           accum_out=stat[:, 2:3]).then_inc(S.exp_ready, 1)

            def turn(n, u):
                for j in range(4):
                    t = n * 4 + j
                    act.wait_ge(S.t_done, t + 1)
                    act.wait_ge(S.kv_done, reuse(t))
                    act.activation(kt[:, j % 2], psT[j % 2][:, :], ACT.Copy).then_inc(S.kt_ready, 1)
            loop(act, NBIG, turn)
            act.wait_ge(S.kvT_done, 1)
            act.activation(ke[:, 0], psT[0][:, :], ACT.Copy).then_inc(S.kvT_ready, 1)
            for c in range(PAIRS):
                act.wait_ge(S.m_done, c + 1)
                act.activation(G.M[:, c], psX[c % 2][:, :], ACT.Copy).then_inc(S.m_ready, 1)


STEPS = 5


def flow_output(nc, G, w):
    FM = 2
    with Phase(nc, "fout") as ph:
        w1 = ph.sb("w1", [P, DC, FM * P])
        w2 = ph.sb("w2", [P, FM, D])
        b1 = ph.sb("b1", [P, FM])
        g2, be2 = (ph.sb(n, [P, DC]) for n in ("g2", "be2"))
        bo, b2 = (ph.sb(n, [P, D]) for n in ("bo", "b2"))
        qf = ph.sb("qf", [P, 2, DC, BLK])
        xin = ph.sb("xin", [P, 2, 2, D])
        x1 = ph.sb("x1", [P, 2, 2, D])
        bn = ph.sb("bn", [P, 2, 6])
        mv = ph.sb("mv", [P, 2, 2])
        rstd = ph.sb("rstd", [P, 2])
        hn = ph.sb("hn", [P, 2, 2, D])
        hT = ph.sb("hT", [P, DC, BLK])
        hid = ph.sb("hid", [P, 2, FM, BLK])
        psX = ph.ps("psX", [P, DC, BLK])
        psO = [ph.ps(f"psO{i}", [P, D]) for i in range(2)]
        psT = ph.ps("psT", [P, DC, BLK])
        psH = ph.ps("psH", [P, FM, BLK])
        psY = ph.ps("psY", [P, D])
        names = ("w_in x_in0 x_in1 x_done qf_ready o_done xo_ready x1_ready bn_ready mv_ready rstd_ready hn_ready t_done "
                 "hT_ready hid_done hid_ready y_done y1_ready y2_ready xr_ready passed passed_pe passed_pool").split()
        S = type("Sems", (), dict(zip(names, ph.sems(*names))))
        x_in = (S.x_in0, S.x_in1)
        block = ph.block()

        @block.sync
        def _(sp):
            sp.dma_start(w1[:, :, :], w["F_W1"].rearrange("(c p) n -> p c n", p=P)).then_inc(S.w_in, 16)
            sp.dma_start(w2[:, :, :], w["F_W2"].rearrange("(c p) n -> p c n", p=P)).then_inc(S.w_in, 16)
            for dst, name in ((b1, "F_b1"), (g2, "g2"), (be2, "be2")):
                sp.dma_start(dst[:, :], w[name]).then_inc(S.w_in, 16)
            for dst, name in ((bo, "F_bo"), (b2, "F_b2")):
                sp.dma_start(dst[:, :], w[name].partition_broadcast(P)).then_inc(S.w_in, 16)

            def load(b, u):
                sp.wait_ge(S.xo_ready, reuse(b, 2))
                sp.dma_start(xin[:, u].rearrange("p j d -> p (j d)"),
                             G.xn_dram[:, bass.ds(b * 2 * D, 2 * D)]).then_inc(x_in[u], 16)
            loop(sp, NB, load)

        @block.gpsimd
        def _(pool):
            def power(t, u):
                gate(pool, S.mv_ready, t + 1, S.passed_pool)
                pool.tensor_tensor(rstd[:, u:u + 1], mv[:, u, 1:2], G.minus_half[:, 0:1],
                                   ALU.pow).then_inc(S.rstd_ready, 1)
            loop(pool, NT, power)

        @block.vector
        def _(dve):
            dve.wait_ge(S.w_in, 16 * 7)
            lead(dve, S.xo_ready, 2)
            lead(dve, S.xr_ready, 2)

            def first(b, u):
                dve.wait_ge(S.x_done, b + 1)
                dve.wait_ge(S.o_done, reuse(b, 2))
                dve.tensor_tensor(qf[:, u], G.Q[:, :, bass.ds(b * BLK, BLK)], psX[:, :, :],
                                  ALU.mult).then_inc(S.qf_ready, 1)
                dve.wait_ge(x_in[u], (b - u) * 8 + 16)
                dve.wait_ge(S.xr_ready, reuse(b, 2))
                for j in range(2):
                    t = b * 2 + j
                    x = x1[:, u, j]
                    dve.wait_ge(S.o_done, t + 1 + 2 * LEAD)
                    dve.tensor_tensor(x, xin[:, u, j], psO[j][:, :], ALU.add).then_inc(S.xo_ready, 1)
                    dve.wait_ge(S.xo_ready, t + 1 + 2 * LEAD)
                    dve.tensor_tensor(x, x, bo[:, :], ALU.add).then_inc(S.x1_ready, 1)
                    dve.wait_ge(S.x1_ready, t + 1)
                    dve.bn_stats(bn[:, j], x).then_inc(S.bn_ready, 1)
                    gate(dve, S.bn_ready, t + 1, S.passed)
                    dve.bn_aggr(mv[:, j], bn[:, j]).then_inc(S.passed, 1)
                    dve.wait_ge(S.passed, t * 2 + 2)
                    dve.tensor_scalar(mv[:, j, 1:2], mv[:, j, 1:2], LN_EPS, None, ALU.add).then_inc(S.mv_ready, 1)
                for j in range(2):
                    t = b * 2 + j
                    dve.wait_ge(S.rstd_ready, t + 1)
                    dve.tensor_scalar(hn[:, u, j], x1[:, u, j], mv[:, j, 0:1], rstd[:, j:j + 1], ALU.subtract,
                                      ALU.mult).then_inc(S.hn_ready, 1)

            def second(b, u):
                for j in range(2):
                    t = b * 2 + j
                    x = x1[:, u, j]
                    dve.tensor_tensor(x, x, b2[:, :], ALU.add).then_inc(S.y1_ready, 1)
                    dve.wait_ge(S.y_done, t + 1)
                    dve.wait_ge(S.y1_ready, t + 1)
                    dve.tensor_tensor(x, x, psY[:, :], ALU.add).then_inc(S.y2_ready, 1)
                    dve.wait_ge(S.y2_ready, t + 1)
                    dve.tensor_tensor(token_tile(G.X, t), token_tile(G.X, t), x, ALU.add).then_inc(S.xr_ready, 1)

            def body(b, u):
                if not is_last(b, NB):
                    first(b + 1, 1 - u)
                second(b, u)
            first(0, 0)
            loop(dve, NB, body, peel=1)

        @block.scalar
        def _(act):
            act.wait_ge(S.w_in, 16 * 7)

            def body(b, u):
                act.wait_ge(S.t_done, done(b))
                act.wait_ge(S.hid_done, b)
                for c in range(DC):
                    act.activation(hT[:, c], psT[:, c], ACT.Identity, bias=be2[:, c:c + 1],
                                   scale=g2[:, c:c + 1]).then_inc(S.hT_ready, 1)
                act.wait_ge(S.hid_done, b + 1)
                for f in range(FM):
                    act.activation(hid[:, u, f], psH[:, f], ACT.Gelu, bias=b1[:, f:f + 1]).then_inc(S.hid_ready, 1)
            loop(act, NB, body)

        @block.tensor
        def _(pe):
            pe.wait_ge(S.w_in, 16 * 7)
            lead(pe, S.o_done, 2)
            lead(pe, S.t_done)

            def first(b, u):
                gate(pe, S.qf_ready, b, S.passed_pe)
                for c in range(DC):
                    mm = pe.matmul(psX[:, c], G.rep[:, c], G.flow[:, bass.ds(b * BLK, BLK)], start=True, stop=True)
                mm.then_inc(S.x_done, 1)
                pe.wait_ge(S.qf_ready, b + 1)
                for j in range(2):
                    pe.wait_ge(S.xo_ready, b * 2 + j - 1 + 2 * LEAD)
                    for c in range(DC):
                        mm = pe.matmul(psO[j][:, :], qf[:, u, c, j * P:(j + 1) * P], G.M[:, c], start=(c == 0),
                                       stop=(c == DC - 1))
                    mm.then_inc(S.o_done, 1)

            def second(b, u):
                pe.wait_ge(S.hn_ready, b * 2 + 2)
                pe.wait_ge(S.hT_ready, b * DC)
                for c in range(DC):
                    for j in range(2):
                        mm = pe.transpose(psT[:, c, j * P:(j + 1) * P], hn[:, u, j, c * P:(c + 1) * P], G.ident[:, :])
                mm.then_inc(S.t_done, 1)
                pe.wait_ge(S.hT_ready, b * DC + DC)
                pe.wait_ge(S.hid_ready, b * FM)
                for f in range(FM):
                    for c in range(DC):
                        mm = pe.matmul(psH[:, f], w1[:, c, f * P:(f + 1) * P], hT[:, c], start=(c == 0),
                                       stop=(c == DC - 1))
                mm.then_inc(S.hid_done, 1)
                pe.wait_ge(S.hid_ready, b * FM + FM)
                for j in range(2):
                    pe.wait_ge(S.y2_ready, b * 2 + j)
                    for f in range(FM):
                        mm = pe.matmul(psY[:, :], hid[:, u, f, j * P:(j + 1) * P], w2[:, f], start=(f == 0),
                                       stop=(f == FM - 1))
                    mm.then_inc(S.y_done, 1)

            def body(b, u):
                if not is_last(b, NB):
                    first(b + 1, 1 - u)
                second(b, u)
            first(0, 0)
            loop(pe, NB, body, peel=1)


def clear_slots(nc, G):
    with Phase(nc, "clear") as ph:
        zero = ph.sb("zero", [P, 2 * D])
        made, cleared = ph.sems("made", "cleared")
        block = ph.block()

        @block.gpsimd
        def _(pool):
            pool.memset(zero[:, :], 0.0).then_inc(made, 1)

        @block.sync
        def _(sp):
            sp.wait_ge(made, 1)
            for g in range(NST):
                sp.dma_start(G.xs_dram.rearrange("(n p j) d -> p n (j d)", p=P, j=2)[:, g, :],
                             zero[:, :]).then_inc(cleared, 16)
            sp.wait_ge(cleared, 16 * NST)


def program(nc, w, out, phases=(0, 1, 2, 3, 4)):
    G = type("Shared", (), {})()

    def scratch(name, shape, dt=F32):
        return nc.dram_tensor(name, shape, dt, kind="Internal").ap()

    with ExitStack() as ctx:
        def sb(name, shape, dt=F32):
            return ctx.enter_context(nc.sbuf_tensor(name, shape, dt))

        G.X = sb("X", [P, NT, D])
        G.ident = sb("ident", [P, P])
        G.upper = sb("upper", [P, P])
        G.ones = sb("ones", [P, P])
        G.headmask = sb("headmask", [P, P])
        G.iota512 = sb("iota512", [P, ACOLS])
        G.iota16x8 = sb("iota16x8", [P, 16, HEADS])
        G.part = sb("part", [P, 1])
        G.minus_half = sb("minus_half", [P, NT])
        G.edge_bucket = sb("edge_bucket", [P, NG], I32)
        G.bn = sb("bn", [P, NT, 6])
        G.place = sb("place", [P, TOPK * NT], I32)
        G.wrow = sb("wrow", [P, NST], I32)
        G.gate = sb("gate", [P, NT, TOPK])
        G.comb = sb("comb", [P, NT, EXPERTS])
        G.rec_dram = scratch("rec_dram", [P * NCH, REC])
        G.adj_dram = scratch("adj_dram", [P, BUCKETS * ACOLS], U16)
        G.xnT_dram = scratch("xnT_dram", [P, NB * DC * BLK])
        G.xn_dram = scratch("xn_dram", [P, NT * D])
        G.xs_dram = scratch("xs_dram", [SLOTS, D])
        G.ys_dram = scratch("ys_dram", [SLOTS, D])
        constants(nc, G, w["x"])
        with ExitStack() as layer:
            if 0 in phases:
                sort_edges(nc, G, w)
                G.BIAS = layer.enter_context(nc.sbuf_tensor("BIAS", [P, BUCKETS * BCOLS], F32))
                build_graph(nc, G)
            if 1 in phases:
                G.M = layer.enter_context(nc.sbuf_tensor("M0", [P, PAIRS, D], F32))
                G.Q = layer.enter_context(nc.sbuf_tensor("Q0", [P, DC, N_TOK], F32))
                linear_attention_scan(nc, G, w)
                graph_attention(nc, G, w)
        if 2 in phases:
            clear_slots(nc, G)
            route(nc, G, w, "A_", False)
            experts(nc, G, w, "A_", 1024)
            combine(nc, G, w, "A_", None)
        if 3 in phases:
            with nc.sbuf_tensor("Y1", [P, NT, D], F32) as G.Y1, nc.sbuf_tensor("Y2", [P, NT, D], F32) as G.Y2, \
                    nc.sbuf_tensor("adj", [P, BUCKETS * ACOLS], U16) as G.adj:
                G.adj3 = G.adj[:, :].rearrange("p (b n) -> p b n", n=ACOLS)
                neighbour_products(nc, G, w)
                neighbour_mean(nc, G)
            with nc.sbuf_tensor("M1", [P, PAIRS, D], F32) as G.M, nc.sbuf_tensor("Q1", [P, DC, N_TOK], F32) as G.Q, \
                    nc.sbuf_tensor("flow", [HEADS, N_TOK], F32) as G.flow, \
                    nc.sbuf_tensor("sel", [P, DC, HEADS], F32) as G.sel, \
                    nc.sbuf_tensor("rep", [HEADS, DC, P], F32) as G.rep:
                head_rows(nc, G)
                with nc.sbuf_tensor("K", [P, DC, N_TOK], F32) as G.K, nc.sbuf_tensor("V", [P, NT, D], F32) as G.V, \
                        nc.sbuf_tensor("qksum", [P, 2, DC], F32) as G.qksum:
                    flow_projections(nc, G, w)
                    flow_scan(nc, G, w)
                flow_output(nc, G, w)
        if 4 in phases:
            route(nc, G, w, "B_", True)
            experts(nc, G, w, "B_", 256)
            combine(nc, G, w, "B_", out)



def layouts(inputs):
    import numpy as np

    def chunks(b):
        return b.reshape(-1, P).T

    a = {k: np.asarray(v) for k, v in inputs.items()}
    wqkv = a["L0_mix_w_qkv"]
    out = {"x": a["x"], "src": a["src"], "dst": a["dst"], "edge_attr": a["edge_attr_16"],
           "We": a["L0_gnn_We"], "be": a["L0_gnn_be"],
           "mix_wq": wqkv[:D].T, "mix_wk": wqkv[D:2 * D].T, "mix_wv": wqkv[2 * D:].T,
           "mix_wo": a["L0_mix_w_out"].T, "b_out": a["L0_mix_b_out"],
           "bq": chunks(a["L0_gnn_bq"]), "bk": chunks(a["L0_gnn_bk"]), "gw": a["L1_gnn_w"].T}
    for n in ("Wq", "Wk", "Wv", "Wo", "bv", "bo"):
        out[n] = a["L0_gnn_" + n]
    for n in ("Wq", "Wk", "Wv", "Wo", "W1", "W2", "bv", "bo", "b2"):
        out["F_" + n] = a["L1_mix_" + n]
    for n in ("bq", "bk", "b1"):
        out["F_" + n] = chunks(a["L1_mix_" + n])
    for n in ("g1", "be1", "g2", "be2"):
        out[n] = chunks(a["L1_mix_" + n])

    def moe(pre, w1, b1, w2, b2, wr, br):
        E, _, F = w1.shape
        out[pre + "W1"] = w1.reshape(E, DC, P, F).transpose(0, 2, 1, 3).reshape(E * P, DC * F)
        out[pre + "W2"] = w2.reshape(E, F // P, P, D).transpose(0, 2, 1, 3).reshape(E * P, F // P * D)
        out[pre + "b1"] = b1.reshape(E, F // P, P).transpose(0, 2, 1).reshape(E * P, F // P)
        out[pre + "b2"], out[pre + "Wr"], out[pre + "br"] = b2, wr.T, br

    moe("A_", *(a["L0_ffn_" + n] for n in ("W1", "b1", "W2", "b2", "Wr", "br")))
    moe("B_", a["L1_ffn_rw1"].transpose(0, 2, 1), a["L1_ffn_rb1"], a["L1_ffn_rw2"].transpose(0, 2, 1),
        a["L1_ffn_rb2"], a["L1_ffn_gate_w"], a["L1_ffn_gate_b"])
    out["sw1"] = a["L1_ffn_sw1"].transpose(2, 0, 1).reshape(D, -1)
    out["sw2"] = a["L1_ffn_sw2"].transpose(0, 2, 1).reshape(-1, D)
    out["sb1"], out["sb2"] = chunks(a["L1_ffn_sb1"].reshape(-1)), a["L1_ffn_sb2"]
    return {k: np.ascontiguousarray(v) for k, v in out.items()}


def kernel(**inputs):
    import concourse.bacc as _bacc
    from concourse.bass_utils import run_bass_kernel_spmd as _run

    nc = _bacc.Bacc("TRN2", target_bir_lowering=False, num_devices=1)
    arrays = layouts(inputs)
    w = {k: nc.dram_tensor("in_" + k, v.shape, mybir.dt.from_np(v.dtype), kind="ExternalInput").ap()
         for k, v in arrays.items()}
    out = nc.dram_tensor("out", (N_TOK, D), F32, kind="ExternalOutput").ap()
    program(nc, w, out)
    r = _run(nc, [{"in_" + k: v for k, v in arrays.items()}], core_ids=[0])
    return r.results[0]["out"]
```

```python
from contextlib import ExitStack

import concourse.bass as bass
from concourse import mybir

F32 = mybir.dt.float32
F32R = mybir.dt.float32r
BF16 = mybir.dt.bfloat16
F16 = mybir.dt.float16
I32 = mybir.dt.int32
U32 = mybir.dt.uint32
U16 = mybir.dt.uint16
ALU = mybir.AluOpType
ACT = mybir.ActivationFunctionType
AX = mybir.AxisListType

P = 128
N_TOK = 2048
D = 512
DC = D // P
NT = N_TOK // P
BLK = 256
NB = N_TOK // BLK
HEADS = 8
DH = D // HEADS
PAIRS = HEADS // 2
GRAPH = 64
E_EDGES = 32768
EJ = E_EDGES // P
ED = 16
LN_EPS = 1e-5
FLOW_EPS = 1e-6

BUCKETS = NT * 4
GROUP = 256
NG = 192
NCH = 2 * NG
REC = 12
ACOLS = (N_TOK // GRAPH) * 16
BCOLS = 16 * HEADS

EXPERTS = 8
TOPK = 2
SLOT_TILE = 256
NST = (N_TOK * TOPK) // SLOT_TILE + EXPERTS - 1
SLOTS = NST * SLOT_TILE


class Step:

    def __init__(self, eng, sem, t, k):
        self.eng, self.sem, self.base, self.k, self.n = eng, sem, t * k, k, 0

    def did(self, ins):
        ins.then_inc(self.sem, 1)
        self.n += 1
        assert self.n <= self.k

    def wait(self):
        self.eng.wait_ge(self.sem, self.base + self.n)

    def do(self, ins):
        self.did(ins)
        self.wait()


def loop(eng, n, body, unroll=2, peel=0, head=0, done_steps=0):
    full = (n - peel) // unroll
    for t in range(done_steps, head):
        body(t, t % unroll)
    with eng.Fori(head // unroll, full) as i:
        for u in range(unroll):
            body(i * unroll + u, u)
    for t in range(full * unroll, n):
        body(t, t % unroll)


LEAD = 1


def lead(eng, sem, k=1):
    eng.sem_inc(sem, LEAD * k)


def done(t, k=1):
    return (t + 1 + LEAD) * k


def reuse(t, k=1):
    return (t - 1 + LEAD) * k


def gate(eng, sem, value, passed):
    eng.wait_ge(sem, value)
    eng.sem_inc(passed, 1)


def is_last(t, n):
    return isinstance(t, int) and t == n - 1


class Phase:

    def __init__(self, nc, name):
        self.nc, self.name, self.ctx = nc, name, ExitStack()
        self.used = []

    def __enter__(self):
        self.ctx.__enter__()
        return self

    def __exit__(self, *a):
        self.ctx.__exit__(*a)
        if a[0] is None:
            self.nc.clear_and_free_semaphores(self.used)
            self.nc.all_engine_barrier()

    def sb(self, name, shape, dt=F32):
        return self.ctx.enter_context(self.nc.sbuf_tensor(f"{self.name}_{name}", shape, dt))

    def ps(self, name, shape, dt=F32):
        return self.ctx.enter_context(self.nc.psum_tensor(f"{self.name}_{name}", shape, dt))

    def sem(self, name):
        self.used.append(self.nc.alloc_semaphore(name=f"{self.name}_{name}"))
        return self.used[-1]

    def sems(self, *names):
        return [self.sem(n) for n in names]

    def block(self):
        return self.ctx.enter_context(self.nc.Block())


def constants(nc, G, x):
    with Phase(nc, "const") as ph:
        raw, made, mask_zero, stats = ph.sems("raw", "made", "mask_zero", "stats")
        x_in = ph.sems(*(f"x_in{i}" for i in range(NT // 4)))
        block = ph.block()

        @block.sync
        def _(sp):
            for t in range(0, NT, 4):
                sp.dma_start(G.X[:, t:t + 4, :], x.rearrange("(t p) d -> p t d", p=P)[:, t:t + 4, :]
                             ).then_inc(x_in[t // 4], 16)

        @block.vector
        def _(dve):
            dve.memset(G.headmask[:, :], 0.0).then_inc(mask_zero, 1)
            dve.wait_ge(mask_zero, 1)
            dve.memset(G.headmask[0:DH, 0:DH], 1.0)
            dve.memset(G.headmask[DH:P, DH:P], 1.0)
            for t in range(NT):
                if t % 4 == 0:
                    dve.wait_ge(x_in[t // 4], 16)
                tile_stats(dve, G, t).then_inc(stats, 1)
            dve.wait_ge(stats, NT)

        @block.gpsimd
        def _(pool):
            pool.memset(G.ident[:, :], 0.0).then_inc(raw, 1)
            pool.memset(G.upper[:, :], 1.0).then_inc(raw, 1)
            pool.memset(G.ones[:, :], 1.0).then_inc(raw, 1)
            pool.memset(G.minus_half[:, :], -0.5).then_inc(raw, 1)
            pool.wait_ge(raw, 4)
            pool.affine_select(out=G.ident[:, :], in_=G.ident[:, :], compare_op=ALU.not_equal, fill=1.0, base=0,
                               pattern=[[-1, P]], channel_multiplier=1).then_inc(made, 1)
            pool.affine_select(out=G.upper[:, :], in_=G.upper[:, :], compare_op=ALU.is_gt, fill=0.0, base=0,
                               pattern=[[1, P]], channel_multiplier=-1).then_inc(made, 1)
            pool.iota(G.iota512[:, :], pattern=[[1, ACOLS]], base=0, channel_multiplier=0,
                      allow_small_or_imprecise_dtypes=True).then_inc(made, 1)
            pool.iota(G.iota16x8[:, :, :], pattern=[[1, 16], [0, HEADS]], base=0, channel_multiplier=0,
                      allow_small_or_imprecise_dtypes=True).then_inc(made, 1)
            pool.iota(G.part[:, :], pattern=[[0, 1]], base=0, channel_multiplier=1,
                      allow_small_or_imprecise_dtypes=True).then_inc(made, 1)
            pool.wait_ge(made, 5)


def head_rows(nc, G):
    with Phase(nc, "heads") as ph:
        sel_zero, sel_ready, rep_done, rep_ready = ph.sems("sel_zero", "sel_ready", "rep_done", "rep_ready")
        psR = ph.ps("psR", [HEADS, DC, P])
        block = ph.block()

        @block.vector
        def _(dve):
            dve.memset(G.sel[:, :, :], 0.0).then_inc(sel_zero, 1)
            dve.wait_ge(sel_zero, 1)
            for h in range(HEADS):
                dve.memset(G.sel[DH * (h % 2):DH * (h % 2 + 1), h // 2, h:h + 1], 1.0).then_inc(sel_ready, 1)
            dve.wait_ge(rep_done, 1)
            dve.tensor_copy(G.rep[:, :, :], psR[:, :, :]).then_inc(rep_ready, 1)

        @block.tensor
        def _(pe):
            pe.wait_ge(sel_ready, HEADS)
            for c in range(DC):
                mm = pe.transpose(psR[:, c], G.sel[:, c], G.ident[:, :])
            mm.then_inc(rep_done, 1)


def ln_stats_buffers(ph):
    s = type("LnStats", (), {})()
    s.mean = ph.sb("ln_mean", [P, NT])
    s.diff = ph.sb("ln_diff", [P, NT])
    s.m2 = ph.sb("ln_m2", [P, NT])
    s.var = ph.sb("ln_var", [P, NT])
    s.rstd = ph.sb("ln_rstd", [P, NT])
    s.shift = ph.sb("ln_shift", [P, NT])
    s.part_done, s.var_ready, s.rstd_ready, s.ready = ph.sems("ln_part", "ln_var", "ln_rstd", "ln_ready")
    return s


def tile_stats(dve, G, t):
    return dve.bn_stats(G.bn[:, bass.ds(t, 1), :].rearrange("p a s -> p (a s)"), token_tile(G.X, t))


def ln_stats_vector(dve, s, bn):
    st = Step(dve, s.part_done, 0, 8)
    st.did(dve.tensor_tensor(s.mean[:, :], bn[:, :, 1], bn[:, :, 4], ALU.add))
    st.did(dve.tensor_tensor(s.diff[:, :], bn[:, :, 1], bn[:, :, 4], ALU.subtract))
    st.did(dve.tensor_tensor(s.m2[:, :], bn[:, :, 2], bn[:, :, 5], ALU.add))
    st.wait()
    st.did(dve.tensor_scalar(s.mean[:, :], s.mean[:, :], 0.5, None, ALU.mult))
    st.did(dve.tensor_tensor(s.diff[:, :], s.diff[:, :], s.diff[:, :], ALU.mult))
    st.did(dve.tensor_scalar(s.m2[:, :], s.m2[:, :], 1.0 / D, LN_EPS, ALU.mult, ALU.add))
    st.wait()
    dve.scalar_tensor_tensor(out=s.var[:, :], in0=s.diff[:, :], scalar=0.25, in1=s.m2[:, :],
                             op0=ALU.mult, op1=ALU.add).then_inc(s.var_ready, 1)
    dve.wait_ge(s.rstd_ready, 1)
    dve.scalar_tensor_tensor(out=s.shift[:, :], in0=s.mean[:, :], scalar=-1.0, in1=s.rstd[:, :],
                             op0=ALU.mult, op1=ALU.mult).then_inc(s.ready, 1)
    dve.wait_ge(s.ready, 1)


def ln_stats_pool(pool, s, G):
    pool.wait_ge(s.var_ready, 1)
    pool.tensor_tensor(s.rstd[:, :], s.var[:, :], G.minus_half[:, :], ALU.pow).then_inc(s.rstd_ready, 1)


def token_tile(X, t):
    return X[:, bass.ds(t, 1), :].rearrange("p a d -> p (a d)")


def col(ap2d, t):
    return ap2d[:, bass.ds(t, 1)]


def bucket_starts(ph, nb, group, n_groups, past):
    s = type("Buckets", (), {})()
    s.nb, s.group, s.n_groups = nb, group, n_groups
    s.count = ph.sb("count", [P, nb])
    s.before = ph.sb("before", [P, nb])
    s.total = ph.sb("total", [P, nb], I32)
    s.padded = ph.sb("padded", [P, nb])
    s.end = ph.sb("end", [P, nb])
    s.first = ph.sb("first", [P, nb])
    s.group_at = ph.sb("group_at", [P, n_groups])
    s.past = past
    s.bucket = ph.sb("bucket", [P, n_groups])
    s.ps = ph.ps("ps_count", [P, 2, nb])
    s.counted, s.summed, s.step, s.numbered = ph.sems("counted", "summed", "bucket_step", "numbered")
    return s


def bucket_starts_pool(pool, s):
    pool.iota(s.group_at[:, :], pattern=[[s.group, s.n_groups]], base=0, channel_multiplier=0,
              allow_small_or_imprecise_dtypes=True).then_inc(s.numbered, 1)


def bucket_starts_tensor(pe, s, G, n_counts):
    pe.wait_ge(s.counted, n_counts)
    pe.matmul(s.ps[:, 0], G.upper[:, :], s.count[:, :], start=True, stop=True)
    pe.matmul(s.ps[:, 1], G.ones[:, :], s.count[:, :], start=True, stop=True).then_inc(s.summed, 1)


def bucket_starts_vector(dve, s):
    st = Step(dve, s.step, 0, 16)
    shift = s.group.bit_length() - 1
    dve.wait_ge(s.summed, 1)
    st.did(dve.tensor_scalar(s.total[:, :], s.ps[:, 1], float(s.group - 1), None, ALU.add))
    st.do(dve.tensor_copy(s.before[:, :], s.ps[:, 0]))
    st.do(dve.tensor_scalar(s.total[:, :], s.total[:, :], shift, shift, ALU.logical_shift_right,
                            ALU.logical_shift_left))
    st.do(dve.tensor_copy(s.padded[:, :], s.total[:, :]))
    st.do(dve.tensor_tensor_scan(s.end[:, :], s.padded[:, :], s.padded[:, :], 0.0, ALU.add, ALU.bypass))
    st.do(dve.tensor_tensor(s.first[:, :], s.end[:, :], s.padded[:, :], ALU.subtract))
    st.did(dve.scalar_tensor_tensor(out=s.first[:, :], in0=s.first[:, :], scalar=-1.0, in1=s.before[:, :],
                                    op0=ALU.add, op1=ALU.add))
    dve.wait_ge(s.numbered, 1)
    st.do(dve.tensor_tensor(s.past[:, :, :], s.group_at[:, :].unsqueeze(2).to_broadcast([P, s.n_groups, s.nb]),
                            s.end[:, :].unsqueeze(1).to_broadcast([P, s.n_groups, s.nb]), ALU.is_ge))
    st.do(dve.tensor_reduce(s.bucket[:, :], s.past[:, :, :], AX.X, ALU.add))
    st.do(dve.tensor_scalar(s.bucket[:, :], s.bucket[:, :], float(s.nb - 1), None, ALU.min))


def sort_edges(nc, G, w):
    HALF = BUCKETS // 2
    with Phase(nc, "sort") as ph:
        src = ph.sb("src", [P, EJ], I32)
        dst = ph.sb("dst", [P, EJ], I32)
        attr = ph.sb("attr", [P, EJ * ED])
        we = ph.sb("we", [P, 8 * HEADS])
        be = ph.sb("be", [P, HEADS])
        attrT = ph.sb("attrT", [P, 2, 4, P])
        rec, place = G.rec, G.rec_place
        zero = ph.sb("zero", [P, 2 * D])
        ka = ph.sb("ka", [P, EJ], I32)
        kb = ph.sb("kb", [P, EJ], I32)
        key = ph.sb("key", [P, EJ])
        onehot = ph.sb("onehot", [P, BUCKETS, EJ], BF16)
        rank = ph.sb("rank", [P, HALF, EJ])
        slot = ph.sb("slot", [P, 2, EJ])
        blank = ph.sb("blank", [P, NCH * REC // 4])
        bs = bucket_starts(ph, BUCKETS, GROUP, NG, rank[:, :, :].rearrange("p b j -> p (b j)").bitcast(BF16)[:, 0:NG * BUCKETS].rearrange(
            "p (g b) -> p g b", b=BUCKETS))
        psA = ph.ps("psA", [P, 2, 4, P])
        psE = ph.ps("psE", [P, 2, 64, HEADS])
        (e_in, a_in, w_in, we_zero, blank_ready, blanked, key_step, ranked, slotted,
         a_done, a_ready, e_done, rec_ready, zero_ready, cleared) = ph.sems(
            "e_in", "a_in", "w_in", "we_zero", "blank_ready", "blanked", "key_step", "ranked", "slotted",
            "a_done", "a_ready", "e_done", "rec_ready", "zero_ready", "cleared")
        block = ph.block()
        n_batches = EJ // 64

        @block.sync
        def _(sp):
            sp.dma_start(src[:, :], w["src"].rearrange("(p j) -> p j", p=P)).then_inc(e_in, 16)
            sp.dma_start(dst[:, :], w["dst"].rearrange("(p j) -> p j", p=P)).then_inc(e_in, 16)
            sp.dma_start(attr[:, :], w["edge_attr"].rearrange("(p j) f -> p (j f)", p=P)).then_inc(a_in, 16)
            sp.dma_start(be[:, :], w["be"].partition_broadcast(P)).then_inc(w_in, 16)
            sp.wait_ge(we_zero, 1)
            for k in range(8):
                sp.dma_start(we[k * ED:(k + 1) * ED, k * HEADS:(k + 1) * HEADS], w["We"]).then_inc(w_in, 16)
            sp.wait_ge(blank_ready, 1)
            for k in range(4):
                n = NCH * REC // 4
                sp.dma_start(G.rec_dram.rearrange("(p c) r -> p (c r)", p=P)[:, k * n:(k + 1) * n],
                             blank[:, :]).then_inc(blanked, 16)
            sp.wait_ge(zero_ready, 1)
            for g in range(NST):
                sp.dma_start(G.xs_dram.rearrange("(n p j) d -> p n (j d)", p=P, j=2)[:, g, :],
                             zero[:, :]).then_inc(cleared, 16)
            sp.wait_ge(blanked, 64)
            sp.wait_ge(cleared, 16 * NST)

        @block.gpsimd
        def _(pool):
            pool.memset(we[:, :], 0.0).then_inc(we_zero, 1)
            pool.memset(blank[:, :], -1.0).then_inc(blank_ready, 1)
            bucket_starts_pool(pool, bs)
            pool.memset(zero[:, :], 0.0).then_inc(zero_ready, 1)

        @block.vector
        def _(dve):
            st = Step(dve, key_step, 0, 16)
            dve.wait_ge(e_in, 32)
            st.did(dve.tensor_scalar(ka[:, :], src[:, :], 7, 2, ALU.logical_shift_right, ALU.logical_shift_left))
            st.do(dve.tensor_scalar(kb[:, :], dst[:, :], 4, 3, ALU.logical_shift_right, ALU.bitwise_and))
            st.do(dve.tensor_tensor(key[:, :], ka[:, :], kb[:, :], ALU.add))
            st.do(dve.tensor_scalar(ka[:, :], dst[:, :], 6, 4, ALU.logical_shift_right, ALU.logical_shift_left))
            st.do(dve.tensor_scalar(kb[:, :], dst[:, :], 15, None, ALU.bitwise_and))
            st.did(dve.tensor_tensor(rec[:, :, 9], ka[:, :], kb[:, :], ALU.add))
            st.do(dve.tensor_copy(rec[:, :, 10], kb[:, :]))
            st.do(dve.tensor_scalar(src[:, :], src[:, :], P - 1, None, ALU.bitwise_and))
            st.did(dve.tensor_copy(rec[:, :, 8], src[:, :]))
            st.do(dve.memset(rec[:, :, 11:REC], 0.0))

            def member(b, u):
                dve.tensor_scalar(onehot[:, bass.ds(b, 1), :].rearrange("p a j -> p (a j)"), key[:, :],
                                  col(G.iota512, b), 0.0, ALU.is_equal, ALU.add,
                                  accum_out=col(bs.count, b)).then_inc(bs.counted, 1)
            loop(dve, BUCKETS, member)
            for n in range(n_batches):
                dve.wait_ge(e_done, 2 * n + 2)
                dve.tensor_tensor(rec[:, n * 64:(n + 1) * 64, 0:HEADS], psE[:, n % 2],
                                  be[:, :].unsqueeze(1).to_broadcast([P, 64, HEADS]), ALU.add).then_inc(rec_ready, 1)
            bucket_starts_vector(dve, bs)

            sl = Step(dve, slotted, 0, 12)
            for half in range(2):
                def number(b, u):
                    hot = onehot[:, bass.ds(b + half * HALF, 1), :].rearrange("p a j -> p (a j)")
                    dve.tensor_tensor_scan(rank[:, bass.ds(b, 1), :].rearrange("p a j -> p (a j)"), hot, hot,
                                           col(bs.first, b + half * HALF), ALU.add, ALU.bypass).then_inc(ranked, 1)
                loop(dve, HALF, number)
                dve.wait_ge(ranked, HALF * (half + 1))
                sl.do(dve.tensor_tensor(rank[:, :, :], rank[:, :, :], onehot[:, half * HALF:(half + 1) * HALF],
                                        ALU.mult))
                sl.do(dve.tensor_reduce(slot[:, half], rank[:, :, :].rearrange("p b j -> p j b"), AX.X, ALU.add))
            sl.do(dve.tensor_tensor(slot[:, 0], slot[:, 0], slot[:, 1], ALU.add))
            sl.do(dve.tensor_copy(ka[:, :], slot[:, 0]))
            sl.did(dve.tensor_scalar(kb[:, :], ka[:, :], 7, None, ALU.logical_shift_right))
            sl.do(dve.tensor_scalar(ka[:, :], ka[:, :], P - 1, None, ALU.bitwise_and))
            sl.did(dve.scalar_tensor_tensor(out=place[:, :], in0=ka[:, :], scalar=float(NCH), in1=kb[:, :],
                                            op0=ALU.mult, op1=ALU.add))
            sl.did(dve.tensor_copy(G.edge_bucket[:, :], bs.bucket[:, :]))

        @block.scalar
        def _(act):
            for n in range(2 * n_batches):
                act.wait_ge(a_done, n + 1)
                if n >= 2:
                    act.wait_ge(e_done, n - 1)
                act.activation(attrT[:, n % 2], psA[:, n % 2], ACT.Copy).then_inc(a_ready, 1)

        @block.tensor
        def _(pe):
            pe.wait_ge(a_in, 16)
            pe.wait_ge(w_in, 16 * 9)
            for n in range(2 * n_batches):
                if n >= 2:
                    pe.wait_ge(a_ready, n - 1)
                for k in range(4):
                    g = 4 * n + k
                    mm = pe.transpose(psA[:, n % 2, k], attr[:, g * P:(g + 1) * P], G.ident[:, :])
                mm.then_inc(a_done, 1)
                pe.wait_ge(a_ready, n + 1)
                if n >= 4 and n % 2 == 0:
                    pe.wait_ge(rec_ready, n // 2 - 1)
                for k in range(4):
                    g = 4 * (n % 2) + k
                    mm = pe.matmul(psE[:, (n // 2) % 2, g * 8:(g + 1) * 8].rearrange("p j h -> p (j h)"),
                                   attrT[:, n % 2, k], we[:, :], start=True, stop=True)
                mm.then_inc(e_done, 1)
            bucket_starts_tensor(pe, bs, G, BUCKETS)


def build_graph(nc, G):
    RING = 4
    with Phase(nc, "graph") as ph:
        rec = ph.sb("rec", [P, NCH, REC])
        adj = ph.sb("adj", [P, BUCKETS * ACOLS], U16)
        far = ph.sb("far", [P, 2, P])
        row = ph.sb("row", [P, RING, 2, P])
        row16 = ph.sb("row16", [P, RING, 2, P], F16)
        number16 = ph.sb("number16", [P, ACOLS], F16)
        cols = ph.sb("cols", [P, RING, 2, ACOLS], F16)
        bias = ph.sb("bias", [P, RING, 2, 16, HEADS])
        sums = ph.sb("sums", [P, 2, BCOLS])
        psA = [ph.ps(f"psA{u}", [P, ACOLS]) for u in range(2)]
        psB = [ph.ps(f"psB{u}", [P, D]) for u in range(2)]
        (rec_in, bias_zero, adj_zero, far_ready, row_ready, cols_ready, g_done, adj_added, bias_added,
         adj_out, numbered, passed, sums_out) = ph.sems("rec_in", "bias_zero", "adj_zero", "far_ready", "row_ready", "cols_ready", "g_done",
                            "adj_added", "bias_added", "adj_out", "numbered", "passed", "sums_out")
        block = ph.block()

        half = BUCKETS * ACOLS // 2

        def group_done(g):
            return g + 1 + RING

        @block.sync
        def _(sp):
            sp.dma_start(rec[:, :, :], G.rec_dram.rearrange("(p c) r -> p c r", p=P)).then_inc(rec_in, 16)
            sp.wait_ge(adj_added, done(NG - 1))
            sp.dma_start(G.adj_dram, adj[:, :]).then_inc(adj_out, 16)
            sp.wait_ge(adj_out, 16)

        @block.gpsimd
        def _(pool):
            pool.memset(adj[:, half:].bitcast(U32), 0).then_inc(adj_zero, 1)
            pool.memset(G.BIAS[:, :], 0.0).then_inc(bias_zero, 1)
            lead(pool, bias_added)
            pool.wait_ge(bias_zero, 1)

            def add(g, u):
                b = pool.value_load(G.edge_bucket[0:1, bass.ds(g, 1)], min_val=0, max_val=BUCKETS - 1)
                a = G.BIAS[:, bass.ds(b * BCOLS, BCOLS)]
                gate(pool, bias_added, g + LEAD, passed)
                gate(pool, sums_out, done(g), passed)
                pool.tensor_tensor(a, a, sums[:, u], ALU.add).then_inc(bias_added, 1)
            loop(pool, NG, add, 2)

        @block.scalar
        def _(act):
            act.wait_ge(rec_in, 16)
            lead(act, row_ready, 2)
            lead(act, sums_out)

            def rows(g, u):
                act.wait_ge(row_ready, reuse(g + 1, 2))
                for k in range(2):
                    act.activation(far[:, k], G.iota512[:, 0:P], ACT.Abs, scale=-1.0,
                                   bias=rec[:, bass.ds(g * 2 + k, 1), :].rearrange("p a r -> p (a r)")[:, 8:9]
                                   ).then_inc(far_ready, 1)
                act.wait_ge(far_ready, g * 2 + 2)
                act.wait_ge(g_done, group_done(g - RING))
                act.activation(row[:, u], far[:, :, :], ACT.Relu, scale=-1.0, bias=1.0).then_inc(row_ready, 1)
                act.activation(row16[:, u], far[:, :, :], ACT.Relu, scale=-1.0, bias=1.0).then_inc(row_ready, 1)

            def body(g, u):
                if not (isinstance(g, int) and g + 2 >= NG):
                    rows(g + 2, (u + 2) % RING)
                act.wait_ge(g_done, group_done(g))
                act.wait_ge(bias_added, reuse(g))
                act.activation(sums[:, u % 2], psB[u % 2][:, 0:BCOLS], ACT.Copy).then_inc(sums_out, 1)
            rows(0, 0)
            rows(1, 1)
            loop(act, NG, body, RING, peel=RING)

        @block.vector
        def _(dve):
            dve.tensor_copy(number16[:, :], G.iota512[:, :]).then_inc(numbered, 1)
            dve.wait_ge(numbered, 1)
            dve.memset(adj[:, 0:half].bitcast(U32), 0).then_inc(adj_zero, 1)
            dve.wait_ge(rec_in, 16)

            def columns(g, u):
                dve.wait_ge(g_done, group_done(g - RING))
                for k in range(2):
                    r = rec[:, bass.ds(g * 2 + k, 1), :].rearrange("p a r -> p (a r)")
                    dve.tensor_scalar(cols[:, u, k], number16[:, :], r[:, 9:10], None,
                                      ALU.is_equal).then_inc(cols_ready, 1)
                    dve.scalar_tensor_tensor(out=bias[:, u, k], in0=G.iota16x8[:, :, :], scalar=r[:, 10:11],
                                             in1=r[:, 0:HEADS].unsqueeze(1).to_broadcast([P, 16, HEADS]),
                                             op0=ALU.is_equal, op1=ALU.mult).then_inc(cols_ready, 1)

            def add(g, u, b):
                dve.wait_ge(g_done, group_done(g))
                a = adj[:, bass.ds(b * ACOLS, ACOLS)]
                dve.wait_ge(adj_added, g + LEAD)
                dve.tensor_tensor(a, a, psA[u % 2][:, :], ALU.add).then_inc(adj_added, 1)

            def body(g, u):
                b = dve.value_load(G.edge_bucket[0:1, bass.ds(g, 1)], min_val=0, max_val=BUCKETS - 1)
                if not (isinstance(g, int) and g + 2 >= NG):
                    columns(g + 2, (u + 2) % RING)
                add(g, u, b)
            lead(dve, adj_added)
            columns(0, 0)
            columns(1, 1)
            dve.wait_ge(adj_zero, 2)
            loop(dve, NG, body, RING, peel=RING)

        @block.tensor
        def _(pe):
            lead(pe, g_done, RING)

            def body(g, u):
                pe.wait_ge(cols_ready, g * 4 + 4)
                pe.wait_ge(row_ready, done(g, 2))
                pe.wait_ge(adj_added, reuse(g))
                for k in range(2):
                    pe.matmul(psA[u % 2][:, :], row16[:, u, k], cols[:, u, k], start=(k == 0), stop=(k == 1))
                pe.wait_ge(sums_out, reuse(g))
                for k in range(2):
                    mm = pe.matmul(psB[u % 2][:, 0:BCOLS], row[:, u, k], bias[:, u, k].rearrange("p r h -> p (r h)"),
                                   start=(k == 0), stop=(k == 1))
                mm.then_inc(g_done, 1)
            loop(pe, NG, body, RING)


def linear_attention_scan(nc, G, w):
    SET = 8
    scale = DH ** -0.5
    with Phase(nc, "lin") as ph:
        wq, wk, wv, wo = (ph.sb(n, [P, DC, D]) for n in ("wq", "wk", "wv", "wo"))
        ln = ln_stats_buffers(ph)
        xn = ph.sb("xn", [P, 2, 2, D])
        xnT = ph.sb("xnT", [P, 2, DC, BLK])
        eq = ph.sb("eq", [P, DC, BLK])
        rq = ph.sb("rq", [P, DC, BLK])
        ek = ph.sb("ek", [P, D])
        rk = ph.sb("rk", [P, D])
        kf = ph.sb("kf", [P, 2, D])
        vf = ph.sb("vf", [P, 2, D])
        ctxT = ph.sb("ctxT", [P, PAIRS, P])
        ksum = ph.sb("ksum", [P, PAIRS])
        kmask = ph.sb("kmask", [P, PAIRS, P])
        den = ph.sb("den", [P, 2, D])
        psT = ph.ps("psT", [P, DC, BLK])
        psQ = ph.ps("psQ", [P, DC, BLK])
        psK = ph.ps("psK", [P, D])
        psV = ph.ps("psV", [P, D])
        psC = ph.ps("psC", [P, PAIRS, P])
        psS = ph.ps("psS", [P, PAIRS, 2])
        wq_in, wk_in, wv_in, wo_in = ph.sems("wq_in", "wk_in", "wv_in", "wo_in")
        xn_ready, t_done, xnT_ready = ph.sems("xn_ready", "t_done", "xnT_ready")
        q_done, q_exp, q_relu, q_ready = ph.sems("q_done", "q_exp", "q_relu", "q_ready")
        k_done, k_exp, k_relu, k_ready = ph.sems("k_done", "k_exp", "k_relu", "k_ready")
        v_done, v_ready, ctx_done = ph.sems("v_done", "v_ready", "ctx_done")
        ctx_zero, ctx_ready, kmask_ready, m_done, m_ready = ph.sems("ctx_zero", "ctx_ready", "kmask_ready", "m_done",
                                                                    "m_ready")
        d_done, d_eps, d_rec, d_used = ph.sems("d_done", "d_eps", "d_rec", "d_used")
        rec_now = ph.sb("rec_now", [P, 2, SET, REC])
        place_now = ph.sb("place_now", [P, 2, SET], I32)
        M = ph.sb("M", [P, PAIRS, D])
        rec_copied, passed, m_out = ph.sems("rec_copied", "passed", "m_out")
        scattered = ph.sems("scattered0", "scattered1")
        spill = ph.sems("spill0", "spill1")
        block = ph.block()
        n_cols = N_TOK // D

        @block.sync
        def _(sp):
            for dst, name, sem in ((wq, "mix_wq", wq_in), (wk, "mix_wk", wk_in), (wv, "mix_wv", wv_in),
                                   (wo, "mix_wo", wo_in)):
                sp.dma_start(dst[:, :, :], w[name].rearrange("(c p) n -> p c n", p=P)).then_inc(sem, 16)

            def body(b, u):
                sp.wait_ge(xnT_ready, b + 1)
                sp.dma_start(G.xnT_dram[:, bass.ds(b * DC * BLK, DC * BLK)],
                             xnT[:, u].rearrange("p c n -> p (c n)")).then_inc(spill[u], 16)
            loop(sp, NB, body)
            sp.wait_ge(m_ready, PAIRS)
            sp.dma_start(G.m_dram, M[:, :, :].rearrange("p c n -> p (c n)")).then_inc(m_out, 16)
            for u in range(2):
                sp.wait_ge(spill[u], 16 * NB // 2)
            sp.wait_ge(m_out, 16)

        @block.gpsimd
        def _(pool):
            ln_stats_pool(pool, ln, G)
            pool.memset(ctxT[:, :, :], 0.0).then_inc(ctx_zero, 1)
            lead(pool, rec_copied, 2)

            def scatter(n, u):
                if not (isinstance(n, int) and n < 2):
                    gate(pool, scattered[u], (n - u) * SET * 8, passed)
                pool.tensor_copy(place_now[:, u], G.rec_place[:, bass.ds(n * SET, SET)]).then_inc(rec_copied, 1)
                pool.tensor_copy(rec_now[:, u], G.rec[:, bass.ds(n * SET, SET), :]).then_inc(rec_copied, 1)
                gate(pool, rec_copied, done(n, 2), passed)
                for k in range(SET):
                    pool.indirect_dma_start(
                        out=G.rec_dram, out_offset=bass.IndirectOffsetOnAxis(ap=place_now[:, u, k:k + 1], axis=0),
                        in_=rec_now[:, u, k], in_offset=None).then_inc(scattered[u], 16)
            loop(pool, EJ // SET, scatter, head=2)
            for u in range(2):
                pool.wait_ge(scattered[u], EJ // 2 * 16)

        @block.vector
        def _(dve):
            ln_stats_vector(dve, ln, G.bn)

            def norm_block(b, u):
                dve.wait_ge(t_done, reuse(b))
                for j in range(2):
                    t = b * 2 + j
                    dve.tensor_scalar(xn[:, u, j], token_tile(G.X, t), col(ln.rstd, t), col(ln.shift, t),
                                      ALU.mult, ALU.add).then_inc(xn_ready, 1)

            def body(b, u):
                if not is_last(b, NB):
                    norm_block(b + 1, 1 - u)
                dve.wait_ge(q_exp, b + 1)
                dve.tensor_scalar(rq[:, :, :], psQ[:, :, :], 0.0, scale, ALU.max, ALU.mult).then_inc(q_relu, 1)
                dve.wait_ge(q_relu, b + 1)
                dve.scalar_tensor_tensor(out=G.Q[:, :, bass.ds(b * BLK, BLK)], in0=eq[:, :, :], scalar=1.0,
                                         in1=rq[:, :, :], op0=ALU.min, op1=ALU.add).then_inc(q_ready, 1)
                for j in range(2):
                    t = b * 2 + j
                    dve.wait_ge(k_exp, t + 1)
                    dve.tensor_scalar(rk[:, :], psK[:, :], 0.0, None, ALU.max).then_inc(k_relu, 1)
                    dve.wait_ge(k_relu, t + 1)
                    dve.wait_ge(ctx_done, reuse(t))
                    dve.scalar_tensor_tensor(out=kf[:, j], in0=ek[:, :], scalar=1.0, in1=rk[:, :],
                                             op0=ALU.min, op1=ALU.add).then_inc(k_ready, 1)
            norm_block(0, 0)
            loop(dve, NB, body, peel=1)
            dve.wait_ge(ctx_done, done(NT - 1))
            dve.wait_ge(ctx_zero, 1)
            dve.tensor_copy(ctxT[0:DH, :, 0:DH], psC[0:DH, :, 0:DH]).then_inc(ctx_ready, 1)
            dve.tensor_copy(ctxT[DH:P, :, DH:P], psC[DH:P, :, DH:P]).then_inc(ctx_ready, 1)
            dve.tensor_copy(ksum[:, :], psS[:, :, 0]).then_inc(ctx_ready, 1)
            dve.wait_ge(ctx_ready, 3)
            for c in range(PAIRS):
                dve.tensor_scalar(kmask[:, c], G.headmask[:, :], ksum[:, c:c + 1], None,
                                  ALU.mult).then_inc(kmask_ready, 1)

            def divide(n, u):
                for c in range(DC):
                    s = n * DC + c
                    r = c % 2
                    q = G.Q[:, c, bass.ds(n * D, D)]
                    dve.wait_ge(d_done, s + 1)
                    dve.wait_ge(d_used, reuse(s))
                    dve.tensor_scalar(den[:, r], (psK, psV)[r][:, :], 1e-8, None, ALU.add).then_inc(d_eps, 1)
                    dve.wait_ge(d_eps, s + 1)
                    dve.reciprocal(den[:, r], den[:, r]).then_inc(d_rec, 1)
                    dve.wait_ge(d_rec, s + 1)
                    dve.tensor_tensor(q, q, den[:, r], ALU.mult).then_inc(d_used, 1)
            lead(dve, d_used)
            loop(dve, n_cols, divide, 1)

        @block.scalar
        def _(act):
            def body(b, u):
                act.wait_ge(t_done, done(b))
                act.wait_ge(v_done, reuse(b, 2))
                act.wait_ge(spill[u], (b - u) * 8)
                act.activation(xnT[:, u], psT[:, :, :], ACT.Copy).then_inc(xnT_ready, 1)
                act.wait_ge(q_done, b + 1)
                act.wait_ge(q_ready, b)
                act.activation(eq[:, :, :], psQ[:, :, :], ACT.Exp, scale=scale).then_inc(q_exp, 1)
                for j in range(2):
                    t = b * 2 + j
                    act.wait_ge(k_done, t + 1)
                    act.wait_ge(k_ready, t)
                    act.activation(ek[:, :], psK[:, :], ACT.Exp).then_inc(k_exp, 1)
                    act.wait_ge(v_done, t + 3)
                    act.wait_ge(ctx_done, reuse(t))
                    act.activation(vf[:, j], psV[:, :], ACT.Copy).then_inc(v_ready, 1)
            loop(act, NB, body)
            for c in range(PAIRS):
                act.wait_ge(m_done, c + 1)
                act.activation(M[:, c], psQ[:, 2 * (c % 2):2 * (c % 2) + 2].rearrange("p c n -> p (c n)"),
                               ACT.Copy).then_inc(m_ready, 1)

        @block.tensor
        def _(pe):
            lead(pe, t_done)
            lead(pe, v_done, 2)
            lead(pe, ctx_done)

            def context(t, j):
                pe.wait_ge(k_ready, t + 1)
                pe.wait_ge(v_ready, t + 1)
                for c in range(PAIRS):
                    first = isinstance(t, int) and t == 0 and c == 0
                    pe.matmul(psC[:, c], vf[:, j, c * P:(c + 1) * P], kf[:, j, c * P:(c + 1) * P],
                              start=first, stop=is_last(t, NT), skip_group_check=True)
                for c in range(PAIRS):
                    first = isinstance(t, int) and t == 0 and c == 0
                    mm = pe.matmul(psS[:, c], kf[:, j, c * P:(c + 1) * P], G.ones[:, 0:2],
                                   start=first, stop=is_last(t, NT), skip_group_check=True)
                mm.then_inc(ctx_done, 1)

            def body(b, u):
                first = isinstance(b, int) and b == 0
                pe.wait_ge(xn_ready, b * 2 + 2)
                pe.wait_ge(xnT_ready, b)
                for c in range(DC):
                    for j in range(2):
                        mm = pe.transpose(psT[:, c, j * P:(j + 1) * P], xn[:, u, j, c * P:(c + 1) * P], G.ident[:, :])
                mm.then_inc(t_done, 1)
                pe.wait_ge(xnT_ready, b + 1)
                pe.wait_ge(q_ready, b)
                if first:
                    pe.wait_ge(wq_in, 16)
                for c in range(DC):
                    for d in range(DC):
                        mm = pe.matmul(psQ[:, c], wq[:, d, c * P:(c + 1) * P], xnT[:, u, d], start=(d == 0),
                                       stop=(d == DC - 1))
                mm.then_inc(q_done, 1)
                for j in range(2):
                    t = b * 2 + j
                    for ps, wt, wt_in, free, sem in ((psK, wk, wk_in, k_ready, k_done),
                                                     (psV, wv, wv_in, v_ready, v_done)):
                        if first and j == 0:
                            pe.wait_ge(wt_in, 16)
                        pe.wait_ge(free, t)
                        for d in range(DC):
                            mm = pe.matmul(ps[:, :], xnT[:, u, d, j * P:(j + 1) * P], wt[:, d], start=(d == 0),
                                           stop=(d == DC - 1))
                        mm.then_inc(sem, 1)
                for j in range(2):
                    context(b * 2 + j, j)
            body(0, 0)
            body(1, 1)
            with pe.Fori(1, NB // 2 - 1) as i:
                for u in range(2):
                    body(i * 2 + u, u)
            body(NB - 2, 0)
            body(NB - 1, 1)
            pe.wait_ge(ctx_ready, 3)
            pe.wait_ge(wo_in, 16)
            for c in range(PAIRS):
                if c == 0:
                    pe.wait_ge(q_ready, NB)
                if c >= 2:
                    pe.wait_ge(m_ready, c - 1)
                pe.matmul(psQ[:, 2 * (c % 2):2 * (c % 2) + 2].rearrange("p c n -> p (c n)"), ctxT[:, c], wo[:, c],
                          start=True, stop=True).then_inc(m_done, 1)
            pe.wait_ge(kmask_ready, PAIRS)

            def denominators(n, u):
                for c in range(DC):
                    s = n * DC + c
                    pe.wait_ge(d_used, reuse(s))
                    pe.matmul((psK, psV)[c % 2][:, :], kmask[:, c], G.Q[:, c, bass.ds(n * D, D)], start=True,
                              stop=True).then_inc(d_done, 1)
            loop(pe, n_cols, denominators, 1)


def graph_attention(nc, G, w):
    VW = DH + 2
    with Phase(nc, "attn") as ph:
        wq, wk, wv, wo = (ph.sb(n, [P, DC, D]) for n in ("wq", "wk", "wv", "wo"))
        bq, bk = (ph.sb(n, [P, DC]) for n in ("bq", "bk"))
        bv, bo, bsum = (ph.sb(n, [P, D]) for n in ("bv", "bo", "bsum"))
        M = ph.sb("M", [P, PAIRS, D])
        xnT = ph.sb("xnT", [P, 2, DC, BLK])
        mq = ph.sb("mq", [P, 2, DC, BLK])
        qT = ph.sb("qT", [P, 2, DC, BLK])
        kT = ph.sb("kT", [P, 2, DC, BLK])
        v = ph.sb("v", [P, 2, HEADS, VW])
        s = ph.sb("s", [P, 2, HEADS, GRAPH])
        top = ph.sb("top", [P, 2, HEADS])
        prob = ph.sb("prob", [P, 2, HEADS, P])
        probT = ph.sb("probT", [P, 2, 4, P])
        rsum = ph.sb("rsum", [P, HEADS])
        o = ph.sb("o", [P, HEADS, DH])
        oT = ph.sb("oT", [P, DC, P])
        y = ph.sb("y", [P, D])
        psQ = ph.ps("psQ", [P, DC, BLK])
        psV = ph.ps("psV", [P, D])
        psS = ph.ps("psS", [P, 2, D])
        psP = ph.ps("psP", [P, 4, P])
        psO = ph.ps("psO", [P, 2, D])
        names = ("w_in wq_in wk_in wv_in wo_in m_in bsum_ready prob_zero v_ones x_in0 x_in1 mq_ready passed_pool passed_pe q_done q_ready v_done "
                 "v_ready s_done s_biased top_ready s_ready p_ready t_done pT_ready o_done rsum_ready o_ready oT_done "
                 "oT_ready y_done y_ready x_ready stats").split()
        S = dict(zip(names, ph.sems(*names)))
        S = type("Sems", (), S)
        x_in = [S.x_in0, S.x_in1]
        block = ph.block()

        @block.sync
        def _(sp):
            def body(b, u):
                sp.wait_ge(S.v_done, reuse(b, 2))
                sp.dma_start(xnT[:, u].rearrange("p c n -> p (c n)"),
                             G.xnT_dram[:, bass.ds(b * DC * BLK, DC * BLK)]).then_inc(x_in[u], 16)
            for dst, name in ((bq, "bq"), (bk, "bk")):
                sp.dma_start(dst[:, :], w[name]).then_inc(S.w_in, 16)
            for dst, name in ((bv, "bv"), (bo, "bo"), (bsum, "b_out")):
                sp.dma_start(dst[:, :], w[name].partition_broadcast(P)).then_inc(S.w_in, 16)
            for dst, name, sem in ((wq, "Wq", S.wq_in), (wk, "Wk", S.wk_in), (wv, "Wv", S.wv_in), (wo, "Wo", S.wo_in)):
                sp.dma_start(dst[:, :, :], w[name].rearrange("(c p) n -> p c n", p=P)).then_inc(sem, 16)
                if sem is S.wq_in:
                    body(0, 0)
            sp.dma_start(M[:, :, :].rearrange("p c n -> p (c n)"), G.m_dram).then_inc(S.m_in, 16)
            loop(sp, NB, body, head=2, done_steps=1)

        @block.gpsimd
        def _(pool):
            pool.memset(prob[:, :, :, :], 0.0).then_inc(S.prob_zero, 1)
            pool.memset(v[:, :, :, DH:VW], 1.0).then_inc(S.v_ones, 1)

            def body(b, u):
                gate(pool, S.y_done, reuse(b, 2), S.passed_pool)
                pool.tensor_copy(mq[:, u], G.Q[:, :, bass.ds(b * BLK, BLK)]).then_inc(S.mq_ready, 1)
            loop(pool, NB, body)

        @block.vector
        def _(dve):
            dve.wait_ge(S.w_in, 16 * 5)
            dve.tensor_tensor(bsum[:, :], bsum[:, :], bo[:, :], ALU.add).then_inc(S.bsum_ready, 1)
            dve.wait_ge(S.bsum_ready, 1)
            dve.wait_ge(S.v_ones, 1)

            def front(t, j):
                dve.wait_ge(S.v_done, t + 1 + 2 * LEAD)
                dve.wait_ge(S.o_done, reuse(t))
                dve.tensor_tensor(v[:, j, :, 0:DH], psV[:, :].rearrange("p (h d) -> p h d", h=HEADS),
                                  bv[:, :].rearrange("p (h d) -> p h d", h=HEADS), ALU.add).then_inc(S.v_ready, 1)
                dve.wait_ge(S.s_done, t + 1)
                dve.wait_ge(S.p_ready, reuse(t, 2))
                bias = G.BIAS[:, bass.ds(t * GRAPH * HEADS, GRAPH * HEADS)].rearrange(
                    "p (m h r) -> p r h m", m=GRAPH, r=2)
                heads = s[:, j].rearrange("p (h r) m -> p r h m", r=2)
                for r in range(2):
                    dve.scalar_tensor_tensor(out=heads[:, r], in0=psS[:, r, 0:4 * GRAPH].rearrange(
                        "p (h m) -> p h m", h=4), scalar=DH ** -0.5, in1=bias[:, r], op0=ALU.mult,
                        op1=ALU.add).then_inc(S.s_biased, 1)
                dve.wait_ge(S.s_biased, t * 2 + 2)
                dve.tensor_reduce(top[:, j], s[:, j], AX.X, ALU.max).then_inc(S.top_ready, 1)
                dve.wait_ge(S.top_ready, t + 1)
                dve.tensor_tensor(s[:, j], s[:, j], top[:, j].unsqueeze(2).to_broadcast([P, HEADS, GRAPH]),
                                  ALU.subtract).then_inc(S.s_ready, 1)

            def back(t, j):
                sums = psO[:, :, 0:4 * VW].rearrange("p r (h d) -> p r h d", h=4)
                dve.wait_ge(S.o_done, done(t))
                dve.reciprocal(rsum[:, :].rearrange("p (r h) -> p r h", r=2), sums[:, :, :, DH]).then_inc(S.rsum_ready, 1)
                dve.wait_ge(S.rsum_ready, t + 1)
                dve.wait_ge(S.oT_done, t)
                for r in range(2):
                    dve.tensor_tensor(o[:, 4 * r:4 * r + 4], sums[:, r, :, 0:DH],
                                      rsum[:, 4 * r:4 * r + 4].unsqueeze(2).to_broadcast([P, 4, DH]),
                                      ALU.mult).then_inc(S.o_ready, 1)
                dve.wait_ge(S.y_done, t + 1 + 2 * LEAD)
                dve.wait_ge(S.x_ready, t)
                dve.tensor_tensor(y[:, :], psV[:, :], bsum[:, :], ALU.add).then_inc(S.y_ready, 1)
                dve.wait_ge(S.y_ready, t + 1)
                dve.tensor_tensor(token_tile(G.X, t), token_tile(G.X, t), y[:, :], ALU.add).then_inc(S.x_ready, 1)
                dve.wait_ge(S.x_ready, t + 1)
                tile_stats(dve, G, t).then_inc(S.stats, 1)

            def body(b, u):
                front(b * 2 + 1, 1)
                back(b * 2, 0)
                if not is_last(b, NB):
                    front(b * 2 + 2, 0)
                back(b * 2 + 1, 1)
            front(0, 0)
            loop(dve, NB, body, peel=1)

        @block.scalar
        def _(act):
            act.wait_ge(S.w_in, 16 * 5)
            act.wait_ge(S.prob_zero, 1)
            lead(act, S.p_ready, 2)

            def project(b, u):
                for k, (dst, bias) in enumerate(((qT, bq), (kT, bk))):
                    act.wait_ge(S.q_done, b * 2 + k + 1)
                    for c in range(DC):
                        act.activation(dst[:, u, c], psQ[:, c], ACT.Identity, bias=bias[:, c:c + 1],
                                       ).then_inc(S.q_ready, 1)

            def exponentials(t, j):
                act.wait_ge(S.s_ready, t + 1)
                act.wait_ge(S.t_done, t * 2)
                for g in range(2):
                    h = slice(g * GRAPH, (g + 1) * GRAPH)
                    act.activation(prob[h, j, :, h], s[h, j], ACT.Exp).then_inc(S.p_ready, 1)

            def transposed(t, j):
                for r in range(2):
                    act.wait_ge(S.t_done, t * 2 + r + 1)
                    if r == 0:
                        act.wait_ge(S.o_done, t + LEAD)
                    act.activation(probT[:, r], psP[:, :, :], ACT.Copy).then_inc(S.pT_ready, 1)

            def output(t, j):
                act.wait_ge(S.oT_done, t + 1)
                act.wait_ge(S.y_done, t + 2 * LEAD)
                act.activation(oT[:, :, :], psP[:, :, :], ACT.Copy).then_inc(S.oT_ready, 1)

            def body(b, u):
                transposed(b * 2, 0)
                exponentials(b * 2 + 1, 1)
                output(b * 2, 0)
                if not is_last(b, NB):
                    project(b + 1, 1 - u)
                transposed(b * 2 + 1, 1)
                if not is_last(b, NB):
                    exponentials(b * 2 + 2, 0)
                output(b * 2 + 1, 1)
            project(0, 0)
            exponentials(0, 0)
            loop(act, NB, body, peel=1)

        @block.tensor
        def _(pe):
            lead(pe, S.v_done, 2)
            lead(pe, S.o_done)
            lead(pe, S.y_done, 2)

            def project(b, u):
                pe.wait_ge(x_in[u], (b - u) * 8 + 16)
                for k, (wt, wt_in) in enumerate(((wq, S.wq_in), (wk, S.wk_in))):
                    if isinstance(b, int) and b == 0:
                        pe.wait_ge(wt_in, 16)
                    pe.wait_ge(S.q_ready, (b * 2 + k) * DC)
                    for c in range(DC):
                        for d in range(DC):
                            mm = pe.matmul(psQ[:, c], wt[:, d, c * P:(c + 1) * P], xnT[:, u, d], start=(d == 0),
                                           stop=(d == DC - 1))
                    mm.then_inc(S.q_done, 1)

            def front(t, u, j):
                pe.wait_ge(S.v_ready, t)
                if not (isinstance(t, int) and t == 0):
                    pe.wait_ge(S.y_ready, t - 1)
                for d in range(DC):
                    mm = pe.matmul(psV[:, :], xnT[:, u, d, j * P:(j + 1) * P], wv[:, d], start=(d == 0),
                                   stop=(d == DC - 1))
                mm.then_inc(S.v_done, 1)
                if j == 0:
                    pe.wait_ge(S.q_ready, (t + 2) * DC)
                gate(pe, S.s_biased, t * 2, S.passed_pe)
                for h in range(HEADS):
                    r = slice((h % 2) * DH, (h % 2 + 1) * DH)
                    for g in range(2):
                        n = slice(j * P + g * GRAPH, j * P + (g + 1) * GRAPH)
                        mm = pe.matmul(psS[g * GRAPH:(g + 1) * GRAPH, h % 2, (h // 2) * GRAPH:(h // 2 + 1) * GRAPH],
                                       qT[r, u, h // 2, n], kT[r, u, h // 2, n], start=True, stop=True)
                mm.then_inc(S.s_done, 1)

            def back(t, b, u, j):
                pe.wait_ge(S.p_ready, (t + 1 + LEAD) * 2)
                for r in range(2):
                    pe.wait_ge(*((S.oT_ready, t) if r == 0 else (S.pT_ready, t * 2 + 1)))
                    for h in range(4):
                        mm = pe.transpose(psP[:, h], prob[:, j, 4 * r + h], G.ident[:, :])
                    mm.then_inc(S.t_done, 1)
                pe.wait_ge(S.v_ready, t + 1)
                pe.wait_ge(S.o_ready, t * 2)
                for r in range(2):
                    pe.wait_ge(S.pT_ready, t * 2 + r + 1)
                    for h in range(4):
                        mm = pe.matmul(psO[:, r, h * VW:(h + 1) * VW], probT[:, r, h], v[:, j, 4 * r + h],
                                       start=True, stop=True)
                mm.then_inc(S.o_done, 1)
                pe.wait_ge(S.o_ready, t * 2 + 2)
                for c in range(DC):
                    mm = pe.transpose(psP[:, c], o[:, 2 * c:2 * c + 2].rearrange("p h d -> p (h d)"), G.ident[:, :])
                mm.then_inc(S.oT_done, 1)
                if is_last(t, NT):
                    pe.wait_ge(S.y_ready, t)
                else:
                    pe.wait_ge(S.v_ready, t + 2)
                if j == 0:
                    pe.wait_ge(S.mq_ready, b + 1)
                for c in range(DC):
                    pe.matmul(psV[:, :], mq[:, u, c, j * P:(j + 1) * P], M[:, c], start=(c == 0), stop=False)
                pe.wait_ge(S.oT_ready, t + 1)
                for c in range(DC):
                    mm = pe.matmul(psV[:, :], oT[:, c], wo[:, c], start=False, stop=(c == DC - 1))
                mm.then_inc(S.y_done, 1)

            def body(b, u):
                front(b * 2 + 1, u, 1)
                back(b * 2, b, u, 0)
                if not is_last(b, NB):
                    project(b + 1, 1 - u)
                    front(b * 2 + 2, 1 - u, 0)
                back(b * 2 + 1, b, u, 1)
            project(0, 0)
            pe.wait_ge(S.wv_in, 16)
            front(0, 0, 0)
            pe.wait_ge(S.wo_in, 16)
            pe.wait_ge(S.m_in, 16)
            loop(pe, NB, body, peel=1)


def route(nc, G, w, pre, shared):
    FS = 4
    with Phase(nc, f"route{pre}") as ph:
        wr = ph.sb("wr", [P, DC, EXPERTS])
        br = ph.sb("br", [P, EXPERTS])
        ln = ln_stats_buffers(ph)
        hn = ph.sb("hn", [P, 2, 2, D])
        H = ph.sb("H", [P, NT, D])
        hT = ph.sb("hT", [P, 2, DC, BLK])
        L = ph.sb("L", [P, NT, EXPERTS])
        small = [ph.sb(f"small{i}", [P, NT]) for i in range(3)]
        pv = ph.sb("pv", [P, NT, 8])
        pidx = ph.sb("pidx", [P, NT, 8], U32)
        which = ph.sb("which", [P, NT, TOPK])
        onehot = ph.sb("onehot", [P, EXPERTS, TOPK * NT])
        rank = ph.sb("rank", [P, EXPERTS, TOPK * NT])
        part1 = ph.sb("part1", [P, NT, EXPERTS])
        slot = ph.sb("slot", [P, TOPK * NT])
        same = ph.sb("same", [P, NST])
        bs = bucket_starts(ph, EXPERTS, SLOT_TILE, NST, ph.sb("past", [P, NST, EXPERTS]))
        psT = ph.ps("psT", [P, DC, BLK])
        psL = ph.ps("psL", [P, 2, EXPERTS])
        names = ("w_in w1_in w2_in b_in passed_pe passed_pool kept h_ready t_done hT_ready l_done l_ready step exps_ready count_step slotted scattered "
                 "hid_done hid_ready y_done y_ready x_ready srow_ready").split()
        S = type("Sems", (), dict(zip(names, ph.sems(*names))))
        n_w = 2
        if shared:
            w1 = ph.sb("w1", [P, DC, FS * P])
            w2 = ph.sb("w2", [P, FS, D])
            b1 = ph.sb("b1", [P, FS])
            brow = ph.sb("brow", [P, 2, D])
            srow = ph.sb("srow", [P, D])
            hid = ph.sb("hid", [P, 2, FS, BLK])
            y = ph.sb("y", [P, D])
            psH = [ph.ps(f"psH{i}", [P, D]) for i in range(2)]
            psY = ph.ps("psY", [P, D])
            n_w = 3
        block = ph.block()

        @block.sync
        def _(sp):
            sp.dma_start(wr[:, :, :], w[pre + "Wr"].rearrange("(c p) n -> p c n", p=P)).then_inc(S.w_in, 16)
            sp.dma_start(br[:, :], w[pre + "br"].partition_broadcast(P)).then_inc(S.w_in, 16)
            if shared:
                sp.dma_start(b1[:, :], w["sb1"]).then_inc(S.w_in, 16)
                for n in range(2):
                    sp.dma_start(brow[:, n], w["sb2"][n].partition_broadcast(P)).then_inc(S.b_in, 16)
                sp.dma_start(w1[:, :, :], w["sw1"].rearrange("(c p) n -> p c n", p=P)).then_inc(S.w1_in, 16)
                sp.dma_start(w2[:, :, :], w["sw2"].rearrange("(c p) n -> p c n", p=P)).then_inc(S.w2_in, 16)

        @block.gpsimd
        def _(pool):
            ln_stats_pool(pool, ln, G)
            bucket_starts_pool(pool, bs)
            lead(pool, S.kept)

            def keep(b, u):
                gate(pool, S.h_ready, b * 2 + 2, S.passed_pool)
                pool.tensor_copy(H[:, bass.ds(b * 2, 2), :], hn[:, u]).then_inc(S.kept, 1)
            loop(pool, NB, keep)
            pool.wait_ge(S.kept, done(NB - 1))
            pool.wait_ge(S.slotted, 5)
            for k in range(TOPK):
                for t in range(NT):
                    n = k * NT + t
                    pool.indirect_dma_start(
                        out=G.xs_dram, out_offset=bass.IndirectOffsetOnAxis(ap=G.place[:, n:n + 1], axis=0),
                        in_=H[:, t], in_offset=None).then_inc(S.scattered, 16)
            pool.wait_ge(S.scattered, 16 * TOPK * NT)

        @block.vector
        def _(dve):
            ln_stats_vector(dve, ln, G.bn)
            if shared:
                dve.wait_ge(S.b_in, 32)
                dve.tensor_tensor(srow[:, :], brow[:, 0], brow[:, 1], ALU.add).then_inc(S.srow_ready, 1)
                dve.wait_ge(S.srow_ready, 1)

            def norm_block(b, u):
                dve.wait_ge(S.t_done, reuse(b))
                dve.wait_ge(S.kept, reuse(b))
                for j in range(2):
                    t = b * 2 + j
                    dve.tensor_scalar(hn[:, u, j], token_tile(G.X, t), col(ln.rstd, t), col(ln.shift, t),
                                      ALU.mult, ALU.add).then_inc(S.h_ready, 1)

            def body(b, u):
                if not is_last(b, NB):
                    norm_block(b + 1, 1 - u)
                dve.wait_ge(S.l_done, b + 1)
                dve.tensor_tensor(L[:, bass.ds(b * 2, 2), :], psL[:, :, :],
                                  br[:, :].unsqueeze(1).to_broadcast([P, 2, EXPERTS]), ALU.add).then_inc(S.l_ready, 1)
                if shared:
                    for j in range(2):
                        t = b * 2 + j
                        dve.wait_ge(S.y_done, t + 1 + 2 * LEAD)
                        dve.wait_ge(S.x_ready, t)
                        dve.tensor_tensor(y[:, :], psY[:, :], srow[:, :], ALU.add).then_inc(S.y_ready, 1)
                        dve.wait_ge(S.y_ready, t + 1)
                        dve.tensor_tensor(token_tile(G.X, t), token_tile(G.X, t), y[:, :],
                                          ALU.add).then_inc(S.x_ready, 1)
            norm_block(0, 0)
            dve.wait_ge(S.w_in, 16 * n_w)
            loop(dve, NB, body, peel=1)
            st = Step(dve, S.step, 0, 64)

            def spread(a):
                return a[:, :].unsqueeze(2).to_broadcast([P, NT, EXPERTS])
            dve.wait_ge(S.l_ready, NB)
            st.do(dve.tensor_reduce(small[0][:, :], L[:, :, :], AX.X, ALU.max))
            st.do(dve.tensor_tensor(L[:, :, :], L[:, :, :], spread(small[0]), ALU.subtract))
            dve.wait_ge(S.exps_ready, 1)
            st.do(dve.tensor_reduce(small[1][:, :], L[:, :, :], AX.X, ALU.add))
            st.do(dve.reciprocal(small[2][:, :], small[1][:, :]))
            st.do(dve.tensor_tensor(L[:, :, :], L[:, :, :], spread(small[2]), ALU.mult))
            for t in range(NT):
                st.did(dve.max(pv[:, t], L[:, t]))
            st.wait()
            for t in range(NT):
                st.did(dve.max_index(pidx[:, t], pv[:, t], L[:, t]))
            st.wait()
            st.did(dve.tensor_copy(which[:, :, :], pidx[:, :, 0:TOPK]))
            st.do(dve.tensor_copy(G.gate[:, :, :], pv[:, :, 0:TOPK]))
            for k in range(TOPK):
                st.did(dve.tensor_tensor(
                    onehot[:, :, k * NT:(k + 1) * NT], G.iota512[:, 0:EXPERTS].unsqueeze(2).to_broadcast([P, EXPERTS, NT]),
                    which[:, :, k].unsqueeze(1).to_broadcast([P, EXPERTS, NT]), ALU.is_equal))
            st.wait()
            dve.tensor_reduce(bs.count[:, :], onehot[:, :, :], AX.X, ALU.add).then_inc(bs.counted, 1)
            for k, dst in enumerate((G.comb, part1)):
                st.did(dve.tensor_tensor(dst[:, :, :], onehot[:, :, k * NT:(k + 1) * NT].rearrange("p e t -> p t e"),
                                         G.gate[:, :, k].unsqueeze(2).to_broadcast([P, NT, EXPERTS]), ALU.mult))
            st.wait()
            st.do(dve.tensor_tensor(G.comb[:, :, :], G.comb[:, :, :], part1[:, :, :], ALU.add))
            bucket_starts_vector(dve, bs)
            for e in range(EXPERTS):
                st.did(dve.tensor_tensor_scan(rank[:, e], onehot[:, e], onehot[:, e], bs.first[:, e:e + 1], ALU.add,
                                              ALU.bypass))
            st.wait()
            sl = Step(dve, S.slotted, 0, 8)
            sl.do(dve.tensor_tensor(rank[:, :, :], rank[:, :, :], onehot[:, :, :], ALU.mult))
            sl.do(dve.tensor_reduce(slot[:, :], rank[:, :, :].rearrange("p e n -> p n e"), AX.X, ALU.add))
            sl.did(dve.tensor_copy(G.place[:, :], slot[:, :]))
            sl.do(dve.tensor_scalar(bs.bucket[:, :], bs.bucket[:, :], float(P), None, ALU.mult))
            sl.did(dve.tensor_scalar(G.wrow[:, :], bs.bucket[:, :], G.part[:, 0:1], None, ALU.add))
            sl.did(dve.memset(same[:, 0:1], 0.0))
            sl.do(dve.tensor_tensor(same[:, 1:NST], bs.bucket[:, 1:NST], bs.bucket[:, 0:NST - 1], ALU.is_equal))
            sl.did(dve.scalar_tensor_tensor(out=G.wnew[:, :], in0=same[:, :], scalar=float(EXPERTS * P),
                                            in1=G.wrow[:, :], op0=ALU.mult, op1=ALU.add))

        @block.scalar
        def _(act):
            act.wait_ge(S.w_in, 16 * n_w)

            lead(act, S.hid_ready)

            def body(b, u):
                act.wait_ge(S.t_done, done(b))
                act.activation(hT[:, u], psT[:, :, :], ACT.Copy).then_inc(S.hT_ready, 1)
                if shared:
                    for f in range(FS):
                        n = b * FS + f
                        act.wait_ge(S.hid_done, n + 1)
                        if f == 0:
                            act.wait_ge(S.y_done, reuse(b, 2))
                        act.activation(hid[:, u, f], psH[f % 2][:, 0:BLK], ACT.Gelu,
                                       bias=b1[:, f:f + 1]).then_inc(S.hid_ready, 1)
            loop(act, NB, body)
            act.wait_ge(S.step, 2)
            act.activation(L[:, :, :], L[:, :, :], ACT.Exp).then_inc(S.exps_ready, 1)

        @block.tensor
        def _(pe):
            lead(pe, S.t_done)
            lead(pe, S.y_done, 2)

            def transposes(b, u):
                pe.wait_ge(S.h_ready, b * 2 + 2)
                pe.wait_ge(S.hT_ready, b)
                for c in range(DC):
                    for j in range(2):
                        mm = pe.transpose(psT[:, c, j * P:(j + 1) * P], hn[:, u, j, c * P:(c + 1) * P], G.ident[:, :])
                mm.then_inc(S.t_done, 1)

            def body(b, u):
                pe.wait_ge(S.hT_ready, b + 1)
                if isinstance(b, int) and b == 0:
                    pe.wait_ge(S.w_in, 16 * n_w)
                gate(pe, S.l_ready, b, S.passed_pe)
                for j in range(2):
                    for c in range(DC):
                        mm = pe.matmul(psL[:, j], hT[:, u, c, j * P:(j + 1) * P], wr[:, c], start=(c == 0),
                                       stop=(c == DC - 1))
                mm.then_inc(S.l_done, 1)
                if shared:
                    if isinstance(b, int) and b == 0:
                        pe.wait_ge(S.w1_in, 16)
                    for f in range(FS):
                        pe.wait_ge(S.hid_ready, b * FS + f - 1 + LEAD)
                        for c in range(DC):
                            mm = pe.matmul(psH[f % 2][:, 0:BLK], w1[:, c, f * P:(f + 1) * P], hT[:, u, c],
                                           start=(c == 0), stop=(c == DC - 1))
                        mm.then_inc(S.hid_done, 1)
                if not is_last(b, NB):
                    transposes(b + 1, 1 - u)
                if shared:
                    if isinstance(b, int) and b == 0:
                        pe.wait_ge(S.w2_in, 16)
                    pe.wait_ge(S.hid_ready, b * FS + FS + LEAD)
                    for j in range(2):
                        pe.wait_ge(S.y_ready, b * 2 + j)
                        for f in range(FS):
                            mm = pe.matmul(psY[:, :], hid[:, u, f, j * P:(j + 1) * P], w2[:, f], start=(f == 0),
                                           stop=(f == FS - 1))
                        mm.then_inc(S.y_done, 1)
            transposes(0, 0)
            loop(pe, NB, body, peel=1, head=2)
            bucket_starts_tensor(pe, bs, G, 1)


def experts(nc, G, w, pre, F):
    FC = F // P
    RING = 4
    RAW = min(RING, FC)
    WP = min(4, FC)
    WN = FC * D // WP
    with Phase(nc, f"experts{pre}") as ph:
        w1 = ph.sb("w1", [P, DC, F])
        w2 = ph.sb("w2", [P, FC * D])
        w1h, w1l = (ph.sb(n, [P, DC, F], F32R) for n in ("w1h", "w1l"))
        w2h, w2l = (ph.sb(n, [P, FC * D], F32R) for n in ("w2h", "w2l"))
        b1 = ph.sb("b1", [P, 2, FC])
        b1_index = ph.sb("b1_index", [P, 2], I32)
        w1_index, w2_index = (ph.sb(n, [P, 1], I32) for n in ("w1_index", "w2_index"))
        xs = ph.sb("xs", [P, 2, 2, D])
        xh, xl = (ph.sb(n, [P, DC, BLK], F32R) for n in ("xh", "xl"))
        raw = ph.sb("raw", [P, RAW, BLK])
        hh, hl = (ph.sb(n, [P, 2, FC, BLK], F32R) for n in ("hh", "hl"))
        y = ph.sb("y", [P, 2, 2, D])
        psT = ph.ps("psT", [P, DC, BLK])
        psH = [ph.ps(f"psH{i}", [P, D]) for i in range(RING)]
        psY = [ph.ps(f"psY{i}", [P, D]) for i in range(2)]
        names = ("passed index_ready b_in0 b_in1 w1_in w2_in xs_in0 xs_in1 w1_hi w1_lo w2_hi w2_lo t_done x_hi x_lo "
                 "hid_done gelu_done h_hi h_lo y_done y_ready stored0 stored1").split()
        S = type("Sems", (), dict(zip(names, ph.sems(*names))))
        b_in, xs_in, stored = (S.b_in0, S.b_in1), (S.xs_in0, S.xs_in1), (S.stored0, S.stored1)
        block = ph.block()
        xs_dram = G.xs_dram.rearrange("(n p j) d -> p n (j d)", p=P, j=2)
        ys_dram = G.ys_dram.rearrange("(n p j) d -> p n (j d)", p=P, j=2)

        @block.gpsimd
        def _(pool):
            def gather(dst, table, index, sem, **bound):
                pool.indirect_dma_start(out=dst, out_offset=None, in_=w[pre + table],
                                        in_offset=bass.IndirectOffsetOnAxis(ap=index, axis=0), **bound
                                        ).then_inc(sem, 16)
            bound = dict(bounds_check=EXPERTS * P - 1, oob_is_err=False)

            def load_weights(g, free, pieces, index, dst, table, sem, k):
                gate(pool, free, done(g - 1, pieces), S.passed)
                pool.tensor_copy(index, col(G.wnew, g)).then_inc(S.index_ready, 1)
                gate(pool, S.index_ready, k, S.passed)
                gather(dst, table, index, sem, **bound)

            def load_w2(g):
                load_weights(g, S.w2_lo, WP, w2_index[:, :], w2[:, :], "W2", S.w2_in,
                             g * 3 + 5 if not is_last(g, NST) else NST * 3)

            def load(g, u):
                first = isinstance(g, int) and g == 0
                gate(pool, S.h_lo, reuse(g, FC), S.passed)
                pool.tensor_copy(b1_index[:, u:u + 1], col(G.wrow, g)).then_inc(S.index_ready, 1)
                gate(pool, S.index_ready, 1 if first else g * 3, S.passed)
                gather(b1[:, u], "b1", b1_index[:, u:u + 1], b_in[u])
                load_weights(g, S.w1_lo, DC, w1_index[:, :], w1[:, :, :].rearrange("p c f -> p (c f)"), "W1", S.w1_in,
                             2 if first else g * 3 + 1)
                if not first:
                    load_w2(g - 1)
            loop(pool, NST, load, head=2)
            load_w2(NST - 1)

        @block.sync
        def _(sp):
            def store(g, u):
                sp.wait_ge(S.y_ready, done(g, 2))
                sp.dma_start(ys_dram[:, bass.ds(g, 1), :].rearrange("p a d -> p (a d)"),
                             y[:, u].rearrange("p j d -> p (j d)")).then_inc(stored[u], 16)

            loop(sp, NST, store)
            for u in range(2):
                sp.wait_ge(stored[u], 16 * ((NST + 1 - u) // 2))

        @block.scalar
        def _(act):
            lead(act, S.gelu_done, RING)

            def load_x(g, u):
                act.wait_ge(S.t_done, reuse(g))
                act.dma_start(xs[:, u].rearrange("p j d -> p (j d)"),
                              xs_dram[:, bass.ds(g, 1), :].rearrange("p a d -> p (a d)")).then_inc(xs_in[u], 16)

            def split_w1(g):
                act.wait_ge(S.w1_in, g * 16 + 16)
                act.wait_ge(S.hid_done, g * FC)
                for c in range(DC):
                    act.activation(w1h[:, c], w1[:, c], ACT.Copy).then_inc(S.w1_hi, 1)

            def split_w2(g):
                act.wait_ge(S.w2_in, g * 16 + 16)
                act.wait_ge(S.y_done, done(g - 1, 2))
                for k in range(WP):
                    n = slice(k * WN, (k + 1) * WN)
                    act.activation(w2h[:, n], w2[:, n], ACT.Copy).then_inc(S.w2_hi, 1)

            def split_x(g):
                act.wait_ge(S.t_done, done(g))
                act.wait_ge(S.hid_done, g * FC)
                act.activation(xh[:, :, :], psT[:, :, :], ACT.Copy).then_inc(S.x_hi, 1)

            def hidden(g, u):
                act.wait_ge(b_in[u], (g - u) * 8 + 16)
                act.wait_ge(S.y_done, reuse(g, 2))
                for f in range(FC + 1):
                    if f < FC:
                        act.wait_ge(S.hid_done, g * FC + f + 1)
                        act.wait_ge(S.h_lo, g * FC + f + 1 - RAW + LEAD * FC)
                        act.activation(raw[:, f % RAW], psH[(u * FC + f) % RING][:, 0:BLK], ACT.Gelu,
                                       bias=b1[:, u, f:f + 1]).then_inc(S.gelu_done, 1)
                    if f:
                        act.wait_ge(S.gelu_done, g * FC + f + RING)
                        act.activation(hh[:, u, f - 1], raw[:, (f - 1) % RAW], ACT.Copy).then_inc(S.h_hi, 1)

            def body(g, u):
                if not (isinstance(g, int) and g + 2 >= NST):
                    load_x(g + 2, u)
                hidden(g, u)
                if not is_last(g, NST):
                    split_x(g + 1)
                    split_w1(g + 1)
                split_w2(g)
            load_x(0, 0)
            load_x(1, 1)
            split_w1(0)
            split_x(0)
            loop(act, NST, body, peel=2)

        @block.vector
        def _(dve):
            lead(dve, S.w1_lo, DC)
            lead(dve, S.w2_lo, WP)
            lead(dve, S.h_lo, FC)
            lead(dve, S.y_ready, 2)

            def rest_w1(g):
                for c in range(DC):
                    dve.wait_ge(S.w1_hi, g * DC + c + 1)
                    dve.tensor_tensor(w1l[:, c], w1[:, c], w1h[:, c], ALU.subtract).then_inc(S.w1_lo, 1)

            def rest_w2(g):
                for k in range(WP):
                    n = slice(k * WN, (k + 1) * WN)
                    dve.wait_ge(S.w2_hi, g * WP + k + 1)
                    dve.tensor_tensor(w2l[:, n], w2[:, n], w2h[:, n], ALU.subtract).then_inc(S.w2_lo, 1)

            def rest_x(g):
                dve.wait_ge(S.x_hi, g + 1)
                dve.tensor_tensor(xl[:, :, :], psT[:, :, :], xh[:, :, :], ALU.subtract).then_inc(S.x_lo, 1)

            def outputs(g, u):
                dve.wait_ge(stored[u], (g - u) * 8)
                for j in range(2):
                    dve.wait_ge(S.y_done, g * 2 + j + 1 + 2 * LEAD)
                    dve.tensor_copy(y[:, u, j], psY[j][:, :]).then_inc(S.y_ready, 1)

            def body(g, u):
                for f in range(FC):
                    dve.wait_ge(S.h_hi, g * FC + f + 1)
                    dve.tensor_tensor(hl[:, u, f], raw[:, f % RAW], hh[:, u, f], ALU.subtract).then_inc(S.h_lo, 1)
                if not is_last(g, NST):
                    rest_x(g + 1)
                    rest_w1(g + 1)
                if not (isinstance(g, int) and g == 0):
                    outputs(g - 1, 1 - u)
                rest_w2(g)
            rest_w1(0)
            rest_x(0)
            loop(dve, NST, body, peel=1, head=2)
            outputs(NST - 1, (NST - 1) % 2)

        @block.tensor
        def _(pe):
            lead(pe, S.t_done)
            lead(pe, S.y_done, 2)

            def transposes(g, u):
                pe.wait_ge(xs_in[u], (g - u) * 8 + 16)
                pe.wait_ge(S.x_lo, g)
                for c in range(DC):
                    for j in range(2):
                        mm = pe.transpose(psT[:, c, j * P:(j + 1) * P], xs[:, u, j, c * P:(c + 1) * P], G.ident[:, :])
                mm.then_inc(S.t_done, 1)

            def hidden(g, u):
                pe.wait_ge(S.x_lo, g + 1)
                pe.wait_ge(S.w1_lo, done(g, DC))
                for f in range(FC):
                    pe.wait_ge(S.gelu_done, g * FC + f + 1)
                    n = slice(f * P, (f + 1) * P)
                    for c in range(DC):
                        for k, (a, b) in enumerate(((w1h, xh), (w1h, xl), (w1l, xh))):
                            mm = pe.matmul(psH[(u * FC + f) % RING][:, 0:BLK], a[:, c, n], b[:, c],
                                           start=(c + k == 0), stop=(c == DC - 1 and k == 2))
                    mm.then_inc(S.hid_done, 1)

            def outputs(g, u):
                pe.wait_ge(S.h_lo, done(g, FC))
                pe.wait_ge(S.w2_lo, done(g, WP))
                for j in range(2):
                    pe.wait_ge(S.y_ready, g * 2 + j + 1)
                    for f in range(FC):
                        n = slice(f * D, (f + 1) * D)
                        for k, (a, b) in enumerate(((hh, w2h), (hh, w2l), (hl, w2h))):
                            mm = pe.matmul(psY[j][:, :], a[:, u, f, j * P:(j + 1) * P], b[:, n],
                                           start=(f + k == 0), stop=(f == FC - 1 and k == 2))
                    mm.then_inc(S.y_done, 1)

            def body(g, u):
                if not is_last(g, NST):
                    hidden(g + 1, 1 - u)
                if not (isinstance(g, int) and g + 2 >= NST):
                    transposes(g + 2, u)
                outputs(g, u)
            transposes(0, 0)
            hidden(0, 0)
            transposes(1, 1)
            loop(pe, NST, body, peel=2)


def combine(nc, G, w, pre, out):
    with Phase(nc, f"combine{pre}") as ph:
        b2 = ph.sb("b2", [EXPERTS, D])
        place = ph.sb("place", [P, 2, TOPK], I32)
        comb = ph.sb("comb", [P, 2, EXPERTS])
        combT = ph.sb("combT", [EXPERTS, 2, P])
        y = ph.sb("y", [P, 2, TOPK, D])
        psT = ph.ps("psT", [EXPERTS, P])
        psB = [ph.ps(f"psB{i}", [P, D]) for i in range(2)]
        names = ("w_in passed place_ready y_in0 y_in1 comb_ready t_done combT_ready b_done x_biased x_first x_ready "
                 "out0 out1 stats").split()
        S = type("Sems", (), dict(zip(names, ph.sems(*names))))
        y_in, stored = (S.y_in0, S.y_in1), (S.out0, S.out1)
        block = ph.block()

        @block.sync
        def _(sp):
            sp.dma_start(b2[:, :], w[pre + "b2"]).then_inc(S.w_in, 16)
            if out is not None:
                rows = out.rearrange("(t p) d -> p t d", p=P)

                def body(t, u):
                    sp.wait_ge(S.x_ready, done(t))
                    sp.dma_start(rows[:, bass.ds(t, 1), :].rearrange("p a d -> p (a d)"),
                                 token_tile(G.X, t)).then_inc(stored[u], 16)
                loop(sp, NT, body)
                for u in range(2):
                    sp.wait_ge(stored[u], 16 * NT // 2)

        @block.gpsimd
        def _(pool):
            lead(pool, S.place_ready)

            def body(t, u):
                gate(pool, S.x_ready, reuse(t), S.passed)
                pool.tensor_copy(place[:, u], G.place[:, :].rearrange("p (k t) -> p t k", k=TOPK)[
                    :, bass.ds(t, 1), :].rearrange("p a k -> p (a k)")).then_inc(S.place_ready, 1)
                gate(pool, S.place_ready, done(t), S.passed)
                for k in range(TOPK):
                    pool.indirect_dma_start(
                        out=y[:, u, k], out_offset=None, in_=G.ys_dram,
                        in_offset=bass.IndirectOffsetOnAxis(ap=place[:, u, k:k + 1], axis=0)).then_inc(y_in[u], 16)
            loop(pool, NT, body)

        @block.vector
        def _(dve):
            lead(dve, S.x_ready)

            def columns(t, u):
                dve.tensor_copy(comb[:, u], G.comb[:, bass.ds(t, 1), :].rearrange("p a e -> p (a e)")
                                ).then_inc(S.comb_ready, 1)

            def body(t, u):
                if not is_last(t, NT):
                    columns(t + 1, 1 - u)
                x = token_tile(G.X, t)
                gates = G.gate[:, bass.ds(t, 1), :].rearrange("p a k -> p (a k)")
                dve.wait_ge(S.b_done, t + 1)
                dve.tensor_tensor(x, x, psB[u][:, :], ALU.add).then_inc(S.x_biased, 1)
                dve.wait_ge(y_in[u], (t - u) * 16 + 32)
                dve.wait_ge(S.x_biased, t + 1)
                dve.scalar_tensor_tensor(out=x, in0=y[:, u, 0], scalar=gates[:, 0:1], in1=x, op0=ALU.mult,
                                         op1=ALU.add).then_inc(S.x_first, 1)
                dve.wait_ge(S.x_first, t + 1)
                dve.scalar_tensor_tensor(out=x, in0=y[:, u, 1], scalar=gates[:, 1:2], in1=x, op0=ALU.mult,
                                         op1=ALU.add).then_inc(S.x_ready, 1)
                if out is None:
                    dve.wait_ge(S.x_ready, done(t))
                    tile_stats(dve, G, t).then_inc(S.stats, 1)
            columns(0, 0)
            loop(dve, NT, body, peel=2)

        @block.scalar
        def _(act):
            def body(t, u):
                act.wait_ge(S.t_done, t + 1)
                act.activation(combT[:, u], psT[:, :], ACT.Copy).then_inc(S.combT_ready, 1)
            loop(act, NT, body)

        @block.tensor
        def _(pe):
            pe.wait_ge(S.w_in, 16)

            def body(t, u):
                pe.wait_ge(S.comb_ready, t + 1)
                pe.wait_ge(S.combT_ready, t)
                pe.transpose(psT[:, :], comb[:, u], G.ident[:, :]).then_inc(S.t_done, 1)
                pe.wait_ge(S.combT_ready, t + 1)
                pe.wait_ge(S.x_ready, reuse(t))
                pe.matmul(psB[u][:, :], combT[:, u], b2[:, :], start=True, stop=True).then_inc(S.b_done, 1)
            loop(pe, NT, body)


def neighbour_products(nc, G, w):
    with Phase(nc, "nprod") as ph:
        w12 = ph.sb("w12", [P, 2, DC, D])
        ln = ln_stats_buffers(ph)
        xn = ph.sb("xn", [P, 2, 2, D])
        xnT = ph.sb("xnT", [P, 2, DC, BLK])
        psT = ph.ps("psT", [P, DC, BLK])
        psY = [[ph.ps(f"psY{k}{j}", [P, D]) for j in range(2)] for k in range(2)]
        names = "w1_in w2_in adj_in xn_ready kept0 kept1 stats t_done xnT_ready y1_done y2_done y1_ready y2_ready".split()
        S = type("Sems", (), dict(zip(names, ph.sems(*names))))
        kept = (S.kept0, S.kept1)
        w_in = (S.w1_in, S.w2_in)
        block = ph.block()

        @block.sync
        def _(sp):
            for k in range(2):
                sp.dma_start(w12[:, k], w["gw"][k * D:(k + 1) * D, :].rearrange("(c p) n -> p c n", p=P)
                             ).then_inc(w_in[k], 16)
            sp.dma_start(G.adj[:, :], G.adj_dram).then_inc(S.adj_in, 16)

            def keep(b, u):
                sp.wait_ge(S.xn_ready, b * 2 + 2)
                sp.dma_start(G.xn_dram[:, bass.ds(b * 2 * D, 2 * D)],
                             xn[:, u].rearrange("p j d -> p (j d)")).then_inc(kept[u], 16)
            loop(sp, NB, keep)
            for u in range(2):
                sp.wait_ge(kept[u], 16 * NB // 2)
            sp.wait_ge(S.adj_in, 16)

        @block.gpsimd
        def _(pool):
            ln_stats_pool(pool, ln, G)

        @block.vector
        def _(dve):
            ln_stats_vector(dve, ln, G.bn)

            def norm_block(b, u):
                dve.wait_ge(S.t_done, reuse(b))
                dve.wait_ge(kept[u], (b - u) * 8)
                for j in range(2):
                    t = b * 2 + j
                    dve.tensor_scalar(xn[:, u, j], token_tile(G.X, t), col(ln.rstd, t), col(ln.shift, t),
                                      ALU.mult, ALU.add).then_inc(S.xn_ready, 1)
                dve.wait_ge(S.xn_ready, b * 2 + 2)
                for j in range(2):
                    dve.bn_stats(G.bn[:, bass.ds(b * 2 + j, 1), :].rearrange("p a s -> p (a s)"),
                                 xn[:, u, j]).then_inc(S.stats, 1)

            def body(b, u):
                if not is_last(b, NB):
                    norm_block(b + 1, 1 - u)
                for j in range(2):
                    t = b * 2 + j
                    dve.wait_ge(S.y2_done, t + 1)
                    dve.tensor_copy(token_tile(G.Y2, t), psY[1][j][:, :]).then_inc(S.y2_ready, 1)
            norm_block(0, 0)
            loop(dve, NB, body, peel=1)

        @block.scalar
        def _(act):
            def body(b, u):
                act.wait_ge(S.t_done, done(b))
                act.activation(xnT[:, u], psT[:, :, :], ACT.Copy).then_inc(S.xnT_ready, 1)
                for j in range(2):
                    t = b * 2 + j
                    act.wait_ge(S.y1_done, t + 1)
                    act.activation(token_tile(G.Y1, t), psY[0][j][:, :], ACT.Copy).then_inc(S.y1_ready, 1)
            loop(act, NB, body)

        @block.tensor
        def _(pe):
            lead(pe, S.t_done)

            def transposes(b, u):
                pe.wait_ge(S.xn_ready, b * 2 + 2)
                pe.wait_ge(S.xnT_ready, b)
                for c in range(DC):
                    for j in range(2):
                        mm = pe.transpose(psT[:, c, j * P:(j + 1) * P], xn[:, u, j, c * P:(c + 1) * P], G.ident[:, :])
                mm.then_inc(S.t_done, 1)

            def body(b, u):
                pe.wait_ge(S.xnT_ready, b + 1)
                for j in range(2):
                    for k, (free, sem) in enumerate(((S.y1_ready, S.y1_done), (S.y2_ready, S.y2_done))):
                        if isinstance(b, int) and b + j == 0:
                            pe.wait_ge(w_in[k], 16)
                        pe.wait_ge(free, b * 2)
                        for c in range(DC):
                            mm = pe.matmul(psY[k][j][:, :], xnT[:, u, c, j * P:(j + 1) * P], w12[:, k, c],
                                           start=(c == 0), stop=(c == DC - 1))
                        mm.then_inc(sem, 1)
                    if j == 0 and not is_last(b, NB):
                        transposes(b + 1, 1 - u)
            transposes(0, 0)
            loop(pe, NB, body, peel=1, head=2)


def neighbour_mean(nc, G):
    with Phase(nc, "nmean") as ph:
        counts = ph.sb("counts", [P, 2, NT, P])
        rdeg = ph.sb("rdeg", [P, 2])
        z = ph.sb("z", [P, 2, D])
        psZ = [ph.ps(f"psZ{i}", [P, D]) for i in range(2)]
        psD = [ph.ps(f"psD{i}", [P, 2]) for i in range(2)]
        names = "counts_ready z_done deg_ready rdeg_ready z_ready x_ready".split()
        S = type("Sems", (), dict(zip(names, ph.sems(*names))))
        block = ph.block()

        @block.vector
        def _(dve):
            def widen(t, u):
                dve.wait_ge(S.z_done, reuse(t))
                for g in range(2):
                    a = G.adj3[:, :, bass.ds(t * 32 + g * 16, 16)]
                    dst = counts[:, u, :, g * GRAPH:(g + 1) * GRAPH].rearrange("p s (q r) -> p s q r", q=4)
                    dve.tensor_copy(dst, a.rearrange("p (s q) r -> p s q r", q=4)).then_inc(S.counts_ready, 1)

            def body(t, u):
                if not is_last(t, NT):
                    widen(t + 1, 1 - u)
                dve.wait_ge(S.z_done, done(t))
                dve.tensor_scalar(rdeg[:, 0:1], psD[u][:, 0:1], 1.0, None, ALU.max).then_inc(S.deg_ready, 1)
                dve.wait_ge(S.deg_ready, t + 1)
                dve.reciprocal(rdeg[:, 1:2], rdeg[:, 0:1]).then_inc(S.rdeg_ready, 1)
                dve.wait_ge(S.rdeg_ready, t + 1)
                dve.scalar_tensor_tensor(out=z[:, u], in0=psZ[u][:, :], scalar=rdeg[:, 1:2], in1=token_tile(G.Y1, t),
                                         op0=ALU.mult, op1=ALU.add).then_inc(S.z_ready, 1)
                dve.wait_ge(S.z_ready, t + 1)
                dve.scalar_tensor_tensor(out=token_tile(G.X, t), in0=z[:, u], scalar=0.0, in1=token_tile(G.X, t),
                                         op0=ALU.max, op1=ALU.add).then_inc(S.x_ready, 1)
            widen(0, 0)
            loop(dve, NT, body, peel=2)

        @block.tensor
        def _(pe):
            lead(pe, S.z_done)

            def body(t, u):
                pe.wait_ge(S.counts_ready, t * 2 + 2)
                for s in range(NT):
                    pe.matmul(psZ[u][:, :], counts[:, u, s], G.Y2[:, s], start=(s == 0), stop=(s == NT - 1))
                    mm = pe.matmul(psD[u][:, :], counts[:, u, s], G.ones[:, 0:2], start=(s == 0), stop=(s == NT - 1))
                mm.then_inc(S.z_done, 1)
            loop(pe, NT, body)


def flow_projections(nc, G, w):
    with Phase(nc, "fproj") as ph:
        wq, wk, wv = (ph.sb(n, [P, DC, D]) for n in ("wq", "wk", "wv"))
        bq, bk, g1, be1 = (ph.sb(n, [P, DC]) for n in ("bq", "bk", "g1", "be1"))
        bv = ph.sb("bv", [P, D])
        ln = ln_stats_buffers(ph)
        xin = ph.sb("xin", [P, 2, 2, D])
        xn = ph.sb("xn", [P, 2, 2, D])
        xnT = ph.sb("xnT", [P, 2, DC, BLK])
        part = ph.sb("part", [P, 2, DC, NB])
        psT = ph.ps("psT", [P, DC, BLK])
        psQ = [ph.ps(f"psQ{i}", [P, DC, BLK]) for i in range(2)]
        psV = [ph.ps(f"psV{i}", [P, D]) for i in range(2)]
        names = ("w_in wq_in wk_in wv_in x_in0 x_in1 xn_ready t_done xnT_ready q_done q_ready v_done v_ready sums_ready").split()
        S = type("Sems", (), dict(zip(names, ph.sems(*names))))
        x_in = (S.x_in0, S.x_in1)
        block = ph.block()

        @block.sync
        def _(sp):
            for dst, name in ((bq, "F_bq"), (bk, "F_bk"), (g1, "g1"), (be1, "be1")):
                sp.dma_start(dst[:, :], w[name]).then_inc(S.w_in, 16)
            sp.dma_start(bv[:, :], w["F_bv"].partition_broadcast(P)).then_inc(S.w_in, 16)
            def load(b, u):
                sp.wait_ge(S.xn_ready, reuse(b, 2))
                sp.dma_start(xin[:, u].rearrange("p j d -> p (j d)"),
                             G.xn_dram[:, bass.ds(b * 2 * D, 2 * D)]).then_inc(x_in[u], 16)
            load(0, 0)
            for dst, name, sem in ((wq, "F_Wq", S.wq_in), (wk, "F_Wk", S.wk_in), (wv, "F_Wv", S.wv_in)):
                sp.dma_start(dst[:, :, :], w[name].rearrange("(c p) n -> p c n", p=P)).then_inc(sem, 16)
            loop(sp, NB, load, head=2, done_steps=1)

        @block.gpsimd
        def _(pool):
            ln_stats_pool(pool, ln, G)

        @block.vector
        def _(dve):
            ln_stats_vector(dve, ln, G.bn)
            dve.wait_ge(S.w_in, 16 * 5)
            lead(dve, S.xn_ready, 2)

            def norm_block(b, u):
                dve.wait_ge(x_in[u], (b - u) * 8 + 16)
                dve.wait_ge(S.t_done, reuse(b))
                for j in range(2):
                    t = b * 2 + j
                    dve.tensor_scalar(xn[:, u, j], xin[:, u, j], col(ln.rstd, t), col(ln.shift, t),
                                      ALU.mult, ALU.add).then_inc(S.xn_ready, 1)

            def body(b, u):
                if not is_last(b, NB):
                    norm_block(b + 1, 1 - u)
                for j in range(2):
                    t = b * 2 + j
                    dve.wait_ge(S.v_done, t + 1)
                    dve.tensor_tensor(token_tile(G.V, t), psV[j][:, :], bv[:, :], ALU.add).then_inc(S.v_ready, 1)
            norm_block(0, 0)
            loop(dve, NB, body, peel=1)
            dve.wait_ge(S.q_ready, NB * 2 * DC)
            dve.tensor_reduce(G.qksum[:, :, :], part[:, :, :, :], AX.X, ALU.add).then_inc(S.sums_ready, 1)

        @block.scalar
        def _(act):
            act.wait_ge(S.w_in, 16 * 5)

            def body(b, u):
                act.wait_ge(S.t_done, done(b))
                for c in range(DC):
                    act.activation(xnT[:, u, c], psT[:, c], ACT.Identity, bias=be1[:, c:c + 1],
                                   scale=g1[:, c:c + 1]).then_inc(S.xnT_ready, 1)
                for k, (dst, bias) in enumerate(((G.Q, bq), (G.K, bk))):
                    act.wait_ge(S.q_done, b * 2 + k + 1)
                    for c in range(DC):
                        act.activation(dst[:, c, bass.ds(b * BLK, BLK)], psQ[k][:, c], ACT.Sigmoid,
                                       bias=bias[:, c:c + 1], accum_out=part[:, k, c, bass.ds(b, 1)]
                                       ).then_inc(S.q_ready, 1)
            loop(act, NB, body)

        @block.tensor
        def _(pe):
            lead(pe, S.t_done)

            def transposes(b, u):
                pe.wait_ge(S.xn_ready, (b + 1 + LEAD) * 2)
                pe.wait_ge(S.xnT_ready, b * DC)
                for c in range(DC):
                    for j in range(2):
                        mm = pe.transpose(psT[:, c, j * P:(j + 1) * P], xn[:, u, j, c * P:(c + 1) * P], G.ident[:, :])
                mm.then_inc(S.t_done, 1)

            def body(b, u):
                pe.wait_ge(S.xnT_ready, b * DC + DC)
                for k, (wt, wt_in) in enumerate(((wq, S.wq_in), (wk, S.wk_in))):
                    if isinstance(b, int) and b == 0:
                        pe.wait_ge(wt_in, 16)
                    pe.wait_ge(S.q_ready, b * 2 * DC)
                    for c in range(DC):
                        for d in range(DC):
                            mm = pe.matmul(psQ[k][:, c], wt[:, d, c * P:(c + 1) * P], xnT[:, u, d],
                                           start=(d == 0), stop=(d == DC - 1))
                    mm.then_inc(S.q_done, 1)
                    if k == 0 and not is_last(b, NB):
                        transposes(b + 1, 1 - u)
                if isinstance(b, int) and b == 0:
                    pe.wait_ge(S.wv_in, 16)
                for j in range(2):
                    pe.wait_ge(S.v_ready, b * 2 + j)
                    for d in range(DC):
                        mm = pe.matmul(psV[j][:, :], xnT[:, u, d, j * P:(j + 1) * P], wv[:, d], start=(d == 0),
                                       stop=(d == DC - 1))
                    mm.then_inc(S.v_done, 1)
            transposes(0, 0)
            loop(pe, NB, body, peel=1, head=2)


def flow_scan(nc, G, w):
    NBIG = N_TOK // D
    NX = NBIG * DC
    with Phase(nc, "fscan") as ph:
        wo = ph.sb("wo", [P, DC, D])
        sums = ph.sb("sums", [P, 4, DC])
        masked = ph.sb("masked", [P, 4, DC, HEADS])
        eps = ph.sb("eps", [P, 2])
        const = ph.sb("const", [HEADS, 4])
        rows = ph.sb("rows", [HEADS, 4, N_TOK])
        part = ph.sb("part", [P, 2, NBIG, DC])
        prod = ph.sb("prod", [P, 2, D])
        junk = ph.sb("junk", [P, D])
        stat = ph.sb("stat", [HEADS, 4])
        ke = ph.sb("ke", [P, DC, D])
        kt = prod
        kv = junk[:, :].rearrange("p (c n) -> p c n", c=PAIRS)
        kvT = ke[:, 0].rearrange("p (c n) -> p c n", c=PAIRS)
        psC = ph.ps("psC", [HEADS, 4, 2])
        psR = [ph.ps(f"psR{i}", [HEADS, D]) for i in range(2)]
        psX = [ph.ps(f"psX{i}", [P, D]) for i in range(2)]
        psT = [ph.ps(f"psT{i}", [P, D]) for i in range(2)]
        psK = ph.ps("psK", [P, PAIRS, P])
        names = ("w_in eps_ready kv_zero sum_step masked_ready c_done c_ready r_done r_ready rec_ready x_done x_used "
                 "summed step sig_ready exp_ready t_done kt_ready kv_done kv_ready kvT_done kvT_ready "
                 "m_done m_ready flow_ready passed passed_dve").split()
        S = type("Sems", (), dict(zip(names, ph.sems(*names))))
        block = ph.block()
        X_of = (G.Q, G.K, G.Q, G.K)

        @block.sync
        def _(sp):
            sp.dma_start(wo[:, :, :], w["F_Wo"].rearrange("(c p) n -> p c n", p=P)).then_inc(S.w_in, 16)

        @block.gpsimd
        def _(pool):
            pool.memset(eps[:, :], FLOW_EPS).then_inc(S.eps_ready, 1)
            pool.wait_ge(S.summed, done(2 * NX - 1))
            pool.memset(junk[:, :], 0.0).then_inc(S.kv_zero, 1)

        @block.tensor
        def _(pe):
            pe.wait_ge(S.eps_ready, 1)
            lead(pe, S.kv_done)

            def head_sums(i):
                pe.wait_ge(S.masked_ready, i + 1)
                pe.wait_ge(S.c_ready, i)
                for c in range(DC):
                    mm = pe.matmul(psC[:, i], masked[:, i, c], eps[:, :], start=(c == 0), stop=(c == DC - 1))
                mm.then_inc(S.c_done, 1)

                def body(n, u):
                    pe.wait_ge(S.r_ready, reuse(n + i * NBIG))
                    for c in range(DC):
                        mm = pe.matmul(psR[u][:, :], masked[:, i, c], X_of[i][:, c, bass.ds(n * D, D)],
                                       start=(c == 0), stop=(c == DC - 1))
                    mm.then_inc(S.r_done, 1)
                loop(pe, NBIG, body)

            def spread(k, row, n):
                for c in range(DC):
                    gate(pe, S.x_used, reuse(n * DC + c + k * NX), S.passed)
                    pe.matmul(psX[c % 2][:, :], G.rep[:, c], rows[:, row, bass.ds(n * D, D)], start=True,
                              stop=True).then_inc(S.x_done, 1)
            head_sums(0)
            head_sums(1)
            for row in range(2):
                pe.wait_ge(S.rec_ready, (row + 1) * NBIG)
                loop(pe, NBIG, lambda n, u: spread(row, row, n))
            head_sums(2)
            head_sums(3)
            pe.wait_ge(S.step, STEPS)

            def context(n, u):
                spread(2, 3, n)
                pe.wait_ge(S.x_used, done(n * DC + DC - 1 + 2 * NX))
                for j in range(5):
                    t = n * 4 + j
                    if j < 4:
                        pe.wait_ge(S.kt_ready, reuse(t))
                        for c in range(DC):
                            mm = pe.transpose(psT[j % 2][:, c * P:(c + 1) * P], ke[:, c, j * P:(j + 1) * P],
                                              G.ident[:, :])
                        mm.then_inc(S.t_done, 1)
                    if j:
                        pe.wait_ge(S.kt_ready, done(t - 1))
                        for c in range(PAIRS):
                            mm = pe.matmul(psK[:, c], kt[:, (j - 1) % 2, c * P:(c + 1) * P],
                                           G.V[:, bass.ds(t - 1, 1), c * P:(c + 1) * P].rearrange("p a m -> p (a m)"),
                                           start=(isinstance(t, int) and t == 1 and c == 0),
                                           stop=is_last(t - 1, NT), skip_group_check=True)
                        mm.then_inc(S.kv_done, 1)
            for n in range(NBIG):
                context(n, n % 2)
            pe.wait_ge(S.kv_ready, 2)
            for c in range(PAIRS):
                mm = pe.transpose(psT[0][:, c * P:(c + 1) * P], kv[:, c], G.ident[:, :])
            mm.then_inc(S.kvT_done, 1)
            pe.wait_ge(S.kvT_ready, 1)
            pe.wait_ge(S.w_in, 16)
            for c in range(PAIRS):
                if c >= 2:
                    pe.wait_ge(S.m_ready, c - 1)
                pe.matmul(psX[c % 2][:, :], kvT[:, c], wo[:, c], start=True, stop=True).then_inc(S.m_done, 1)

        @block.vector
        def _(dve):
            lead(dve, S.r_ready)
            lead(dve, S.x_used)
            ss = Step(dve, S.sum_step, 0, 8)
            ss.did(dve.tensor_scalar(sums[:, 0], G.qksum[:, 1], FLOW_EPS, None, ALU.add))
            ss.do(dve.tensor_scalar(sums[:, 1], G.qksum[:, 0], FLOW_EPS, None, ALU.add))

            def mask(i):
                dve.tensor_tensor(masked[:, i], G.sel[:, :, :], sums[:, i].unsqueeze(2).to_broadcast([P, DC, HEADS]),
                                  ALU.mult).then_inc(S.masked_ready, 1)

            def take(i, invert):
                dve.wait_ge(S.c_done, i + 1)
                dve.tensor_copy(const[:, i:i + 1], psC[:, i, 0:1]).then_inc(S.c_ready, 1)
                dve.wait_ge(S.c_ready, i + 1)

                def body(n, u):
                    m = n + i * NBIG
                    r = rows[:, i, bass.ds(n * D, D)]
                    dve.wait_ge(S.r_done, m + 1)
                    dve.tensor_scalar(r, psR[u][:, :], const[:, i:i + 1], None, ALU.add).then_inc(S.r_ready, 1)
                    if invert:
                        gate(dve, S.r_ready, done(m), S.passed_dve)
                        dve.reciprocal(r, r).then_inc(S.rec_ready, 1)
                loop(dve, NBIG, body)

            def weigh(row, X):
                def body(n, u):
                    for c in range(DC):
                        m = n * DC + c + row * NX
                        dve.wait_ge(S.x_done, m + 1)
                        dve.wait_ge(S.summed, reuse(m))
                        dve.tensor_tensor(prod[:, c % 2], X[:, c, bass.ds(n * D, D)], psX[c % 2][:, :],
                                          ALU.mult).then_inc(S.x_used, 1)
                loop(dve, NBIG, body)
            mask(0)
            mask(1)
            take(0, True)
            take(1, True)
            weigh(0, G.Q)
            weigh(1, G.K)
            dve.wait_ge(S.summed, done(2 * NX - 1))
            for i, k in ((2, 1), (3, 0)):
                ss.do(dve.tensor_reduce(sums[:, i], part[:, k].rearrange("p n c -> p c n"), AX.X, ALU.add))
                ss.do(dve.tensor_scalar(sums[:, i], sums[:, i], FLOW_EPS, None, ALU.add))
                mask(i)
            take(2, False)
            take(3, False)
            st = Step(dve, S.step, 0, STEPS)
            dve.wait_ge(S.r_ready, done(4 * NBIG - 1))
            st.do(dve.tensor_scalar(rows[:, 3], rows[:, 3], -1.0, 1.0, ALU.max, ALU.min))
            st.do(dve.tensor_reduce(stat[:, 0:1], rows[:, 3], AX.X, ALU.max))
            st.do(dve.tensor_scalar(stat[:, 1:2], stat[:, 0:1], -1.0, None, ALU.mult))
            dve.wait_ge(S.exp_ready, 1)
            st.do(dve.reciprocal(stat[:, 3:4], stat[:, 2:3]))
            st.do(dve.tensor_scalar(rows[:, 3], rows[:, 3], stat[:, 3:4], float(N_TOK), ALU.mult, ALU.mult))
            dve.wait_ge(S.sig_ready, 1)
            dve.tensor_tensor(G.flow[:, :], rows[:, 0], rows[:, 2], ALU.mult).then_inc(S.flow_ready, 1)

            def compete(n, u):
                for c in range(DC):
                    m = n * DC + c + 2 * NX
                    dve.wait_ge(S.x_done, m + 1)
                    if c == 0:
                        dve.wait_ge(S.t_done, n * 4)
                    dve.tensor_tensor(ke[:, c], G.K[:, c, bass.ds(n * D, D)], psX[c % 2][:, :], ALU.mult)\
                        .then_inc(S.x_used, 1)
            loop(dve, NBIG, compete)
            dve.wait_ge(S.kv_done, done(NT - 1))
            dve.wait_ge(S.kv_zero, 1)
            for h in (slice(0, DH), slice(DH, P)):
                dve.tensor_copy(kv[h, :, h], psK[h, :, h]).then_inc(S.kv_ready, 1)

        @block.scalar
        def _(act):
            lead(act, S.summed)
            lead(act, S.kt_ready)
            for k in range(2):
                def body(n, u):
                    for c in range(DC):
                        m = n * DC + c + k * NX
                        act.wait_ge(S.x_used, done(m))
                        act.wait_ge(S.summed, m + LEAD)
                        act.activation(junk[:, :], prod[:, c % 2], ACT.Copy,
                                       accum_out=part[:, k, bass.ds(n, 1), c]).then_inc(S.summed, 1)
                loop(act, NBIG, body)
            act.wait_ge(S.r_ready, done(3 * NBIG - 1))
            act.activation(rows[:, 2], rows[:, 2], ACT.Sigmoid).then_inc(S.sig_ready, 1)
            act.wait_ge(S.step, 3)
            act.activation(rows[:, 3], rows[:, 3], ACT.Exp, bias=stat[:, 1:2],
                           accum_out=stat[:, 2:3]).then_inc(S.exp_ready, 1)

            def turn(n, u):
                for j in range(4):
                    t = n * 4 + j
                    act.wait_ge(S.t_done, t + 1)
                    act.wait_ge(S.kv_done, reuse(t))
                    act.activation(kt[:, j % 2], psT[j % 2][:, :], ACT.Copy).then_inc(S.kt_ready, 1)
            loop(act, NBIG, turn)
            act.wait_ge(S.kvT_done, 1)
            act.activation(ke[:, 0], psT[0][:, :], ACT.Copy).then_inc(S.kvT_ready, 1)
            for c in range(PAIRS):
                act.wait_ge(S.m_done, c + 1)
                act.activation(G.M[:, c], psX[c % 2][:, :], ACT.Copy).then_inc(S.m_ready, 1)


STEPS = 5


def flow_output(nc, G, w):
    FM = 2
    with Phase(nc, "fout") as ph:
        w1 = ph.sb("w1", [P, DC, FM * P])
        w2 = ph.sb("w2", [P, FM, D])
        b1 = ph.sb("b1", [P, FM])
        g2, be2 = (ph.sb(n, [P, DC]) for n in ("g2", "be2"))
        bo, b2 = (ph.sb(n, [P, D]) for n in ("bo", "b2"))
        qf = ph.sb("qf", [P, 2, DC, BLK])
        xin = ph.sb("xin", [P, 2, 2, D])
        x1 = ph.sb("x1", [P, 2, 2, D])
        bn = ph.sb("bn", [P, 2, 6])
        mv = ph.sb("mv", [P, 2, 2])
        rstd = ph.sb("rstd", [P, 2])
        hn = ph.sb("hn", [P, 2, 2, D])
        hT = ph.sb("hT", [P, DC, BLK])
        hid = ph.sb("hid", [P, 2, FM, BLK])
        psX = ph.ps("psX", [P, DC, BLK])
        psO = [ph.ps(f"psO{i}", [P, D]) for i in range(2)]
        psT = ph.ps("psT", [P, DC, BLK])
        psH = ph.ps("psH", [P, FM, BLK])
        psY = ph.ps("psY", [P, D])
        names = ("w_in x_in0 x_in1 x_done qf_ready o_done xo_ready x1_ready bn_ready mv_ready rstd_ready hn_ready t_done "
                 "hT_ready hid_done hid_ready y_done y1_ready y2_ready xr_ready passed passed_pe passed_pool stats").split()
        S = type("Sems", (), dict(zip(names, ph.sems(*names))))
        x_in = (S.x_in0, S.x_in1)
        block = ph.block()

        @block.sync
        def _(sp):
            sp.dma_start(w1[:, :, :], w["F_W1"].rearrange("(c p) n -> p c n", p=P)).then_inc(S.w_in, 16)
            sp.dma_start(w2[:, :, :], w["F_W2"].rearrange("(c p) n -> p c n", p=P)).then_inc(S.w_in, 16)
            for dst, name in ((b1, "F_b1"), (g2, "g2"), (be2, "be2")):
                sp.dma_start(dst[:, :], w[name]).then_inc(S.w_in, 16)
            for dst, name in ((bo, "F_bo"), (b2, "F_b2")):
                sp.dma_start(dst[:, :], w[name].partition_broadcast(P)).then_inc(S.w_in, 16)

            def load(b, u):
                sp.wait_ge(S.xo_ready, reuse(b, 2))
                sp.dma_start(xin[:, u].rearrange("p j d -> p (j d)"),
                             G.xn_dram[:, bass.ds(b * 2 * D, 2 * D)]).then_inc(x_in[u], 16)
            loop(sp, NB, load)

        @block.gpsimd
        def _(pool):
            def power(t, u):
                gate(pool, S.mv_ready, t + 1, S.passed_pool)
                pool.tensor_tensor(rstd[:, u:u + 1], mv[:, u, 1:2], G.minus_half[:, 0:1],
                                   ALU.pow).then_inc(S.rstd_ready, 1)
            loop(pool, NT, power)

        @block.vector
        def _(dve):
            dve.wait_ge(S.w_in, 16 * 7)
            lead(dve, S.xo_ready, 2)
            lead(dve, S.xr_ready, 2)

            def first(b, u):
                dve.wait_ge(S.x_done, b + 1)
                dve.wait_ge(S.o_done, reuse(b, 2))
                dve.tensor_tensor(qf[:, u], G.Q[:, :, bass.ds(b * BLK, BLK)], psX[:, :, :],
                                  ALU.mult).then_inc(S.qf_ready, 1)
                dve.wait_ge(x_in[u], (b - u) * 8 + 16)
                dve.wait_ge(S.xr_ready, reuse(b, 2))
                for j in range(2):
                    t = b * 2 + j
                    x = x1[:, u, j]
                    dve.wait_ge(S.o_done, t + 1 + 2 * LEAD)
                    dve.tensor_tensor(x, xin[:, u, j], psO[j][:, :], ALU.add).then_inc(S.xo_ready, 1)
                    dve.wait_ge(S.xo_ready, t + 1 + 2 * LEAD)
                    dve.tensor_tensor(x, x, bo[:, :], ALU.add).then_inc(S.x1_ready, 1)
                    dve.wait_ge(S.x1_ready, t + 1)
                    dve.bn_stats(bn[:, j], x).then_inc(S.bn_ready, 1)
                    gate(dve, S.bn_ready, t + 1, S.passed)
                    dve.bn_aggr(mv[:, j], bn[:, j]).then_inc(S.passed, 1)
                    dve.wait_ge(S.passed, t * 2 + 2)
                    dve.tensor_scalar(mv[:, j, 1:2], mv[:, j, 1:2], LN_EPS, None, ALU.add).then_inc(S.mv_ready, 1)
                for j in range(2):
                    t = b * 2 + j
                    dve.wait_ge(S.rstd_ready, t + 1)
                    dve.tensor_scalar(hn[:, u, j], x1[:, u, j], mv[:, j, 0:1], rstd[:, j:j + 1], ALU.subtract,
                                      ALU.mult).then_inc(S.hn_ready, 1)

            def second(b, u):
                for j in range(2):
                    t = b * 2 + j
                    x = x1[:, u, j]
                    dve.tensor_tensor(x, x, b2[:, :], ALU.add).then_inc(S.y1_ready, 1)
                    dve.wait_ge(S.y_done, t + 1)
                    dve.wait_ge(S.y1_ready, t + 1)
                    dve.tensor_tensor(x, x, psY[:, :], ALU.add).then_inc(S.y2_ready, 1)
                    dve.wait_ge(S.y2_ready, t + 1)
                    dve.tensor_tensor(token_tile(G.X, t), token_tile(G.X, t), x, ALU.add).then_inc(S.xr_ready, 1)
                    dve.wait_ge(S.xr_ready, t + 1 + 2 * LEAD)
                    tile_stats(dve, G, t).then_inc(S.stats, 1)

            def body(b, u):
                if not is_last(b, NB):
                    first(b + 1, 1 - u)
                second(b, u)
            first(0, 0)
            loop(dve, NB, body, peel=1)

        @block.scalar
        def _(act):
            act.wait_ge(S.w_in, 16 * 7)

            def body(b, u):
                act.wait_ge(S.t_done, done(b))
                act.wait_ge(S.hid_done, b)
                for c in range(DC):
                    act.activation(hT[:, c], psT[:, c], ACT.Identity, bias=be2[:, c:c + 1],
                                   scale=g2[:, c:c + 1]).then_inc(S.hT_ready, 1)
                act.wait_ge(S.hid_done, b + 1)
                for f in range(FM):
                    act.activation(hid[:, u, f], psH[:, f], ACT.Gelu, bias=b1[:, f:f + 1]).then_inc(S.hid_ready, 1)
            loop(act, NB, body)

        @block.tensor
        def _(pe):
            pe.wait_ge(S.w_in, 16 * 7)
            lead(pe, S.o_done, 2)
            lead(pe, S.t_done)

            def first(b, u):
                gate(pe, S.qf_ready, b, S.passed_pe)
                for c in range(DC):
                    mm = pe.matmul(psX[:, c], G.rep[:, c], G.flow[:, bass.ds(b * BLK, BLK)], start=True, stop=True)
                mm.then_inc(S.x_done, 1)
                pe.wait_ge(S.qf_ready, b + 1)
                for j in range(2):
                    pe.wait_ge(S.xo_ready, b * 2 + j - 1 + 2 * LEAD)
                    for c in range(DC):
                        mm = pe.matmul(psO[j][:, :], qf[:, u, c, j * P:(j + 1) * P], G.M[:, c], start=(c == 0),
                                       stop=(c == DC - 1))
                    mm.then_inc(S.o_done, 1)

            def second(b, u):
                pe.wait_ge(S.hn_ready, b * 2 + 2)
                pe.wait_ge(S.hT_ready, b * DC)
                for c in range(DC):
                    for j in range(2):
                        mm = pe.transpose(psT[:, c, j * P:(j + 1) * P], hn[:, u, j, c * P:(c + 1) * P], G.ident[:, :])
                mm.then_inc(S.t_done, 1)
                pe.wait_ge(S.hT_ready, b * DC + DC)
                pe.wait_ge(S.hid_ready, b * FM)
                for f in range(FM):
                    for c in range(DC):
                        mm = pe.matmul(psH[:, f], w1[:, c, f * P:(f + 1) * P], hT[:, c], start=(c == 0),
                                       stop=(c == DC - 1))
                mm.then_inc(S.hid_done, 1)
                pe.wait_ge(S.hid_ready, b * FM + FM)
                for j in range(2):
                    pe.wait_ge(S.y2_ready, b * 2 + j)
                    for f in range(FM):
                        mm = pe.matmul(psY[:, :], hid[:, u, f, j * P:(j + 1) * P], w2[:, f], start=(f == 0),
                                       stop=(f == FM - 1))
                    mm.then_inc(S.y_done, 1)

            def body(b, u):
                if not is_last(b, NB):
                    first(b + 1, 1 - u)
                second(b, u)
            first(0, 0)
            loop(pe, NB, body, peel=1)


def program(nc, w, out, phases=(0, 1, 2, 3, 4)):
    G = type("Shared", (), {})()

    def scratch(name, shape, dt=F32):
        return nc.dram_tensor(name, shape, dt, kind="Internal").ap()

    with ExitStack() as ctx:
        def sb(name, shape, dt=F32):
            return ctx.enter_context(nc.sbuf_tensor(name, shape, dt))

        G.X = sb("X", [P, NT, D])
        G.ident = sb("ident", [P, P])
        G.upper = sb("upper", [P, P])
        G.ones = sb("ones", [P, P])
        G.headmask = sb("headmask", [P, P])
        G.iota512 = sb("iota512", [P, ACOLS])
        G.iota16x8 = sb("iota16x8", [P, 16, HEADS])
        G.part = sb("part", [P, 1])
        G.minus_half = sb("minus_half", [P, NT])
        G.edge_bucket = sb("edge_bucket", [P, NG], I32)
        G.bn = sb("bn", [P, NT, 6])
        G.place = sb("place", [P, TOPK * NT], I32)
        G.wrow = sb("wrow", [P, NST], I32)
        G.wnew = sb("wnew", [P, NST], I32)
        G.gate = sb("gate", [P, NT, TOPK])
        G.comb = sb("comb", [P, NT, EXPERTS])
        G.rec_dram = scratch("rec_dram", [P * NCH, REC])
        G.adj_dram = scratch("adj_dram", [P, BUCKETS * ACOLS], U16)
        G.xnT_dram = scratch("xnT_dram", [P, NB * DC * BLK])
        G.m_dram = scratch("m_dram", [P, PAIRS * D])
        G.xn_dram = scratch("xn_dram", [P, NT * D])
        G.xs_dram = scratch("xs_dram", [SLOTS, D])
        G.ys_dram = scratch("ys_dram", [SLOTS, D])
        constants(nc, G, w["x"])
        with ExitStack() as layer:
            G.Q = layer.enter_context(nc.sbuf_tensor("Q0", [P, DC, N_TOK], F32))
            with nc.sbuf_tensor("rec", [P, EJ, REC], F32) as G.rec, \
                    nc.sbuf_tensor("rec_place", [P, EJ], I32) as G.rec_place:
                sort_edges(nc, G, w)
                linear_attention_scan(nc, G, w)
            G.BIAS = layer.enter_context(nc.sbuf_tensor("BIAS", [P, BUCKETS * BCOLS], F32))
            build_graph(nc, G)
            graph_attention(nc, G, w)
        if 2 in phases:
            route(nc, G, w, "A_", False)
            experts(nc, G, w, "A_", 1024)
            combine(nc, G, w, "A_", None)
        if 3 in phases:
            with nc.sbuf_tensor("Y1", [P, NT, D], F32) as G.Y1, nc.sbuf_tensor("Y2", [P, NT, D], F32) as G.Y2, \
                    nc.sbuf_tensor("adj", [P, BUCKETS * ACOLS], U16) as G.adj:
                G.adj3 = G.adj[:, :].rearrange("p (b n) -> p b n", n=ACOLS)
                neighbour_products(nc, G, w)
                neighbour_mean(nc, G)
            with nc.sbuf_tensor("M1", [P, PAIRS, D], F32) as G.M, nc.sbuf_tensor("Q1", [P, DC, N_TOK], F32) as G.Q, \
                    nc.sbuf_tensor("flow", [HEADS, N_TOK], F32) as G.flow, \
                    nc.sbuf_tensor("sel", [P, DC, HEADS], F32) as G.sel, \
                    nc.sbuf_tensor("rep", [HEADS, DC, P], F32) as G.rep:
                head_rows(nc, G)
                with nc.sbuf_tensor("K", [P, DC, N_TOK], F32) as G.K, nc.sbuf_tensor("V", [P, NT, D], F32) as G.V, \
                        nc.sbuf_tensor("qksum", [P, 2, DC], F32) as G.qksum:
                    flow_projections(nc, G, w)
                    flow_scan(nc, G, w)
                flow_output(nc, G, w)
        if 4 in phases:
            route(nc, G, w, "B_", True)
            experts(nc, G, w, "B_", 256)
            combine(nc, G, w, "B_", out)
        elif phases:
            with nc.semaphore("dbg") as s_, nc.Block() as blk:
                @blk.sync
                def _(sp):
                    sp.dma_start(out.rearrange("(t p) d -> p t d", p=P), G.X[:, :, :]).then_inc(s_, 16)
                    sp.wait_ge(s_, 16)



def layouts(inputs):
    import numpy as np

    def chunks(b):
        return b.reshape(-1, P).T

    a = {k: np.asarray(v) for k, v in inputs.items()}
    wqkv = a["L0_mix_w_qkv"]
    out = {"x": a["x"], "src": a["src"], "dst": a["dst"], "edge_attr": a["edge_attr_16"],
           "We": a["L0_gnn_We"], "be": a["L0_gnn_be"],
           "mix_wq": wqkv[:D].T, "mix_wk": wqkv[D:2 * D].T, "mix_wv": wqkv[2 * D:].T,
           "mix_wo": a["L0_mix_w_out"].T, "b_out": a["L0_mix_b_out"],
           "bq": chunks(a["L0_gnn_bq"]), "bk": chunks(a["L0_gnn_bk"]), "gw": a["L1_gnn_w"].T}
    for n in ("Wq", "Wk", "Wv", "Wo", "bv", "bo"):
        out[n] = a["L0_gnn_" + n]
    for n in ("Wq", "Wk", "Wv", "Wo", "W1", "W2", "bv", "bo", "b2"):
        out["F_" + n] = a["L1_mix_" + n]
    for n in ("bq", "bk", "b1"):
        out["F_" + n] = chunks(a["L1_mix_" + n])
    for n in ("g1", "be1", "g2", "be2"):
        out[n] = chunks(a["L1_mix_" + n])

    def moe(pre, w1, b1, w2, b2, wr, br):
        E, _, F = w1.shape
        out[pre + "W1"] = w1.reshape(E, DC, P, F).transpose(0, 2, 1, 3).reshape(E * P, DC * F)
        out[pre + "W2"] = w2.reshape(E, F // P, P, D).transpose(0, 2, 1, 3).reshape(E * P, F // P * D)
        out[pre + "b1"] = b1.reshape(E, F // P, P).transpose(0, 2, 1).reshape(E * P, F // P)
        out[pre + "b2"], out[pre + "Wr"], out[pre + "br"] = b2, wr.T, br

    moe("A_", *(a["L0_ffn_" + n] for n in ("W1", "b1", "W2", "b2", "Wr", "br")))
    moe("B_", a["L1_ffn_rw1"].transpose(0, 2, 1), a["L1_ffn_rb1"], a["L1_ffn_rw2"].transpose(0, 2, 1),
        a["L1_ffn_rb2"], a["L1_ffn_gate_w"], a["L1_ffn_gate_b"])
    out["sw1"] = a["L1_ffn_sw1"].transpose(2, 0, 1).reshape(D, -1)
    out["sw2"] = a["L1_ffn_sw2"].transpose(0, 2, 1).reshape(-1, D)
    out["sb1"], out["sb2"] = chunks(a["L1_ffn_sb1"].reshape(-1)), a["L1_ffn_sb2"]
    return {k: np.ascontiguousarray(v) for k, v in out.items()}


def kernel(**inputs):
    import concourse.bacc as _bacc
    from concourse.bass_utils import run_bass_kernel_spmd as _run

    nc = _bacc.Bacc("TRN2", target_bir_lowering=False, num_devices=1)
    arrays = layouts(inputs)
    w = {k: nc.dram_tensor("in_" + k, v.shape, mybir.dt.from_np(v.dtype), kind="ExternalInput").ap()
         for k, v in arrays.items()}
    out = nc.dram_tensor("out", (N_TOK, D), F32, kind="ExternalOutput").ap()
    program(nc, w, out)
    r = _run(nc, [{"in_" + k: v for k, v in arrays.items()}], core_ids=[0])
    return r.results[0]["out"]
```

```python
from contextlib import ExitStack

import concourse.bass as bass
from concourse import mybir

F32 = mybir.dt.float32
F32R = mybir.dt.float32r
BF16 = mybir.dt.bfloat16
F16 = mybir.dt.float16
I32 = mybir.dt.int32
U32 = mybir.dt.uint32
U16 = mybir.dt.uint16
ALU = mybir.AluOpType
ACT = mybir.ActivationFunctionType
AX = mybir.AxisListType

P = 128
N_TOK = 2048
D = 512
DC = D // P
NT = N_TOK // P
BLK = 256
NB = N_TOK // BLK
HEADS = 8
DH = D // HEADS
PAIRS = HEADS // 2
GRAPH = 64
E_EDGES = 32768
EJ = E_EDGES // P
ED = 16
LN_EPS = 1e-5
FLOW_EPS = 1e-6

BUCKETS = NT * 4
GROUP = 256
NG = 192
NCH = 2 * NG
REC = 12
ACOLS = (N_TOK // GRAPH) * 16
BCOLS = 16 * HEADS

EXPERTS = 8
TOPK = 2
SLOT_TILE = 256
NST = (N_TOK * TOPK) // SLOT_TILE + EXPERTS - 1
SLOTS = NST * SLOT_TILE


class Step:

    def __init__(self, eng, sem, t, k):
        self.eng, self.sem, self.base, self.k, self.n = eng, sem, t * k, k, 0

    def did(self, ins):
        ins.then_inc(self.sem, 1)
        self.n += 1
        assert self.n <= self.k

    def wait(self):
        self.eng.wait_ge(self.sem, self.base + self.n + BASE)

    def do(self, ins):
        self.did(ins)
        self.wait()


def loop(eng, n, body, unroll=2, peel=0, head=0, done_steps=0):
    full = (n - peel) // unroll
    for t in range(done_steps, head):
        body(t, t % unroll)
    with eng.Fori(head // unroll, full) as i:
        for u in range(unroll):
            body(i * unroll + u, u)
    for t in range(full * unroll, n):
        body(t, t % unroll)


LEAD = 1

BASE = 1


def lead(eng, sem, k=1):
    eng.sem_inc(sem, LEAD * k)


def done(t, k=1):
    return (t + 1 + LEAD) * k


def reuse(t, k=1):
    return (t - 1 + LEAD) * k


def gate(eng, sem, value, passed):
    eng.wait_ge(sem, value + BASE)
    eng.sem_inc(passed, 1)


def is_last(t, n):
    return isinstance(t, int) and t == n - 1


class Phase:

    def __init__(self, nc, name):
        self.nc, self.name, self.ctx = nc, name, ExitStack()
        self.used, self.counted = [], []

    def __enter__(self):
        self.ctx.__enter__()
        return self

    def __exit__(self, *a):
        self.ctx.__exit__(*a)
        if a[0] is None:
            self.nc.clear_and_free_semaphores(self.used)

    def sb(self, name, shape, dt=F32):
        return self.ctx.enter_context(self.nc.sbuf_tensor(f"{self.name}_{name}", shape, dt))

    def ps(self, name, shape, dt=F32):
        return self.ctx.enter_context(self.nc.psum_tensor(f"{self.name}_{name}", shape, dt))

    def sem(self, name):
        self.used.append(self.nc.alloc_semaphore(name=f"{self.name}_{name}"))
        if not name.startswith("sw_"):
            self.counted.append(self.used[-1])
        return self.used[-1]

    def sems(self, *names):
        return [self.sem(n) for n in names]

    def block(self):
        for sem in self.counted:
            self.nc.gpsimd.sem_inc(sem, BASE)
        self.nc.all_engine_barrier()
        return self.ctx.enter_context(self.nc.Block())


def constants(nc, G):
    with Phase(nc, "const") as ph:
        raw, made, mask_zero = ph.sems("raw", "made", "mask_zero")
        block = ph.block()

        @block.vector
        def _(dve):
            dve.memset(G.headmask[:, :], 0.0).then_inc(mask_zero, 1)
            dve.wait_ge(mask_zero, 1 + BASE)
            dve.memset(G.headmask[0:DH, 0:DH], 1.0)
            dve.memset(G.headmask[DH:P, DH:P], 1.0)

        @block.gpsimd
        def _(pool):
            pool.memset(G.ident[:, :], 0.0).then_inc(raw, 1)
            pool.memset(G.upper[:, :], 1.0).then_inc(raw, 1)
            pool.memset(G.ones[:, :], 1.0).then_inc(raw, 1)
            pool.memset(G.minus_half[:, :], -0.5).then_inc(raw, 1)
            pool.wait_ge(raw, 4 + BASE)
            pool.affine_select(out=G.ident[:, :], in_=G.ident[:, :], compare_op=ALU.not_equal, fill=1.0, base=0,
                               pattern=[[-1, P]], channel_multiplier=1).then_inc(made, 1)
            pool.affine_select(out=G.upper[:, :], in_=G.upper[:, :], compare_op=ALU.is_gt, fill=0.0, base=0,
                               pattern=[[1, P]], channel_multiplier=-1).then_inc(made, 1)
            pool.iota(G.iota512[:, :], pattern=[[1, ACOLS]], base=0, channel_multiplier=0,
                      allow_small_or_imprecise_dtypes=True).then_inc(made, 1)
            pool.iota(G.part[:, :], pattern=[[0, 1]], base=0, channel_multiplier=1,
                      allow_small_or_imprecise_dtypes=True).then_inc(made, 1)
            pool.wait_ge(made, 4 + BASE)


def head_rows(nc, G):
    with Phase(nc, "heads") as ph:
        sel_zero, sel_ready, rep_done, rep_ready = ph.sems("sel_zero", "sel_ready", "rep_done", "rep_ready")
        psR = ph.ps("psR", [HEADS, DC, P])
        block = ph.block()

        @block.vector
        def _(dve):
            dve.memset(G.sel[:, :, :], 0.0).then_inc(sel_zero, 1)
            dve.wait_ge(sel_zero, 1 + BASE)
            for h in range(HEADS):
                dve.memset(G.sel[DH * (h % 2):DH * (h % 2 + 1), h // 2, h:h + 1], 1.0).then_inc(sel_ready, 1)
            dve.wait_ge(rep_done, 1 + BASE)
            dve.tensor_copy(G.rep[:, :, :], psR[:, :, :]).then_inc(rep_ready, 1)

        @block.tensor
        def _(pe):
            pe.wait_ge(sel_ready, HEADS + BASE)
            for c in range(DC):
                mm = pe.transpose(psR[:, c], G.sel[:, c], G.ident[:, :])
            mm.then_inc(rep_done, 1)


def ln_stats_buffers(ph):
    s = type("LnStats", (), {})()
    s.mean = ph.sb("ln_mean", [P, NT])
    s.diff = ph.sb("ln_diff", [P, NT])
    s.m2 = ph.sb("ln_m2", [P, NT])
    s.var = ph.sb("ln_var", [P, NT])
    s.rstd = ph.sb("ln_rstd", [P, NT])
    s.shift = ph.sb("ln_shift", [P, NT])
    s.part_done, s.var_ready, s.rstd_ready, s.ready = ph.sems("ln_part", "ln_var", "ln_rstd", "ln_ready")
    return s


def tile_stats(dve, G, t):
    return dve.bn_stats(G.bn[:, bass.ds(t, 1), :].rearrange("p a s -> p (a s)"), token_tile(G.X, t))


def ln_stats_vector(dve, s, bn):
    st = Step(dve, s.part_done, 0, 8)
    st.did(dve.tensor_tensor(s.mean[:, :], bn[:, :, 1], bn[:, :, 4], ALU.add))
    st.did(dve.tensor_tensor(s.diff[:, :], bn[:, :, 1], bn[:, :, 4], ALU.subtract))
    st.did(dve.tensor_tensor(s.m2[:, :], bn[:, :, 2], bn[:, :, 5], ALU.add))
    st.wait()
    st.did(dve.tensor_scalar(s.mean[:, :], s.mean[:, :], 0.5, None, ALU.mult))
    st.did(dve.tensor_tensor(s.diff[:, :], s.diff[:, :], s.diff[:, :], ALU.mult))
    st.did(dve.tensor_scalar(s.m2[:, :], s.m2[:, :], 1.0 / D, LN_EPS, ALU.mult, ALU.add))
    st.wait()
    dve.scalar_tensor_tensor(out=s.var[:, :], in0=s.diff[:, :], scalar=0.25, in1=s.m2[:, :],
                             op0=ALU.mult, op1=ALU.add).then_inc(s.var_ready, 1)
    dve.wait_ge(s.rstd_ready, 1 + BASE)
    dve.scalar_tensor_tensor(out=s.shift[:, :], in0=s.mean[:, :], scalar=-1.0, in1=s.rstd[:, :],
                             op0=ALU.mult, op1=ALU.mult).then_inc(s.ready, 1)
    dve.wait_ge(s.ready, 1 + BASE)


def ln_stats_pool(pool, s, G):
    pool.wait_ge(s.var_ready, 1 + BASE)
    pool.tensor_tensor(s.rstd[:, :], s.var[:, :], G.minus_half[:, :], ALU.pow).then_inc(s.rstd_ready, 1)


def token_tile(X, t):
    return X[:, bass.ds(t, 1), :].rearrange("p a d -> p (a d)")


def col(ap2d, t):
    return ap2d[:, bass.ds(t, 1)]


def bucket_groups(ph, nb, group, n_groups, end, past):
    s = type("Groups", (), {})()
    s.nb, s.group, s.n_groups, s.end, s.past = nb, group, n_groups, end, past
    s.group_at = ph.sb("group_at", [P, n_groups])
    s.bucket = ph.sb("bucket", [P, n_groups])
    s.numbered = ph.sem("numbered")
    return s


def bucket_starts(ph, nb, group):
    s = type("Buckets", (), {})()
    s.nb, s.group = nb, group
    s.count = ph.sb("count", [P, nb])
    s.before = ph.sb("before", [P, nb])
    s.total = ph.sb("total", [P, nb], I32)
    s.padded = ph.sb("padded", [P, nb])
    s.end = ph.sb("end", [P, nb])
    s.first = ph.sb("first", [P, nb])
    s.ps = ph.ps("ps_count", [P, 2, nb])
    s.counted, s.summed, s.step = ph.sems("counted", "summed", "bucket_step")
    return s


def bucket_groups_pool(pool, s):
    pool.iota(s.group_at[:, :], pattern=[[s.group, s.n_groups]], base=0, channel_multiplier=0,
              allow_small_or_imprecise_dtypes=True).then_inc(s.numbered, 1)


def bucket_groups_vector(dve, s, st):
    dve.wait_ge(s.numbered, 1 + BASE)
    st.do(dve.tensor_tensor(s.past[:, :, :], s.group_at[:, :].unsqueeze(2).to_broadcast([P, s.n_groups, s.nb]),
                            s.end[:, :].unsqueeze(1).to_broadcast([P, s.n_groups, s.nb]), ALU.is_ge))
    st.do(dve.tensor_reduce(s.bucket[:, :], s.past[:, :, :], AX.X, ALU.add))
    st.do(dve.tensor_scalar(s.bucket[:, :], s.bucket[:, :], float(s.nb - 1), None, ALU.min))


def bucket_starts_tensor(pe, s, G, n_counts):
    pe.wait_ge(s.counted, n_counts + BASE)
    pe.matmul(s.ps[:, 0], G.upper[:, :], s.count[:, :], start=True, stop=True)
    pe.matmul(s.ps[:, 1], G.ones[:, :], s.count[:, :], start=True, stop=True).then_inc(s.summed, 1)


def bucket_starts_vector(dve, s):
    st = Step(dve, s.step, 0, 16)
    shift = s.group.bit_length() - 1
    dve.wait_ge(s.summed, 1 + BASE)
    st.did(dve.tensor_scalar(s.total[:, :], s.ps[:, 1], float(s.group - 1), None, ALU.add))
    st.do(dve.tensor_copy(s.before[:, :], s.ps[:, 0]))
    st.do(dve.tensor_scalar(s.total[:, :], s.total[:, :], shift, shift, ALU.logical_shift_right,
                            ALU.logical_shift_left))
    st.do(dve.tensor_copy(s.padded[:, :], s.total[:, :]))
    st.do(dve.tensor_tensor_scan(s.end[:, :], s.padded[:, :], s.padded[:, :], 0.0, ALU.add, ALU.bypass))
    st.do(dve.tensor_tensor(s.first[:, :], s.end[:, :], s.padded[:, :], ALU.subtract))
    st.did(dve.scalar_tensor_tensor(out=s.first[:, :], in0=s.first[:, :], scalar=-1.0, in1=s.before[:, :],
                                    op0=ALU.add, op1=ALU.add))
    st.wait()


def sort_edges(nc, G, w):
    HALF = BUCKETS // 2
    with Phase(nc, "sort") as ph:
        src = ph.sb("src", [P, EJ], I32)
        dst = ph.sb("dst", [P, EJ], I32)
        attr = ph.sb("attr", [P, EJ * ED])
        we = ph.sb("we", [P, 8 * HEADS])
        be = ph.sb("be", [P, HEADS])
        attrT = ph.sb("attrT", [P, 2, 4, P])
        rec, place = G.rec, G.rec_place
        zero = ph.sb("zero", [P, 2 * D])
        ka = ph.sb("ka", [P, EJ], I32)
        kb = ph.sb("kb", [P, EJ], I32)
        key = ph.sb("key", [P, EJ], BF16)
        onehot = ph.sb("onehot", [P, BUCKETS, EJ], BF16)
        rank = ph.sb("rank", [P, BUCKETS, EJ])
        slot = ph.sb("slot", [P, 2, EJ])
        blank = ph.sb("blank", [P, NCH * REC // 4])
        bs = bucket_starts(ph, BUCKETS, GROUP)
        psA = ph.ps("psA", [P, 2, 4, P])
        psE = ph.ps("psE", [P, EJ // 64, 64, HEADS])
        (e_in, a_in, w_in, we_zero, blank_ready, blanked, key_step, ranked, slotted,
         a_done, a_ready, e_done, rec_ready, zero_ready, cleared, x_in, weighed) = ph.sems(
            "e_in", "a_in", "w_in", "we_zero", "blank_ready", "blanked", "key_step", "ranked", "slotted",
            "a_done", "a_ready", "e_done", "rec_ready", "zero_ready", "cleared", "x_in", "weighed")
        block = ph.block()
        n_batches = EJ // 64

        @block.sync
        def _(sp):
            sp.dma_start(src[:, :], w["src"].rearrange("(p j) -> p j", p=P)).then_inc(e_in, 16)
            sp.dma_start(dst[:, :], w["dst"].rearrange("(p j) -> p j", p=P)).then_inc(e_in, 16)
            sp.dma_start(attr[:, :], w["edge_attr"].rearrange("(p j) f -> p (j f)", p=P)).then_inc(a_in, 16)
            sp.dma_start(be[:, :], w["be"].partition_broadcast(P)).then_inc(w_in, 16)
            sp.wait_ge(we_zero, 1 + BASE)
            for k in range(8):
                sp.dma_start(we[k * ED:(k + 1) * ED, k * HEADS:(k + 1) * HEADS], w["We"]).then_inc(w_in, 16)
            sp.wait_ge(blank_ready, 1 + BASE)
            for k in range(4):
                n = NCH * REC // 4
                sp.dma_start(G.rec_dram.rearrange("(p c) r -> p (c r)", p=P)[:, k * n:(k + 1) * n],
                             blank[:, :]).then_inc(blanked, 16)
            sp.wait_ge(zero_ready, 1 + BASE)
            for g in range(NST):
                sp.dma_start(G.xs_dram.rearrange("(n p j) d -> p n (j d)", p=P, j=2)[:, g, :],
                             zero[:, :]).then_inc(cleared, 16)
            sp.dma_start(G.X[:, :, :], w["x"].rearrange("(t p) d -> p t d", p=P)).then_inc(x_in, 16)
            sp.wait_ge(blanked, 64 + BASE)
            sp.wait_ge(cleared, 16 * NST + BASE)
            sp.wait_ge(x_in, 16 + BASE)

        @block.gpsimd
        def _(pool):
            pool.memset(we[:, :], 0.0).then_inc(we_zero, 1)
            pool.memset(blank[:, :], -1.0).then_inc(blank_ready, 1)
            pool.memset(zero[:, :], 0.0).then_inc(zero_ready, 1)
            pool.wait_ge(ranked, HALF + BASE)
            pool.tensor_tensor(rank[:, 0:HALF], rank[:, 0:HALF], onehot[:, 0:HALF], ALU.mult).then_inc(weighed, 1)
            pool.wait_ge(weighed, 1 + BASE)
            pool.tensor_tensor(rank[:, 0:HALF // 2], rank[:, 0:HALF // 2], rank[:, HALF // 2:HALF],
                               ALU.add).then_inc(weighed, 1)

        @block.vector
        def _(dve):
            st = Step(dve, key_step, 0, 16)
            dve.wait_ge(e_in, 32 + BASE)
            st.did(dve.tensor_scalar(ka[:, :], src[:, :], 7, 2, ALU.logical_shift_right, ALU.logical_shift_left))
            st.do(dve.tensor_scalar(kb[:, :], dst[:, :], 4, 3, ALU.logical_shift_right, ALU.bitwise_and))
            st.do(dve.tensor_tensor(key[:, :], ka[:, :], kb[:, :], ALU.add))
            st.do(dve.tensor_scalar(ka[:, :], dst[:, :], 6, 4, ALU.logical_shift_right, ALU.logical_shift_left))
            st.do(dve.tensor_scalar(kb[:, :], dst[:, :], 15, None, ALU.bitwise_and))
            st.did(dve.tensor_tensor(rec[:, :, 9], ka[:, :], kb[:, :], ALU.add))
            st.do(dve.tensor_copy(rec[:, :, 10], kb[:, :]))
            st.do(dve.tensor_scalar(src[:, :], src[:, :], P - 1, None, ALU.bitwise_and))
            st.did(dve.tensor_copy(rec[:, :, 8], src[:, :]))
            st.do(dve.memset(rec[:, :, 11:REC], 0.0))

            def member(b, u):
                dve.tensor_scalar(onehot[:, bass.ds(b, 1), :].rearrange("p a j -> p (a j)"), key[:, :],
                                  col(G.iota512, b), 0.0, ALU.is_equal, ALU.add,
                                  accum_out=col(bs.count, b)).then_inc(bs.counted, 1)
            loop(dve, BUCKETS, member, 4)
            bucket_starts_vector(dve, bs)

            sl = Step(dve, slotted, 0, 12)
            sl.did(dve.tensor_copy(G.edge_end[:, :], bs.end[:, :]))

            def number(b, u):
                hot = onehot[:, bass.ds(b, 1), :].rearrange("p a j -> p (a j)")
                dve.tensor_tensor_scan(rank[:, bass.ds(b, 1), :].rearrange("p a j -> p (a j)"), hot, hot,
                                       col(bs.first, b), ALU.add, ALU.bypass).then_inc(ranked, 1)
            loop(dve, BUCKETS, number, 4)
            for n in range(n_batches):
                dve.wait_ge(e_done, 2 * n + 2 + BASE)
                dve.tensor_tensor(rec[:, n * 64:(n + 1) * 64, 0:HEADS], psE[:, n],
                                  be[:, :].unsqueeze(1).to_broadcast([P, 64, HEADS]), ALU.add).then_inc(rec_ready, 1)
            dve.wait_ge(ranked, BUCKETS + BASE)
            sl.do(dve.tensor_tensor(rank[:, HALF:], rank[:, HALF:], onehot[:, HALF:], ALU.mult))
            sl.do(dve.tensor_reduce(slot[:, 0], rank[:, HALF:].rearrange("p b j -> p j b"), AX.X, ALU.add))
            dve.wait_ge(weighed, 2 + BASE)
            sl.do(dve.tensor_reduce(slot[:, 1], rank[:, 0:HALF // 2].rearrange("p b j -> p j b"), AX.X, ALU.add))
            sl.do(dve.tensor_tensor(slot[:, 0], slot[:, 0], slot[:, 1], ALU.add))
            sl.do(dve.tensor_copy(ka[:, :], slot[:, 0]))
            sl.did(dve.tensor_scalar(kb[:, :], ka[:, :], 7, None, ALU.logical_shift_right))
            sl.do(dve.tensor_scalar(ka[:, :], ka[:, :], P - 1, None, ALU.bitwise_and))
            sl.did(dve.scalar_tensor_tensor(out=place[:, :], in0=ka[:, :], scalar=float(NCH), in1=kb[:, :],
                                            op0=ALU.mult, op1=ALU.add))
            sl.wait()

        @block.scalar
        def _(act):
            for n in range(2 * n_batches):
                act.wait_ge(a_done, n + 1 + BASE)
                if n >= 2:
                    act.wait_ge(e_done, n - 1 + BASE)
                act.activation(attrT[:, n % 2], psA[:, n % 2], ACT.Copy).then_inc(a_ready, 1)

        @block.tensor
        def _(pe):
            pe.wait_ge(a_in, 16 + BASE)
            pe.wait_ge(w_in, 16 * 9 + BASE)
            for n in range(2 * n_batches):
                if n >= 2:
                    pe.wait_ge(a_ready, n - 1 + BASE)
                for k in range(4):
                    g = 4 * n + k
                    mm = pe.transpose(psA[:, n % 2, k], attr[:, g * P:(g + 1) * P], G.ident[:, :])
                mm.then_inc(a_done, 1)
                pe.wait_ge(a_ready, n + 1 + BASE)
                for k in range(4):
                    g = 4 * (n % 2) + k
                    mm = pe.matmul(psE[:, n // 2, g * 8:(g + 1) * 8].rearrange("p j h -> p (j h)"),
                                   attrT[:, n % 2, k], we[:, :], start=True, stop=True)
                mm.then_inc(e_done, 1)
            bucket_starts_tensor(pe, bs, G, BUCKETS)


class AttentionWeights:

    def __init__(self, nc, ctx):
        def sb(name, shape):
            return ctx.enter_context(nc.sbuf_tensor(f"attn_{name}", shape, F32))
        self.wq, self.wk, self.wv, self.wo = (sb(n, [P, DC, D]) for n in ("wq", "wk", "wv", "wo"))
        self.bq, self.bk = (sb(n, [P, DC]) for n in ("bq", "bk"))
        self.bv, self.bo, self.bsum = (sb(n, [P, D]) for n in ("bv", "bo", "bsum"))
        self.M = sb("M", [P, PAIRS, D])
        self.xnT = sb("xnT", [P, DC, BLK])
        self.loads = 11

    def load(self, eng, G, w, weights_in):
        for dst, name in ((self.bq, "bq"), (self.bk, "bk")):
            eng.dma_start(dst[:, :], w[name]).then_inc(weights_in, 16)
        for dst, name in ((self.bv, "bv"), (self.bo, "bo"), (self.bsum, "b_out")):
            eng.dma_start(dst[:, :], w[name].partition_broadcast(P)).then_inc(weights_in, 16)
        for dst, name in ((self.wq, "Wq"), (self.wk, "Wk"), (self.wv, "Wv"), (self.wo, "Wo")):
            eng.dma_start(dst[:, :, :], w[name].rearrange("(c p) n -> p c n", p=P)).then_inc(weights_in, 16)
        eng.dma_start(self.M[:, :, :].rearrange("p c n -> p (c n)"), G.m_dram).then_inc(weights_in, 16)
        eng.dma_start(self.xnT[:, :, :].rearrange("p c n -> p (c n)"),
                      G.xnT_dram[:, 0:DC * BLK]).then_inc(weights_in, 16)


def build_graph(nc, G, w, W):
    RING = 4
    AHEAD = 2
    BATCH = 4
    UNROLL = 2 * BATCH
    CH = 2 * BATCH
    n_batches = NG // BATCH
    with Phase(nc, "graph") as ph:
        rec = ph.sb("rec", [P, 2, CH, REC])
        bucket = ph.sb("bucket", [1, 2, BATCH], I32)
        adj = ph.sb("adj", [P, BUCKETS * ACOLS], U16)
        far = ph.sb("far", [P, 2, 2, P])
        row = ph.sb("row", [P, RING, 2, P])
        row16 = ph.sb("row16", [P, RING, 2, P], F16)
        number16 = ph.sb("number16", [P, ACOLS], F16)
        cols = ph.sb("cols", [P, RING, 2, ACOLS], F16)
        hot = ph.sb("hot", [P, 2, CH, 16], F16)
        bias = ph.sb("bias", [P, RING, 2, 16, HEADS])
        sums = ph.sb("sums", [P, 2, BCOLS])
        psA = [ph.ps(f"psA{u}", [P, ACOLS]) for u in range(RING)]
        psB = [ph.ps(f"psB{u}", [P, D]) for u in range(2)]
        names = ("rec_in0 rec_in1 bias_zero adj_zero numbered hot_ready bucket_ready far_ready row_ready "
                 "row16_even row16_odd cols_ready bias_ready g_done adj_added sums_out bias_added adj_out "
                 "weights_in passed passed_dve").split()
        S = type("Sems", (), dict(zip(names, ph.sems(*names))))
        rec_in = (S.rec_in0, S.rec_in1)
        block = ph.block()
        half = BUCKETS * ACOLS // 2

        def group_done(g):
            return g + 1 + UNROLL

        def ahead(eng, make, finish):
            def body(g, k):
                if not (isinstance(g, int) and g + AHEAD >= NG):
                    make(g + AHEAD, (k + AHEAD) % UNROLL)
                finish(g, k)
            for g in range(AHEAD):
                make(g, g)
            loop(eng, NG, body, UNROLL, peel=UNROLL)

        @block.sync
        def _(sp):
            def load(m, u):
                sp.wait_ge(S.g_done, group_done(m * BATCH - BATCH - 1) + BASE)
                sp.dma_start(rec[:, u].rearrange("p c r -> p (c r)"),
                             G.rec_dram.rearrange("(p c) r -> p (c r)", p=P)[:, bass.ds(m * CH * REC, CH * REC)]
                             ).then_inc(rec_in[u], 16)
            for m in range(2):
                load(m, m)
            W.load(sp, G, w, S.weights_in)
            loop(sp, n_batches, load, head=2, done_steps=2)
            sp.wait_ge(S.adj_added, group_done(NG - 1) + BASE)
            sp.dma_start(G.adj_dram, adj[:, :]).then_inc(S.adj_out, 16)
            sp.wait_ge(S.weights_in, 16 * W.loads + BASE)
            sp.wait_ge(S.adj_out, 16 + BASE)

        def batch_in(eng, g, k):
            if k % BATCH == 0:
                eng.wait_ge(rec_in[k // BATCH], (g - k) * 2 + 16 + BASE)

        @block.gpsimd
        def _(pool):
            pool.memset(adj[:, half:].bitcast(U32), 0).then_inc(S.adj_zero, 1)
            pool.memset(G.BIAS[:, :], 0.0).then_inc(S.bias_zero, 1)
            lead(pool, S.bias_added, UNROLL)
            pool.wait_ge(S.bias_zero, 1 + BASE)

            def weigh(g, k):
                u, c, n = k // BATCH, 2 * (k % BATCH), k % RING
                if k % BATCH == 0:
                    gate(pool, S.hot_ready, g + BATCH, S.passed)
                gate(pool, S.g_done, group_done(g - RING), S.passed)
                pool.tensor_tensor(bias[:, n], hot[:, u, c:c + 2].unsqueeze(3).to_broadcast([P, 2, 16, HEADS]),
                                   rec[:, u, c:c + 2, 0:HEADS].unsqueeze(2).to_broadcast([P, 2, 16, HEADS]),
                                   ALU.mult).then_inc(S.bias_ready, 1)

            def add(g, k):
                if k % BATCH == 0:
                    gate(pool, S.bucket_ready, g + BATCH, S.passed)
                b = pool.value_load(bucket[0:1, k // BATCH, k % BATCH:k % BATCH + 1], min_val=0, max_val=BUCKETS - 1)
                a = G.BIAS[:, bass.ds(b * BCOLS, BCOLS)]
                gate(pool, S.bias_added, group_done(g - 1), S.passed)
                gate(pool, S.sums_out, done(g), S.passed)
                pool.tensor_tensor(a, a, sums[:, k % 2], ALU.add).then_inc(S.bias_added, 1)
            ahead(pool, weigh, add)

        @block.scalar
        def _(act):
            lead(act, S.row_ready)
            lead(act, S.sums_out)

            def rows(g, k):
                u, c = k // BATCH, 2 * (k % BATCH)
                batch_in(act, g, k)
                act.wait_ge(S.row_ready, reuse(g) + BASE)
                for i in range(2):
                    act.activation(far[:, k % 2, i], G.iota512[:, 0:P], ACT.Abs, scale=-1.0,
                                   bias=rec[:, u, c + i, 8:9]).then_inc(S.far_ready, 1)
                act.wait_ge(S.far_ready, g * 2 + 2 + BASE)
                act.wait_ge(S.g_done, group_done(g - RING) + BASE)
                if k % 2:
                    act.activation(row16[:, k % RING], far[:, k % 2], ACT.Relu, scale=-1.0, bias=1.0
                                   ).then_inc(S.row16_odd, 2)
                act.activation(row[:, k % RING], far[:, k % 2], ACT.Relu, scale=-1.0, bias=1.0).then_inc(S.row_ready, 1)

            def out(g, k):
                act.wait_ge(S.g_done, group_done(g) + BASE)
                act.wait_ge(S.bias_added, group_done(g - 2) + BASE)
                act.activation(sums[:, k % 2], psB[k % 2][:, 0:BCOLS], ACT.Copy).then_inc(S.sums_out, 1)
            ahead(act, rows, out)

        @block.vector
        def _(dve):
            dve.tensor_copy(number16[:, :], G.iota512[:, :]).then_inc(S.numbered, 1)
            dve.memset(adj[:, 0:half].bitcast(U32), 0).then_inc(S.adj_zero, 1)
            dve.wait_ge(S.numbered, 1 + BASE)
            dve.wait_ge(S.adj_zero, 2 + BASE)
            lead(dve, S.adj_added, UNROLL)

            def columns(g, k):
                u, c, n = k // BATCH, 2 * (k % BATCH), k % RING
                batch_in(dve, g, k)
                dve.wait_ge(S.g_done, group_done(g - RING) + BASE)
                if k % BATCH == 0:
                    dve.wait_ge(S.bias_added, group_done(g - BATCH - 1) + BASE)
                    dve.tensor_copy(bucket[:, u], G.edge_bucket[0:1, bass.ds(g, BATCH)]).then_inc(S.bucket_ready, BATCH)
                    dve.tensor_tensor(hot[:, u], rec[:, u, :, 10:11].to_broadcast([P, CH, 16]),
                                      number16[:, 0:16].unsqueeze(1).to_broadcast([P, CH, 16]),
                                      ALU.is_equal).then_inc(S.hot_ready, BATCH)
                for i in range(2):
                    dve.tensor_scalar(cols[:, n, i], number16[:, :], rec[:, u, c + i, 9:10], None,
                                      ALU.is_equal).then_inc(S.cols_ready, 1)
                    if k % 2 == 0:
                        dve.tensor_scalar(row16[:, n, i], number16[:, 0:P], rec[:, u, c + i, 8:9], None,
                                          ALU.is_equal).then_inc(S.row16_even, 1)

            def add(g, k):
                if k % BATCH == 0:
                    gate(dve, S.bucket_ready, g + BATCH, S.passed_dve)
                b = dve.value_load(bucket[0:1, k // BATCH, k % BATCH:k % BATCH + 1], min_val=0, max_val=BUCKETS - 1)
                dve.wait_ge(S.g_done, group_done(g) + BASE)
                a = adj[:, :].rearrange("p (t n) -> p t n", t=NT)[:, :, bass.ds(b * 32, 32)]
                dve.wait_ge(S.adj_added, group_done(g - 1) + BASE)
                dve.tensor_tensor(a, a, psA[k % RING][:, :].rearrange("p (t c) -> p t c", t=NT),
                                  ALU.add).then_inc(S.adj_added, 1)
            ahead(dve, columns, add)

        @block.tensor
        def _(pe):
            lead(pe, S.g_done, UNROLL)

            def body(g, k):
                n = k % RING
                pe.wait_ge(S.cols_ready, g * 2 + 2 + BASE)
                pe.wait_ge(*((S.row16_odd, g + 1 + BASE) if k % 2 else (S.row16_even, g + 2 + BASE)))
                pe.wait_ge(S.adj_added, group_done(g - RING) + BASE)
                for i in range(2):
                    pe.matmul(psA[n][:, :], row16[:, n, i], cols[:, n, i], start=(i == 0), stop=(i == 1))
                pe.wait_ge(S.sums_out, reuse(g) + BASE)
                pe.wait_ge(S.row_ready, done(g) + BASE)
                pe.wait_ge(S.bias_ready, g + 1 + BASE)
                for i in range(2):
                    mm = pe.matmul(psB[k % 2][:, 0:BCOLS], row[:, n, i], bias[:, n, i].rearrange("p r h -> p (r h)"),
                                   start=(i == 0), stop=(i == 1))
                mm.then_inc(S.g_done, 1)
            loop(pe, NG, body, UNROLL)


def linear_attention_scan(nc, G, w):
    SET = 8
    scale = DH ** -0.5
    with Phase(nc, "lin") as ph:
        G.Q = ph.sb("Q", [P, DC, N_TOK])
        wq, wk, wv, wo = (ph.sb(n, [P, DC, D]) for n in ("wq", "wk", "wv", "wo"))
        ln = ln_stats_buffers(ph)
        xn = ph.sb("xn", [P, 2, 2, D])
        xnT = ph.sb("xnT", [P, 2, DC, BLK])
        eq = ph.sb("eq", [P, DC, BLK])
        rq = ph.sb("rq", [P, DC, BLK])
        ek = ph.sb("ek", [P, D])
        rk = ph.sb("rk", [P, D])
        kf = ph.sb("kf", [P, 2, D])
        vf = ph.sb("vf", [P, 2, D])
        ctxT = ph.sb("ctxT", [P, PAIRS, P])
        ksum = ph.sb("ksum", [P, PAIRS])
        kmask = ph.sb("kmask", [P, PAIRS, P])
        den = ph.sb("den", [P, 2, D])
        psT = ph.ps("psT", [P, DC, BLK])
        psQ = ph.ps("psQ", [P, DC, BLK])
        psK = ph.ps("psK", [P, D])
        psV = ph.ps("psV", [P, D])
        psC = ph.ps("psC", [P, PAIRS, P])
        psS = ph.ps("psS", [P, PAIRS, 2])
        wq_in, wk_in, wv_in, wo_in = ph.sems("wq_in", "wk_in", "wv_in", "wo_in")
        xn_ready, t_done, xnT_ready = ph.sems("xn_ready", "t_done", "xnT_ready")
        q_done, q_exp, q_relu, q_ready = ph.sems("q_done", "q_exp", "q_relu", "q_ready")
        k_done, k_exp, k_relu, k_ready = ph.sems("k_done", "k_exp", "k_relu", "k_ready")
        v_done, v_ready, ctx_done = ph.sems("v_done", "v_ready", "ctx_done")
        ctx_zero, ctx_ready, kmask_ready, m_done, m_ready = ph.sems("ctx_zero", "ctx_ready", "kmask_ready", "m_done",
                                                                    "m_ready")
        d_done, d_eps, d_rec, d_used = ph.sems("d_done", "d_eps", "d_rec", "d_used")
        rec_now = ph.sb("rec_now", [P, 2, SET, REC])
        place_now = ph.sb("place_now", [P, 2, SET], I32)
        M = ph.sb("M", [P, PAIRS, D])
        rec_copied, passed, m_out, q_out, stats, edge_step = ph.sems("rec_copied", "passed", "m_out", "q_out", "stats",
                                                                          "edge_step")
        bg = bucket_groups(ph, BUCKETS, GROUP, NG, G.edge_end, ph.sb("past", [P, NG // NB, BUCKETS]))
        scattered = ph.sems("sw_scattered0", "sw_scattered1")
        spill = ph.sems("spill0", "spill1")
        block = ph.block()
        n_cols = N_TOK // D

        @block.sync
        def _(sp):
            for dst, name, sem in ((wq, "mix_wq", wq_in), (wk, "mix_wk", wk_in), (wv, "mix_wv", wv_in),
                                   (wo, "mix_wo", wo_in)):
                sp.dma_start(dst[:, :, :], w[name].rearrange("(c p) n -> p c n", p=P)).then_inc(sem, 16)

            def body(b, u):
                sp.wait_ge(xnT_ready, b + 1 + BASE)
                sp.dma_start(G.xnT_dram[:, bass.ds(b * DC * BLK, DC * BLK)],
                             xnT[:, u].rearrange("p c n -> p (c n)")).then_inc(spill[u], 16)
            loop(sp, NB, body)
            sp.wait_ge(m_ready, PAIRS + BASE)
            sp.dma_start(G.m_dram, M[:, :, :].rearrange("p c n -> p (c n)")).then_inc(m_out, 16)
            per = D // BLK
            for n in range(n_cols):
                sp.wait_ge(d_used, done(n * DC + DC - 1) + BASE)
                for b in range(n * per, (n + 1) * per):
                    sp.dma_start(G.q_dram[:, b * DC * BLK:(b + 1) * DC * BLK].rearrange("p (c n) -> p c n", c=DC),
                                 G.Q[:, :, b * BLK:(b + 1) * BLK]).then_inc(q_out, 16)
            for u in range(2):
                sp.wait_ge(spill[u], 16 * NB // 2 + BASE)
            sp.wait_ge(m_out, 16 + BASE)
            sp.wait_ge(q_out, 16 * NB + BASE)

        @block.gpsimd
        def _(pool):
            pool.memset(ctxT[:, :, :], 0.0).then_inc(ctx_zero, 1)
            bucket_groups_pool(pool, bg)
            lead(pool, rec_copied, 2)

            def scatter(n, u):
                if not (isinstance(n, int) and n < 2):
                    pool.wait_ge(scattered[u], (n - u) * SET * 8)
                    pool.sem_inc(passed, 1)
                pool.tensor_copy(place_now[:, u], G.rec_place[:, bass.ds(n * SET, SET)]).then_inc(rec_copied, 1)
                pool.tensor_copy(rec_now[:, u], G.rec[:, bass.ds(n * SET, SET), :]).then_inc(rec_copied, 1)
                gate(pool, rec_copied, done(n, 2), passed)
                for k in range(SET):
                    pool.indirect_dma_start(
                        out=G.rec_dram, out_offset=bass.IndirectOffsetOnAxis(ap=place_now[:, u, k:k + 1], axis=0),
                        in_=rec_now[:, u, k], in_offset=None).then_inc(scattered[u], 16)
            scatter(0, 0)
            ln_stats_pool(pool, ln, G)
            loop(pool, EJ // SET, scatter, head=2, done_steps=1)
            for u in range(2):
                pool.wait_ge(scattered[u], EJ // 2 * 16)

        @block.vector
        def _(dve):
            for t in range(NT):
                tile_stats(dve, G, t).then_inc(stats, 1)
            dve.wait_ge(stats, NT + BASE)
            ln_stats_vector(dve, ln, G.bn)

            def norm_block(b, u):
                dve.wait_ge(t_done, reuse(b) + BASE)
                for j in range(2):
                    t = b * 2 + j
                    dve.tensor_scalar(xn[:, u, j], token_tile(G.X, t), col(ln.rstd, t), col(ln.shift, t),
                                      ALU.mult, ALU.add).then_inc(xn_ready, 1)

            def body(b, u):
                if not is_last(b, NB):
                    norm_block(b + 1, 1 - u)
                dve.wait_ge(q_exp, b + 1 + BASE)
                dve.tensor_scalar(rq[:, :, :], psQ[:, :, :], 0.0, scale, ALU.max, ALU.mult).then_inc(q_relu, 1)
                dve.wait_ge(q_relu, b + 1 + BASE)
                dve.scalar_tensor_tensor(out=G.Q[:, :, bass.ds(b * BLK, BLK)], in0=eq[:, :, :], scalar=1.0,
                                         in1=rq[:, :, :], op0=ALU.min, op1=ALU.add).then_inc(q_ready, 1)
                n = NG // NB
                at = bg.group_at[:, bass.ds(b * n, n)].unsqueeze(2).to_broadcast([P, n, BUCKETS])
                dve.wait_ge(edge_step, b * 2 + BASE)
                dve.tensor_tensor(bg.past[:, :, :], at, G.edge_end[:, :].unsqueeze(1).to_broadcast([P, n, BUCKETS]),
                                  ALU.is_ge).then_inc(edge_step, 1)
                for j in range(2):
                    t = b * 2 + j
                    dve.wait_ge(k_exp, t + 1 + BASE)
                    dve.tensor_scalar(rk[:, :], psK[:, :], 0.0, None, ALU.max).then_inc(k_relu, 1)
                    dve.wait_ge(k_relu, t + 1 + BASE)
                    dve.wait_ge(ctx_done, reuse(t) + BASE)
                    dve.scalar_tensor_tensor(out=kf[:, j], in0=ek[:, :], scalar=1.0, in1=rk[:, :],
                                             op0=ALU.min, op1=ALU.add).then_inc(k_ready, 1)
                dve.wait_ge(edge_step, b * 2 + 1 + BASE)
                dve.tensor_reduce(bg.bucket[:, bass.ds(b * n, n)], bg.past[:, :, :], AX.X,
                                  ALU.add).then_inc(edge_step, 1)
            norm_block(0, 0)
            dve.wait_ge(bg.numbered, 1 + BASE)
            loop(dve, NB, body, peel=1)
            dve.wait_ge(ctx_done, done(NT - 1) + BASE)
            dve.wait_ge(ctx_zero, 1 + BASE)
            dve.tensor_copy(ctxT[0:DH, :, 0:DH], psC[0:DH, :, 0:DH]).then_inc(ctx_ready, 1)
            dve.tensor_copy(ctxT[DH:P, :, DH:P], psC[DH:P, :, DH:P]).then_inc(ctx_ready, 1)
            dve.tensor_copy(ksum[:, :], psS[:, :, 0]).then_inc(ctx_ready, 1)
            dve.wait_ge(ctx_ready, 3 + BASE)
            for c in range(PAIRS):
                dve.tensor_scalar(kmask[:, c], G.headmask[:, :], ksum[:, c:c + 1], None,
                                  ALU.mult).then_inc(kmask_ready, 1)

            def divide(n, u):
                for c in range(DC):
                    s = n * DC + c
                    r = c % 2
                    q = G.Q[:, c, bass.ds(n * D, D)]
                    dve.wait_ge(d_done, s + 1 + BASE)
                    dve.wait_ge(d_used, reuse(s) + BASE)
                    dve.tensor_scalar(den[:, r], (psK, psV)[r][:, :], 1e-8, None, ALU.add).then_inc(d_eps, 1)
                    dve.wait_ge(d_eps, s + 1 + BASE)
                    dve.reciprocal(den[:, r], den[:, r]).then_inc(d_rec, 1)
                    dve.wait_ge(d_rec, s + 1 + BASE)
                    dve.tensor_tensor(q, q, den[:, r], ALU.mult).then_inc(d_used, 1)
            lead(dve, d_used)
            loop(dve, n_cols, divide, 1)
            dve.wait_ge(edge_step, 2 * NB + BASE)
            dve.tensor_scalar(bg.bucket[:, :], bg.bucket[:, :], float(BUCKETS - 1), None,
                              ALU.min).then_inc(edge_step, 1)
            dve.wait_ge(edge_step, 2 * NB + 1 + BASE)
            dve.tensor_copy(G.edge_bucket[:, :], bg.bucket[:, :]).then_inc(edge_step, 1)

        @block.scalar
        def _(act):
            def body(b, u):
                act.wait_ge(t_done, done(b) + BASE)
                act.wait_ge(v_done, reuse(b, 2) + BASE)
                act.wait_ge(spill[u], (b - u) * 8 + BASE)
                act.activation(xnT[:, u], psT[:, :, :], ACT.Copy).then_inc(xnT_ready, 1)
                act.wait_ge(q_done, b + 1 + BASE)
                act.wait_ge(q_ready, b + BASE)
                act.activation(eq[:, :, :], psQ[:, :, :], ACT.Exp, scale=scale).then_inc(q_exp, 1)
                for j in range(2):
                    t = b * 2 + j
                    act.wait_ge(k_done, t + 1 + BASE)
                    act.wait_ge(k_ready, t + BASE)
                    act.activation(ek[:, :], psK[:, :], ACT.Exp).then_inc(k_exp, 1)
                    act.wait_ge(v_done, t + 3 + BASE)
                    act.wait_ge(ctx_done, reuse(t) + BASE)
                    act.activation(vf[:, j], psV[:, :], ACT.Copy).then_inc(v_ready, 1)
            loop(act, NB, body)
            for c in range(PAIRS):
                act.wait_ge(m_done, c + 1 + BASE)
                act.activation(M[:, c], psQ[:, 2 * (c % 2):2 * (c % 2) + 2].rearrange("p c n -> p (c n)"),
                               ACT.Copy).then_inc(m_ready, 1)

        @block.tensor
        def _(pe):
            lead(pe, t_done)
            lead(pe, v_done, 2)
            lead(pe, ctx_done)

            def context(t, j):
                pe.wait_ge(k_ready, t + 1 + BASE)
                pe.wait_ge(v_ready, t + 1 + BASE)
                for c in range(PAIRS):
                    first = isinstance(t, int) and t == 0 and c == 0
                    pe.matmul(psC[:, c], vf[:, j, c * P:(c + 1) * P], kf[:, j, c * P:(c + 1) * P],
                              start=first, stop=is_last(t, NT), skip_group_check=True)
                for c in range(PAIRS):
                    first = isinstance(t, int) and t == 0 and c == 0
                    mm = pe.matmul(psS[:, c], kf[:, j, c * P:(c + 1) * P], G.ones[:, 0:2],
                                   start=first, stop=is_last(t, NT), skip_group_check=True)
                mm.then_inc(ctx_done, 1)

            def body(b, u):
                first = isinstance(b, int) and b == 0
                pe.wait_ge(xn_ready, b * 2 + 2 + BASE)
                pe.wait_ge(xnT_ready, b + BASE)
                for c in range(DC):
                    for j in range(2):
                        mm = pe.transpose(psT[:, c, j * P:(j + 1) * P], xn[:, u, j, c * P:(c + 1) * P], G.ident[:, :])
                mm.then_inc(t_done, 1)
                pe.wait_ge(xnT_ready, b + 1 + BASE)
                pe.wait_ge(q_ready, b + BASE)
                if first:
                    pe.wait_ge(wq_in, 16 + BASE)
                for c in range(DC):
                    for d in range(DC):
                        mm = pe.matmul(psQ[:, c], wq[:, d, c * P:(c + 1) * P], xnT[:, u, d], start=(d == 0),
                                       stop=(d == DC - 1))
                mm.then_inc(q_done, 1)
                for j in range(2):
                    t = b * 2 + j
                    for ps, wt, wt_in, free, sem in ((psK, wk, wk_in, k_ready, k_done),
                                                     (psV, wv, wv_in, v_ready, v_done)):
                        if first and j == 0:
                            pe.wait_ge(wt_in, 16 + BASE)
                        pe.wait_ge(free, t + BASE)
                        for d in range(DC):
                            mm = pe.matmul(ps[:, :], xnT[:, u, d, j * P:(j + 1) * P], wt[:, d], start=(d == 0),
                                           stop=(d == DC - 1))
                        mm.then_inc(sem, 1)
                for j in range(2):
                    context(b * 2 + j, j)
            body(0, 0)
            body(1, 1)
            with pe.Fori(1, NB // 2 - 1) as i:
                for u in range(2):
                    body(i * 2 + u, u)
            body(NB - 2, 0)
            body(NB - 1, 1)
            pe.wait_ge(ctx_ready, 3 + BASE)
            pe.wait_ge(wo_in, 16 + BASE)
            for c in range(PAIRS):
                if c == 0:
                    pe.wait_ge(q_ready, NB + BASE)
                if c >= 2:
                    pe.wait_ge(m_ready, c - 1 + BASE)
                pe.matmul(psQ[:, 2 * (c % 2):2 * (c % 2) + 2].rearrange("p c n -> p (c n)"), ctxT[:, c], wo[:, c],
                          start=True, stop=True).then_inc(m_done, 1)
            pe.wait_ge(kmask_ready, PAIRS + BASE)

            def denominators(n, u):
                for c in range(DC):
                    s = n * DC + c
                    pe.wait_ge(d_used, reuse(s) + BASE)
                    pe.matmul((psK, psV)[c % 2][:, :], kmask[:, c], G.Q[:, c, bass.ds(n * D, D)], start=True,
                              stop=True).then_inc(d_done, 1)
            loop(pe, n_cols, denominators, 1)


def graph_attention(nc, G, W):
    VW = DH + 2
    with Phase(nc, "attn") as ph:
        wq, wk, wv, wo, M = W.wq, W.wk, W.wv, W.wo, W.M
        bq, bk, bv, bo, bsum = W.bq, W.bk, W.bv, W.bo, W.bsum
        xnT = (W.xnT, ph.sb("xnT1", [P, DC, BLK]))
        mq = ph.sb("mq", [P, 2, DC, BLK])
        qT = ph.sb("qT", [P, 2, DC, BLK])
        kT = ph.sb("kT", [P, 2, DC, BLK])
        v = ph.sb("v", [P, 2, HEADS, VW])
        s = ph.sb("s", [P, 2, HEADS, GRAPH])
        top = ph.sb("top", [P, 2, HEADS])
        prob = ph.sb("prob", [P, 2, HEADS, P])
        probT = ph.sb("probT", [P, 2, 4, P])
        rsum = ph.sb("rsum", [P, HEADS])
        o = ph.sb("o", [P, HEADS, DH])
        oT = ph.sb("oT", [P, DC, P])
        y = ph.sb("y", [P, D])
        psQ = ph.ps("psQ", [P, DC, BLK])
        psV = ph.ps("psV", [P, D])
        psS = ph.ps("psS", [P, 2, D])
        psP = ph.ps("psP", [P, 4, P])
        psO = ph.ps("psO", [P, 2, D])
        names = ("bsum_ready prob_zero v_ones x_in0 x_in1 mq_in0 mq_in1 passed_pe q_done q_ready v_done v_ready "
                 "s_done s_biased top_ready s_ready p_ready t_done pT_ready o_done rsum_ready o_ready oT_done "
                 "oT_ready y_done y_ready x_ready stats").split()
        S = dict(zip(names, ph.sems(*names)))
        S = type("Sems", (), S)
        x_in, mq_in = [S.x_in0, S.x_in1], [S.mq_in0, S.mq_in1]
        block = ph.block()

        @block.sync
        def _(sp):
            def load_mq(b, u):
                sp.wait_ge(S.y_done, reuse(b, 2) + BASE)
                sp.dma_start(mq[:, u].rearrange("p c n -> p (c n)"),
                             G.q_dram[:, bass.ds(b * DC * BLK, DC * BLK)]).then_inc(mq_in[u], 16)

            def body(b, u):
                sp.wait_ge(S.v_done, reuse(b, 2) + BASE)
                sp.dma_start(xnT[u][:, :, :].rearrange("p c n -> p (c n)"),
                             G.xnT_dram[:, bass.ds(b * DC * BLK, DC * BLK)]).then_inc(x_in[u], 16)
                load_mq(b, u)
            sp.sem_inc(x_in[0], 16)
            load_mq(0, 0)
            loop(sp, NB, body, head=2, done_steps=1)

        @block.gpsimd
        def _(pool):
            pool.memset(prob[:, :, :, :], 0.0).then_inc(S.prob_zero, 1)
            pool.memset(v[:, :, :, DH:VW], 1.0).then_inc(S.v_ones, 1)

        @block.vector
        def _(dve):
            dve.tensor_tensor(bsum[:, :], bsum[:, :], bo[:, :], ALU.add).then_inc(S.bsum_ready, 1)
            dve.wait_ge(S.bsum_ready, 1 + BASE)
            dve.wait_ge(S.v_ones, 1 + BASE)

            def values(t, j):
                dve.wait_ge(S.v_done, t + 1 + 2 * LEAD + BASE)
                dve.wait_ge(S.o_done, reuse(t) + BASE)
                dve.tensor_tensor(v[:, j, :, 0:DH], psV[:, :].rearrange("p (h d) -> p h d", h=HEADS),
                                  bv[:, :].rearrange("p (h d) -> p h d", h=HEADS), ALU.add).then_inc(S.v_ready, 1)

            def scores(t, j):
                dve.wait_ge(S.s_done, t + 1 + BASE)
                dve.wait_ge(S.p_ready, reuse(t, 2) + BASE)
                bias = G.BIAS[:, bass.ds(t * GRAPH * HEADS, GRAPH * HEADS)].rearrange(
                    "p (m h r) -> p r h m", m=GRAPH, r=2)
                heads = s[:, j].rearrange("p (h r) m -> p r h m", r=2)
                for r in range(2):
                    dve.scalar_tensor_tensor(out=heads[:, r], in0=psS[:, r, 0:4 * GRAPH].rearrange(
                        "p (h m) -> p h m", h=4), scalar=DH ** -0.5, in1=bias[:, r], op0=ALU.mult,
                        op1=ALU.add).then_inc(S.s_biased, 1)
                dve.wait_ge(S.s_biased, t * 2 + 2 + BASE)
                dve.tensor_reduce(top[:, j], s[:, j], AX.X, ALU.max).then_inc(S.top_ready, 1)
                dve.wait_ge(S.top_ready, t + 1 + BASE)
                dve.tensor_tensor(s[:, j], s[:, j], top[:, j].unsqueeze(2).to_broadcast([P, HEADS, GRAPH]),
                                  ALU.subtract).then_inc(S.s_ready, 1)

            def back(t, j):
                sums = psO[:, :, 0:4 * VW].rearrange("p r (h d) -> p r h d", h=4)
                dve.wait_ge(S.o_done, done(t) + BASE)
                dve.reciprocal(rsum[:, :].rearrange("p (r h) -> p r h", r=2),
                               sums[:, :, :, DH]).then_inc(S.rsum_ready, 1)
                dve.wait_ge(S.rsum_ready, t + 1 + BASE)
                dve.wait_ge(S.oT_done, t + BASE)
                for r in range(2):
                    dve.tensor_tensor(o[:, 4 * r:4 * r + 4], sums[:, r, :, 0:DH],
                                      rsum[:, 4 * r:4 * r + 4].unsqueeze(2).to_broadcast([P, 4, DH]),
                                      ALU.mult).then_inc(S.o_ready, 1)
                dve.wait_ge(S.y_done, t + 1 + 2 * LEAD + BASE)
                dve.wait_ge(S.x_ready, t + BASE)
                dve.tensor_tensor(y[:, :], psV[:, :], bsum[:, :], ALU.add).then_inc(S.y_ready, 1)
                dve.wait_ge(S.y_ready, t + 1 + BASE)
                dve.tensor_tensor(token_tile(G.X, t), token_tile(G.X, t), y[:, :], ALU.add).then_inc(S.x_ready, 1)
                dve.wait_ge(S.x_ready, t + 1 + BASE)
                tile_stats(dve, G, t).then_inc(S.stats, 1)

            def body(b, u):
                scores(b * 2 + 1, 1)
                values(b * 2 + 1, 1)
                back(b * 2, 0)
                if not is_last(b, NB):
                    values(b * 2 + 2, 0)
                    scores(b * 2 + 2, 0)
                back(b * 2 + 1, 1)
            values(0, 0)
            scores(0, 0)
            loop(dve, NB, body, peel=1)

        @block.scalar
        def _(act):
            act.wait_ge(S.prob_zero, 1 + BASE)
            lead(act, S.p_ready, 2)

            def project(b, u):
                for k, (dst, bias) in enumerate(((qT, bq), (kT, bk))):
                    for c in range(DC):
                        if c % 2 == 0:
                            act.wait_ge(S.q_done, b * 4 + k * 2 + c // 2 + 1 + BASE)
                        act.activation(dst[:, u, c], psQ[:, c], ACT.Identity, bias=bias[:, c:c + 1],
                                       ).then_inc(S.q_ready, 1)

            def exponentials(t, j):
                act.wait_ge(S.s_ready, t + 1 + BASE)
                act.wait_ge(S.t_done, t * 2 + BASE)
                for g in range(2):
                    h = slice(g * GRAPH, (g + 1) * GRAPH)
                    act.activation(prob[h, j, :, h], s[h, j], ACT.Exp).then_inc(S.p_ready, 1)

            def transposed(t, j):
                for r in range(2):
                    act.wait_ge(S.t_done, t * 2 + r + 1 + BASE)
                    if r == 0:
                        act.wait_ge(S.o_done, t + LEAD + BASE)
                    act.activation(probT[:, r], psP[:, :, :], ACT.Copy).then_inc(S.pT_ready, 1)

            def output(t, j):
                act.wait_ge(S.oT_done, t + 1 + BASE)
                act.wait_ge(S.y_done, t + 2 * LEAD + BASE)
                act.activation(oT[:, :, :], psP[:, :, :], ACT.Copy).then_inc(S.oT_ready, 1)

            def body(b, u):
                transposed(b * 2, 0)
                exponentials(b * 2 + 1, 1)
                output(b * 2, 0)
                if not is_last(b, NB):
                    project(b + 1, 1 - u)
                transposed(b * 2 + 1, 1)
                if not is_last(b, NB):
                    exponentials(b * 2 + 2, 0)
                output(b * 2 + 1, 1)
            project(0, 0)
            exponentials(0, 0)
            loop(act, NB, body, peel=1)

        @block.tensor
        def _(pe):
            lead(pe, S.v_done, 2)
            lead(pe, S.o_done)
            lead(pe, S.y_done, 2)

            def project(b, u):
                pe.wait_ge(x_in[u], (b - u) * 8 + 16 + BASE)
                for k, wt in enumerate((wq, wk)):
                    pe.wait_ge(S.q_ready, (b * 2 + k) * DC + BASE)
                    for c in range(DC):
                        for d in range(DC):
                            mm = pe.matmul(psQ[:, c], wt[:, d, c * P:(c + 1) * P], xnT[u][:, d], start=(d == 0),
                                           stop=(d == DC - 1))
                        if c % 2:
                            mm.then_inc(S.q_done, 1)
                    if k == 0:
                        values(b * 2, u, 0)

            def values(t, u, j):
                pe.wait_ge(S.v_ready, t + BASE)
                if not (isinstance(t, int) and t == 0):
                    pe.wait_ge(S.y_ready, t - 1 + BASE)
                for d in range(DC):
                    mm = pe.matmul(psV[:, :], xnT[u][:, d, j * P:(j + 1) * P], wv[:, d], start=(d == 0),
                                   stop=(d == DC - 1))
                mm.then_inc(S.v_done, 1)

            def scores(t, u, j):
                if j == 0:
                    pe.wait_ge(S.q_ready, (t + 2) * DC + BASE)
                gate(pe, S.s_biased, t * 2, S.passed_pe)
                for h in range(HEADS):
                    r = slice((h % 2) * DH, (h % 2 + 1) * DH)
                    for g in range(2):
                        n = slice(j * P + g * GRAPH, j * P + (g + 1) * GRAPH)
                        mm = pe.matmul(psS[g * GRAPH:(g + 1) * GRAPH, h % 2, (h // 2) * GRAPH:(h // 2 + 1) * GRAPH],
                                       qT[r, u, h // 2, n], kT[r, u, h // 2, n], start=True, stop=True)
                mm.then_inc(S.s_done, 1)

            def back(t, b, u, j):
                pe.wait_ge(S.p_ready, (t + 1 + LEAD) * 2 + BASE)
                def linear(c):
                    pe.matmul(psV[:, :], mq[:, u, c, j * P:(j + 1) * P], M[:, c], start=(c == 0), stop=False)
                for r in range(2):
                    pe.wait_ge(*((S.oT_ready, t + BASE) if r == 0 else (S.pT_ready, t * 2 + 1 + BASE)))
                    for h in range(4):
                        mm = pe.transpose(psP[:, h], prob[:, j, 4 * r + h], G.ident[:, :])
                    mm.then_inc(S.t_done, 1)
                    if r == 0:
                        if is_last(t, NT):
                            pe.wait_ge(S.y_ready, t + BASE)
                        else:
                            pe.wait_ge(S.v_ready, t + 2 + BASE)
                        if j == 0:
                            pe.wait_ge(mq_in[u], (b - u) * 8 + 16 + BASE)
                        linear(0)
                pe.wait_ge(S.v_ready, t + 1 + BASE)
                pe.wait_ge(S.o_ready, t * 2 + BASE)
                for r in range(2):
                    pe.wait_ge(S.pT_ready, t * 2 + r + 1 + BASE)
                    for h in range(4):
                        mm = pe.matmul(psO[:, r, h * VW:(h + 1) * VW], probT[:, r, h], v[:, j, 4 * r + h],
                                       start=True, stop=True)
                mm.then_inc(S.o_done, 1)
                linear(1)
                linear(2)
                pe.wait_ge(S.o_ready, t * 2 + 2 + BASE)
                for c in range(DC):
                    mm = pe.transpose(psP[:, c], o[:, 2 * c:2 * c + 2].rearrange("p h d -> p (h d)"), G.ident[:, :])
                mm.then_inc(S.oT_done, 1)
                linear(3)
                pe.wait_ge(S.oT_ready, t + 1 + BASE)
                for c in range(DC):
                    mm = pe.matmul(psV[:, :], oT[:, c], wo[:, c], start=False, stop=(c == DC - 1))
                mm.then_inc(S.y_done, 1)

            def body(b, u):
                scores(b * 2 + 1, u, 1)
                values(b * 2 + 1, u, 1)
                back(b * 2, b, u, 0)
                if not is_last(b, NB):
                    project(b + 1, 1 - u)
                    scores(b * 2 + 2, 1 - u, 0)
                back(b * 2 + 1, b, u, 1)
            project(0, 0)
            scores(0, 0, 0)
            loop(pe, NB, body, peel=1)


def route(nc, G, w, pre, shared, E):
    FS = 4
    with Phase(nc, f"route{pre}") as ph:
        wr = ph.sb("wr", [P, DC, EXPERTS])
        br = ph.sb("br", [P, EXPERTS])
        ln = ln_stats_buffers(ph)
        hn = ph.sb("hn", [P, 2, 2, D])
        H = ph.sb("H", [P, NT, D])
        hT = ph.sb("hT", [P, 2, DC, BLK])
        L = ph.sb("L", [P, NT, EXPERTS])
        small = [ph.sb(f"small{i}", [P, NT]) for i in range(3)]
        pv = ph.sb("pv", [P, NT, 8])
        pidx = ph.sb("pidx", [P, NT, 8], U32)
        which = ph.sb("which", [P, NT, TOPK])
        onehot = ph.sb("onehot", [P, EXPERTS, TOPK * NT])
        rank = ph.sb("rank", [P, EXPERTS, TOPK * NT])
        part1 = ph.sb("part1", [P, NT, EXPERTS])
        slot = ph.sb("slot", [P, TOPK * NT])
        same = ph.sb("same", [P, NST])
        bs = bucket_starts(ph, EXPERTS, SLOT_TILE)
        bg = bucket_groups(ph, EXPERTS, SLOT_TILE, NST, bs.end, ph.sb("past", [P, NST, EXPERTS]))
        psT = ph.ps("psT", [P, DC, BLK])
        psL = ph.ps("psL", [P, 2, EXPERTS])
        names = ("w_in w1_in w2_in b_in passed_pe sw_w1_first sw_w2_first first_hi first_lo kept h_ready "
                 "t_done hT_ready "
                 "l_done l_ready step exps_ready slotted sw_scattered hid_done hid_ready y_done y_ready x_ready "
                 "srow_ready").split()
        S = type("Sems", (), dict(zip(names, ph.sems(*names))))
        n_w = 2
        if shared:
            w1 = ph.sb("w1", [P, DC, FS * P])
            w2 = ph.sb("w2", [P, FS, D])
            b1 = ph.sb("b1", [P, FS])
            brow = ph.sb("brow", [P, 2, D])
            srow = ph.sb("srow", [P, D])
            hid = ph.sb("hid", [P, 2, FS, BLK])
            y = ph.sb("y", [P, D])
            psH = [ph.ps(f"psH{i}", [P, D]) for i in range(2)]
            psY = ph.ps("psY", [P, D])
            n_w = 3
        block = ph.block()

        @block.sync
        def _(sp):
            sp.dma_start(wr[:, :, :], w[pre + "Wr"].rearrange("(c p) n -> p c n", p=P)).then_inc(S.w_in, 16)
            sp.dma_start(br[:, :], w[pre + "br"].partition_broadcast(P)).then_inc(S.w_in, 16)
            if shared:
                sp.dma_start(b1[:, :], w["sb1"]).then_inc(S.w_in, 16)
                for n in range(2):
                    sp.dma_start(brow[:, n], w["sb2"][n].partition_broadcast(P)).then_inc(S.b_in, 16)
                sp.dma_start(w1[:, :, :], w["sw1"].rearrange("(c p) n -> p c n", p=P)).then_inc(S.w1_in, 16)
                sp.dma_start(w2[:, :, :], w["sw2"].rearrange("(c p) n -> p c n", p=P)).then_inc(S.w2_in, 16)

        @block.gpsimd
        def _(pool):
            ln_stats_pool(pool, ln, G)
            bucket_groups_pool(pool, bg)
            pool.wait_ge(S.kept, NT + BASE)
            pool.wait_ge(S.slotted, 5 + BASE)
            row = bass.IndirectOffsetOnAxis(ap=G.wrow[:, 0:1], axis=0)
            pool.indirect_dma_start(out=E.w1[:, :, :].rearrange("p c f -> p (c f)"), out_offset=None,
                                    in_=w[pre + "W1"], in_offset=row).then_inc(S.sw_w1_first, 16)
            pool.indirect_dma_start(out=E.w2[:, :], out_offset=None, in_=w[pre + "W2"],
                                    in_offset=row).then_inc(S.sw_w2_first, 16)
            for k in range(TOPK):
                for t in range(NT):
                    n = k * NT + t
                    pool.indirect_dma_start(
                        out=G.xs_dram, out_offset=bass.IndirectOffsetOnAxis(ap=G.place[:, n:n + 1], axis=0),
                        in_=H[:, t], in_offset=None).then_inc(S.sw_scattered, 16)
            pool.wait_ge(S.sw_scattered, 16 * TOPK * NT)
            pool.wait_ge(S.sw_w2_first, 16)

        @block.vector
        def _(dve):
            ln_stats_vector(dve, ln, G.bn)
            if shared:
                dve.wait_ge(S.b_in, 32 + BASE)
                dve.tensor_tensor(srow[:, :], brow[:, 0], brow[:, 1], ALU.add).then_inc(S.srow_ready, 1)
                dve.wait_ge(S.srow_ready, 1 + BASE)

            def norm_block(b, u):
                dve.wait_ge(S.t_done, reuse(b) + BASE)
                for j in range(2):
                    t = b * 2 + j
                    dve.tensor_scalar(hn[:, u, j], token_tile(G.X, t), col(ln.rstd, t), col(ln.shift, t),
                                      ALU.mult, ALU.add).then_inc(S.h_ready, 1)
                for j in range(2):
                    t = b * 2 + j
                    dve.tensor_scalar(token_tile(H, t), token_tile(G.X, t), col(ln.rstd, t), col(ln.shift, t),
                                      ALU.mult, ALU.add).then_inc(S.kept, 1)

            def body(b, u):
                if not (isinstance(b, int) and b + 2 >= NB):
                    norm_block(b + 2, u)
                dve.wait_ge(S.l_done, b + 1 + BASE)
                dve.tensor_tensor(L[:, bass.ds(b * 2, 2), :], psL[:, :, :],
                                  br[:, :].unsqueeze(1).to_broadcast([P, 2, EXPERTS]), ALU.add).then_inc(S.l_ready, 1)
                if shared:
                    for j in range(2):
                        t = b * 2 + j
                        dve.wait_ge(S.y_done, t + 1 + 2 * LEAD + BASE)
                        dve.wait_ge(S.x_ready, t + BASE)
                        dve.tensor_tensor(y[:, :], psY[:, :], srow[:, :], ALU.add).then_inc(S.y_ready, 1)
                        dve.wait_ge(S.y_ready, t + 1 + BASE)
                        dve.tensor_tensor(token_tile(G.X, t), token_tile(G.X, t), y[:, :],
                                          ALU.add).then_inc(S.x_ready, 1)
            norm_block(0, 0)
            norm_block(1, 1)
            dve.wait_ge(S.w_in, 16 * n_w + BASE)
            loop(dve, NB, body, peel=2)
            st = Step(dve, S.step, 0, 64)

            def spread(a):
                return a[:, :].unsqueeze(2).to_broadcast([P, NT, EXPERTS])
            dve.wait_ge(S.l_ready, NB + BASE)
            st.do(dve.tensor_reduce(small[0][:, :], L[:, :, :], AX.X, ALU.max))
            st.do(dve.tensor_tensor(L[:, :, :], L[:, :, :], spread(small[0]), ALU.subtract))
            dve.wait_ge(S.exps_ready, 1 + BASE)
            st.do(dve.tensor_reduce(small[1][:, :], L[:, :, :], AX.X, ALU.add))
            st.do(dve.reciprocal(small[2][:, :], small[1][:, :]))
            st.do(dve.tensor_tensor(L[:, :, :], L[:, :, :], spread(small[2]), ALU.mult))
            for t in range(NT):
                st.did(dve.max(pv[:, t], L[:, t]))
            st.wait()
            for t in range(NT):
                st.did(dve.max_index(pidx[:, t], pv[:, t], L[:, t]))
            st.wait()
            st.did(dve.tensor_copy(which[:, :, :], pidx[:, :, 0:TOPK]))
            st.do(dve.tensor_copy(G.gate[:, :, :], pv[:, :, 0:TOPK]))
            for k in range(TOPK):
                st.did(dve.tensor_tensor(
                    onehot[:, :, k * NT:(k + 1) * NT], G.iota512[:, 0:EXPERTS].unsqueeze(2).to_broadcast([P, EXPERTS, NT]),
                    which[:, :, k].unsqueeze(1).to_broadcast([P, EXPERTS, NT]), ALU.is_equal))
            st.wait()
            dve.tensor_reduce(bs.count[:, :], onehot[:, :, :], AX.X, ALU.add).then_inc(bs.counted, 1)
            for k, dst in enumerate((G.comb, part1)):
                st.did(dve.tensor_tensor(dst[:, :, :], onehot[:, :, k * NT:(k + 1) * NT].rearrange("p e t -> p t e"),
                                         G.gate[:, :, k].unsqueeze(2).to_broadcast([P, NT, EXPERTS]), ALU.mult))
            st.wait()
            st.do(dve.tensor_tensor(G.comb[:, :, :], G.comb[:, :, :], part1[:, :, :], ALU.add))
            bucket_starts_vector(dve, bs)
            bucket_groups_vector(dve, bg, st)
            for e in range(EXPERTS):
                st.did(dve.tensor_tensor_scan(rank[:, e], onehot[:, e], onehot[:, e], bs.first[:, e:e + 1], ALU.add,
                                              ALU.bypass))
            st.wait()
            sl = Step(dve, S.slotted, 0, 8)
            sl.do(dve.tensor_tensor(rank[:, :, :], rank[:, :, :], onehot[:, :, :], ALU.mult))
            sl.do(dve.tensor_reduce(slot[:, :], rank[:, :, :].rearrange("p e n -> p n e"), AX.X, ALU.add))
            sl.did(dve.tensor_copy(G.place[:, :], slot[:, :]))
            sl.do(dve.tensor_scalar(bg.bucket[:, :], bg.bucket[:, :], float(P), None, ALU.mult))
            sl.did(dve.tensor_scalar(G.wrow[:, :], bg.bucket[:, :], G.part[:, 0:1], None, ALU.add))
            sl.did(dve.memset(same[:, 0:1], 0.0))
            sl.do(dve.tensor_tensor(same[:, 1:NST], bg.bucket[:, 1:NST], bg.bucket[:, 0:NST - 1], ALU.is_equal))
            sl.did(dve.scalar_tensor_tensor(out=G.wnew[:, :], in0=same[:, :], scalar=float(EXPERTS * P),
                                            in1=G.wrow[:, :], op0=ALU.mult, op1=ALU.add))
            for c in range(DC):
                dve.wait_ge(S.first_hi, c + 1 + BASE)
                dve.tensor_tensor(E.w1l[:, c], E.w1[:, c], E.w1h[:, c], ALU.subtract).then_inc(S.first_lo, 1)
            dve.wait_ge(S.first_lo, DC + BASE)

        @block.scalar
        def _(act):
            act.wait_ge(S.w_in, 16 * n_w + BASE)

            lead(act, S.hid_ready)

            def body(b, u):
                act.wait_ge(S.t_done, done(b) + BASE)
                act.activation(hT[:, u], psT[:, :, :], ACT.Copy).then_inc(S.hT_ready, 1)
                if shared:
                    for f in range(FS):
                        n = b * FS + f
                        act.wait_ge(S.hid_done, n + 1 + BASE)
                        if f == 0:
                            act.wait_ge(S.y_done, reuse(b, 2) + BASE)
                        act.activation(hid[:, u, f], psH[f % 2][:, 0:BLK], ACT.Gelu,
                                       bias=b1[:, f:f + 1]).then_inc(S.hid_ready, 1)
            loop(act, NB, body)
            act.wait_ge(S.step, 2 + BASE)
            act.activation(L[:, :, :], L[:, :, :], ACT.Exp).then_inc(S.exps_ready, 1)
            act.wait_ge(S.sw_w1_first, 16)
            for c in range(DC):
                act.activation(E.w1h[:, c], E.w1[:, c], ACT.Copy).then_inc(S.first_hi, 1)

        @block.tensor
        def _(pe):
            lead(pe, S.t_done)
            lead(pe, S.y_done, 2)

            def transposes(b, u):
                pe.wait_ge(S.h_ready, b * 2 + 2 + BASE)
                pe.wait_ge(S.hT_ready, b + BASE)
                for c in range(DC):
                    for j in range(2):
                        mm = pe.transpose(psT[:, c, j * P:(j + 1) * P], hn[:, u, j, c * P:(c + 1) * P], G.ident[:, :])
                mm.then_inc(S.t_done, 1)

            def body(b, u):
                if not (shared or is_last(b, NB)):
                    transposes(b + 1, 1 - u)
                pe.wait_ge(S.hT_ready, b + 1 + BASE)
                if isinstance(b, int) and b == 0:
                    pe.wait_ge(S.w_in, 16 * n_w + BASE)
                gate(pe, S.l_ready, b, S.passed_pe)
                for j in range(2):
                    for c in range(DC):
                        mm = pe.matmul(psL[:, j], hT[:, u, c, j * P:(j + 1) * P], wr[:, c], start=(c == 0),
                                       stop=(c == DC - 1))
                mm.then_inc(S.l_done, 1)
                if shared:
                    if isinstance(b, int) and b == 0:
                        pe.wait_ge(S.w1_in, 16 + BASE)
                    for f in range(FS):
                        pe.wait_ge(S.hid_ready, b * FS + f - 1 + LEAD + BASE)
                        for c in range(DC):
                            mm = pe.matmul(psH[f % 2][:, 0:BLK], w1[:, c, f * P:(f + 1) * P], hT[:, u, c],
                                           start=(c == 0), stop=(c == DC - 1))
                        mm.then_inc(S.hid_done, 1)
                if shared and not is_last(b, NB):
                    transposes(b + 1, 1 - u)
                if shared:
                    if isinstance(b, int) and b == 0:
                        pe.wait_ge(S.w2_in, 16 + BASE)
                    pe.wait_ge(S.hid_ready, b * FS + FS + LEAD + BASE)
                    for j in range(2):
                        pe.wait_ge(S.y_ready, b * 2 + j + BASE)
                        for f in range(FS):
                            mm = pe.matmul(psY[:, :], hid[:, u, f, j * P:(j + 1) * P], w2[:, f], start=(f == 0),
                                           stop=(f == FS - 1))
                        mm.then_inc(S.y_done, 1)
            transposes(0, 0)
            loop(pe, NB, body, peel=1, head=2)
            bucket_starts_tensor(pe, bs, G, 1)


class ExpertWeights:

    def __init__(self, nc, ctx, pre, F):
        def sb(name, shape, dt=F32):
            return ctx.enter_context(nc.sbuf_tensor(f"experts{pre}_{name}", shape, dt))
        self.F = F
        self.w1 = sb("w1", [P, DC, F])
        self.w2 = sb("w2", [P, F // P * D])
        self.w1h, self.w1l = (sb(n, [P, DC, F], F32R) for n in ("w1h", "w1l"))


def experts(nc, G, w, pre, E):
    F, w1, w2, w1h, w1l = E.F, E.w1, E.w2, E.w1h, E.w1l
    FC = F // P
    RING = 4
    RAW = min(RING, FC)
    WP = min(4, FC)
    WN = FC * D // WP
    with Phase(nc, f"experts{pre}") as ph:
        w2h, w2l = (ph.sb(n, [P, FC * D], F32R) for n in ("w2h", "w2l"))
        b1 = ph.sb("b1", [P, 2, FC])
        b1_index = ph.sb("b1_index", [P, 2], I32)
        w1_index, w2_index = (ph.sb(n, [P, 1], I32) for n in ("w1_index", "w2_index"))
        xs = ph.sb("xs", [P, 2, 2, D])
        xh, xl = (ph.sb(n, [P, DC, BLK], F32R) for n in ("xh", "xl"))
        raw = ph.sb("raw", [P, RAW, BLK])
        hh, hl = (ph.sb(n, [P, 2, FC, BLK], F32R) for n in ("hh", "hl"))
        y = ph.sb("y", [P, 2, 2, D])
        psT = ph.ps("psT", [P, DC, BLK])
        psH = [ph.ps(f"psH{i}", [P, D]) for i in range(RING)]
        psY = [ph.ps(f"psY{i}", [P, D]) for i in range(2)]
        names = ("passed index_ready sw_b_in0 sw_b_in1 sw_w1_in sw_w2_in xs_in0 xs_in1 "
                 "w1_hi w1_lo w2_hi w2_lo t_done x_hi x_lo "
                 "hid_done gelu_done h_hi h_lo y_done y_ready stored0 stored1").split()
        S = type("Sems", (), dict(zip(names, ph.sems(*names))))
        b_in, xs_in, stored = (S.sw_b_in0, S.sw_b_in1), (S.xs_in0, S.xs_in1), (S.stored0, S.stored1)
        block = ph.block()
        xs_dram = G.xs_dram.rearrange("(n p j) d -> p n (j d)", p=P, j=2)
        ys_dram = G.ys_dram.rearrange("(n p j) d -> p n (j d)", p=P, j=2)

        @block.gpsimd
        def _(pool):
            def gather(dst, table, index, sem, **bound):
                pool.indirect_dma_start(out=dst, out_offset=None, in_=w[pre + table],
                                        in_offset=bass.IndirectOffsetOnAxis(ap=index, axis=0), **bound
                                        ).then_inc(sem, 16)
            bound = dict(bounds_check=EXPERTS * P - 1, oob_is_err=False)

            def load_weights(g, free, pieces, index, dst, table, sem, k):
                gate(pool, free, done(g - 1, pieces), S.passed)
                pool.tensor_copy(index, col(G.wnew, g)).then_inc(S.index_ready, 1)
                gate(pool, S.index_ready, k, S.passed)
                gather(dst, table, index, sem, **bound)

            def load_w2(g, k):
                load_weights(g, S.w2_lo, WP, w2_index[:, :], w2[:, :], "W2", S.sw_w2_in, k)

            def load(g, u):
                first, early = (isinstance(g, int) and g < n for n in (1, 2))
                gate(pool, S.h_lo, reuse(g, FC), S.passed)
                pool.tensor_copy(b1_index[:, u:u + 1], col(G.wrow, g)).then_inc(S.index_ready, 1)
                gate(pool, S.index_ready, 1 if first else g * 3 - (1 if early else 2), S.passed)
                gather(b1[:, u], "b1", b1_index[:, u:u + 1], b_in[u])
                if first:
                    return
                load_weights(g, S.w1_lo, DC, w1_index[:, :], w1[:, :, :].rearrange("p c f -> p (c f)"), "W1", S.sw_w1_in,
                             g * 3 - (0 if early else 1))
                if not early:
                    load_w2(g - 1, g * 3)
            loop(pool, NST, load, head=2)
            load_w2(NST - 1, NST * 3 - 2)

        @block.sync
        def _(sp):
            def store(g, u):
                sp.wait_ge(S.y_ready, done(g, 2) + BASE)
                sp.dma_start(ys_dram[:, bass.ds(g, 1), :].rearrange("p a d -> p (a d)"),
                             y[:, u].rearrange("p j d -> p (j d)")).then_inc(stored[u], 16)

            loop(sp, NST, store)
            for u in range(2):
                sp.wait_ge(stored[u], 16 * ((NST + 1 - u) // 2) + BASE)

        @block.scalar
        def _(act):
            lead(act, S.gelu_done, RING)

            def load_x(g, u):
                act.wait_ge(S.t_done, reuse(g) + BASE)
                act.dma_start(xs[:, u].rearrange("p j d -> p (j d)"),
                              xs_dram[:, bass.ds(g, 1), :].rearrange("p a d -> p (a d)")).then_inc(xs_in[u], 16)

            def split_w1(g):
                act.wait_ge(S.sw_w1_in, g * 16)
                act.wait_ge(S.hid_done, g * FC + BASE)
                for c in range(DC):
                    act.activation(w1h[:, c], w1[:, c], ACT.Copy).then_inc(S.w1_hi, 1)

            def split_w2(g):
                if not (isinstance(g, int) and g == 0):
                    act.wait_ge(S.sw_w2_in, g * 16)
                act.wait_ge(S.y_done, done(g - 1, 2) + BASE)
                for k in range(WP):
                    n = slice(k * WN, (k + 1) * WN)
                    act.activation(w2h[:, n], w2[:, n], ACT.Copy).then_inc(S.w2_hi, 1)

            def split_x(g):
                act.wait_ge(S.t_done, done(g) + BASE)
                act.wait_ge(S.hid_done, g * FC + BASE)
                act.activation(xh[:, :, :], psT[:, :, :], ACT.Copy).then_inc(S.x_hi, 1)

            def hidden(g, u):
                act.wait_ge(b_in[u], (g - u) * 8 + 16)
                act.wait_ge(S.y_done, reuse(g, 2) + BASE)
                for f in range(FC + 1):
                    if f < FC:
                        act.wait_ge(S.hid_done, g * FC + f + 1 + BASE)
                        act.wait_ge(S.h_lo, g * FC + f + 1 - RAW + LEAD * FC + BASE)
                        act.activation(raw[:, f % RAW], psH[(u * FC + f) % RING][:, 0:BLK], ACT.Gelu,
                                       bias=b1[:, u, f:f + 1]).then_inc(S.gelu_done, 1)
                    if f:
                        act.wait_ge(S.gelu_done, g * FC + f + RING + BASE)
                        act.activation(hh[:, u, f - 1], raw[:, (f - 1) % RAW], ACT.Copy).then_inc(S.h_hi, 1)

            def body(g, u):
                if not (isinstance(g, int) and g + 2 >= NST):
                    load_x(g + 2, u)
                hidden(g, u)
                if not is_last(g, NST):
                    split_x(g + 1)
                    split_w1(g + 1)
                split_w2(g)
            load_x(0, 0)
            load_x(1, 1)
            act.sem_inc(S.w1_hi, DC)
            split_x(0)
            loop(act, NST, body, peel=2, head=2)

        @block.vector
        def _(dve):
            lead(dve, S.w1_lo, 2 * DC)
            lead(dve, S.w2_lo, WP)
            lead(dve, S.h_lo, FC)
            lead(dve, S.y_ready, 2)

            def rest_w1(g):
                for c in range(DC):
                    dve.wait_ge(S.w1_hi, g * DC + c + 1 + BASE)
                    dve.tensor_tensor(w1l[:, c], w1[:, c], w1h[:, c], ALU.subtract).then_inc(S.w1_lo, 1)

            def rest_w2(g):
                for k in range(WP):
                    n = slice(k * WN, (k + 1) * WN)
                    dve.wait_ge(S.w2_hi, g * WP + k + 1 + BASE)
                    dve.tensor_tensor(w2l[:, n], w2[:, n], w2h[:, n], ALU.subtract).then_inc(S.w2_lo, 1)

            def rest_x(g):
                dve.wait_ge(S.x_hi, g + 1 + BASE)
                dve.tensor_tensor(xl[:, :, :], psT[:, :, :], xh[:, :, :], ALU.subtract).then_inc(S.x_lo, 1)

            def outputs(g, u):
                dve.wait_ge(stored[u], (g - u) * 8 + BASE)
                for j in range(2):
                    dve.wait_ge(S.y_done, g * 2 + j + 1 + 2 * LEAD + BASE)
                    dve.tensor_copy(y[:, u, j], psY[j][:, :]).then_inc(S.y_ready, 1)

            def body(g, u):
                for f in range(FC):
                    dve.wait_ge(S.h_hi, g * FC + f + 1 + BASE)
                    dve.tensor_tensor(hl[:, u, f], raw[:, f % RAW], hh[:, u, f], ALU.subtract).then_inc(S.h_lo, 1)
                if not is_last(g, NST):
                    rest_x(g + 1)
                    rest_w1(g + 1)
                if not (isinstance(g, int) and g == 0):
                    outputs(g - 1, 1 - u)
                rest_w2(g)
            rest_x(0)
            loop(dve, NST, body, peel=1, head=2)
            outputs(NST - 1, (NST - 1) % 2)

        @block.tensor
        def _(pe):
            lead(pe, S.t_done)
            lead(pe, S.y_done, 2)

            def transposes(g, u):
                pe.wait_ge(xs_in[u], (g - u) * 8 + 16 + BASE)
                pe.wait_ge(S.x_lo, g + BASE)
                for c in range(DC):
                    for j in range(2):
                        mm = pe.transpose(psT[:, c, j * P:(j + 1) * P], xs[:, u, j, c * P:(c + 1) * P], G.ident[:, :])
                mm.then_inc(S.t_done, 1)

            def hidden(g, u):
                pe.wait_ge(S.x_lo, g + 1 + BASE)
                pe.wait_ge(S.w1_lo, done(g, DC) + BASE)
                for f in range(FC):
                    pe.wait_ge(S.gelu_done, g * FC + f + 1 + BASE)
                    n = slice(f * P, (f + 1) * P)
                    for c in range(DC):
                        for k, (a, b) in enumerate(((w1h, xh), (w1h, xl), (w1l, xh))):
                            mm = pe.matmul(psH[(u * FC + f) % RING][:, 0:BLK], a[:, c, n], b[:, c],
                                           start=(c + k == 0), stop=(c == DC - 1 and k == 2))
                    mm.then_inc(S.hid_done, 1)

            def outputs(g, u):
                pe.wait_ge(S.h_lo, done(g, FC) + BASE)
                pe.wait_ge(S.w2_lo, done(g, WP) + BASE)
                for j in range(2):
                    pe.wait_ge(S.y_ready, g * 2 + j + 1 + BASE)
                    for f in range(FC):
                        n = slice(f * D, (f + 1) * D)
                        for k, (a, b) in enumerate(((hh, w2h), (hh, w2l), (hl, w2h))):
                            mm = pe.matmul(psY[j][:, :], a[:, u, f, j * P:(j + 1) * P], b[:, n],
                                           start=(f + k == 0), stop=(f == FC - 1 and k == 2))
                    mm.then_inc(S.y_done, 1)

            def body(g, u):
                if not is_last(g, NST):
                    hidden(g + 1, 1 - u)
                if not (isinstance(g, int) and g + 2 >= NST):
                    transposes(g + 2, u)
                outputs(g, u)
            transposes(0, 0)
            hidden(0, 0)
            transposes(1, 1)
            loop(pe, NST, body, peel=2)


def combine(nc, G, w, pre, out):
    RING = 4
    with Phase(nc, f"combine{pre}") as ph:
        b2 = ph.sb("b2", [EXPERTS, D])
        place = ph.sb("place", [P, RING, TOPK], I32)
        comb = ph.sb("comb", [P, 2, EXPERTS])
        combT = ph.sb("combT", [EXPERTS, 2, P])
        y = ph.sb("y", [P, RING, TOPK, D])
        psT = ph.ps("psT", [EXPERTS, P])
        psB = [ph.ps(f"psB{i}", [P, D]) for i in range(2)]
        names = ("w_in passed place_ready sw_y_in0 sw_y_in1 sw_y_in2 sw_y_in3 comb_ready "
                 "t_done combT_ready b_done x_biased "
                 "x_first x_ready out0 out1 stats").split()
        S = type("Sems", (), dict(zip(names, ph.sems(*names))))
        y_in, stored = (S.sw_y_in0, S.sw_y_in1, S.sw_y_in2, S.sw_y_in3), (S.out0, S.out1)
        block = ph.block()

        def x_done(t):
            return t + 1 + RING

        @block.sync
        def _(sp):
            sp.dma_start(b2[:, :], w[pre + "b2"]).then_inc(S.w_in, 16)
            if out is not None:
                rows = out.rearrange("(t p) d -> p t d", p=P)

                def body(t, u):
                    sp.wait_ge(S.x_ready, x_done(t) + BASE)
                    sp.dma_start(rows[:, bass.ds(t, 1), :].rearrange("p a d -> p (a d)"),
                                 token_tile(G.X, t)).then_inc(stored[u], 16)
                loop(sp, NT, body)
                for u in range(2):
                    sp.wait_ge(stored[u], 16 * NT // 2 + BASE)

        @block.gpsimd
        def _(pool):
            lead(pool, S.place_ready)

            def body(t, u):
                gate(pool, S.x_ready, x_done(t - RING), S.passed)
                pool.tensor_copy(place[:, u], G.place[:, :].rearrange("p (k t) -> p t k", k=TOPK)[
                    :, bass.ds(t, 1), :].rearrange("p a k -> p (a k)")).then_inc(S.place_ready, 1)
                gate(pool, S.place_ready, done(t), S.passed)
                for k in range(TOPK):
                    pool.indirect_dma_start(
                        out=y[:, u, k], out_offset=None, in_=G.ys_dram,
                        in_offset=bass.IndirectOffsetOnAxis(ap=place[:, u, k:k + 1], axis=0)).then_inc(y_in[u], 16)
            loop(pool, NT, body, RING)

        @block.vector
        def _(dve):
            lead(dve, S.x_ready, RING)

            def columns(t, u):
                dve.tensor_copy(comb[:, u], G.comb[:, bass.ds(t, 1), :].rearrange("p a e -> p (a e)")
                                ).then_inc(S.comb_ready, 1)

            def body(t, k):
                u = k % 2
                if not is_last(t, NT):
                    columns(t + 1, 1 - u)
                x = token_tile(G.X, t)
                gates = G.gate[:, bass.ds(t, 1), :].rearrange("p a k -> p (a k)")
                dve.wait_ge(S.b_done, t + 1 + BASE)
                dve.tensor_tensor(x, x, psB[u][:, :], ALU.add).then_inc(S.x_biased, 1)
                dve.wait_ge(y_in[k], (t - k) * 8 + 32)
                dve.wait_ge(S.x_biased, t + 1 + BASE)
                dve.scalar_tensor_tensor(out=x, in0=y[:, k, 0], scalar=gates[:, 0:1], in1=x, op0=ALU.mult,
                                         op1=ALU.add).then_inc(S.x_first, 1)
                dve.wait_ge(S.x_first, t + 1 + BASE)
                dve.scalar_tensor_tensor(out=x, in0=y[:, k, 1], scalar=gates[:, 1:2], in1=x, op0=ALU.mult,
                                         op1=ALU.add).then_inc(S.x_ready, 1)
                if out is None:
                    dve.wait_ge(S.x_ready, x_done(t) + BASE)
                    tile_stats(dve, G, t).then_inc(S.stats, 1)
            columns(0, 0)
            loop(dve, NT, body, RING, peel=RING)

        @block.scalar
        def _(act):
            def body(t, u):
                act.wait_ge(S.t_done, t + 1 + BASE)
                act.activation(combT[:, u], psT[:, :], ACT.Copy).then_inc(S.combT_ready, 1)
            loop(act, NT, body)

        @block.tensor
        def _(pe):
            pe.wait_ge(S.w_in, 16 + BASE)

            def body(t, u):
                pe.wait_ge(S.comb_ready, t + 1 + BASE)
                pe.wait_ge(S.combT_ready, t + BASE)
                pe.transpose(psT[:, :], comb[:, u], G.ident[:, :]).then_inc(S.t_done, 1)
                pe.wait_ge(S.combT_ready, t + 1 + BASE)
                pe.wait_ge(S.x_ready, x_done(t - 2) + BASE)
                pe.matmul(psB[u][:, :], combT[:, u], b2[:, :], start=True, stop=True).then_inc(S.b_done, 1)
            loop(pe, NT, body)


def neighbour_products(nc, G, w):
    with Phase(nc, "nprod") as ph:
        raw = (ph.sb("raw", [P, DC, D])[:, :, :], G.Y1[:, NT - DC:NT, :])
        wh, wl = (ph.sb(n, [P, 2, DC, D], F32R) for n in ("wh", "wl"))
        ln = ln_stats_buffers(ph)
        xn = ph.sb("xn", [P, 2, 2, D])
        xh, xl = (ph.sb(n, [P, 2, DC, BLK], F32R) for n in ("xh", "xl"))
        psT = ph.ps("psT", [P, DC, BLK])
        psY = [[ph.ps(f"psY{k}{j}", [P, D]) for j in range(2)] for k in range(2)]
        names = ("w_in0 w_in1 w_hi w_lo xn_ready kept0 kept1 stats t_done x_hi x_lo y1_done y2_done y1_ready y2_hi "
                 "y2_lo").split()
        S = type("Sems", (), dict(zip(names, ph.sems(*names))))
        kept = (S.kept0, S.kept1)
        w_in = (S.w_in0, S.w_in1)
        block = ph.block()

        @block.sync
        def _(sp):
            for k in range(2):
                sp.dma_start(raw[k], w["gw"][k * D:(k + 1) * D, :].rearrange("(c p) n -> p c n", p=P)
                             ).then_inc(w_in[k], 16)

            def keep(b, u):
                sp.wait_ge(S.xn_ready, b * 2 + 2 + BASE)
                sp.dma_start(G.xn_dram[:, bass.ds(b * 2 * D, 2 * D)],
                             xn[:, u].rearrange("p j d -> p (j d)")).then_inc(kept[u], 16)
            loop(sp, NB, keep)
            for u in range(2):
                sp.wait_ge(kept[u], 16 * NB // 2 + BASE)

        @block.gpsimd
        def _(pool):
            ln_stats_pool(pool, ln, G)

        @block.vector
        def _(dve):
            ln_stats_vector(dve, ln, G.bn)

            def norm_block(b, u):
                dve.wait_ge(S.t_done, reuse(b) + BASE)
                dve.wait_ge(kept[u], (b - u) * 8 + BASE)
                for j in range(2):
                    t = b * 2 + j
                    dve.tensor_scalar(xn[:, u, j], token_tile(G.X, t), col(ln.rstd, t), col(ln.shift, t),
                                      ALU.mult, ALU.add).then_inc(S.xn_ready, 1)
                dve.wait_ge(S.xn_ready, b * 2 + 2 + BASE)
                for j in range(2):
                    dve.bn_stats(G.bn[:, bass.ds(b * 2 + j, 1), :].rearrange("p a s -> p (a s)"),
                                 xn[:, u, j]).then_inc(S.stats, 1)

            def rest_x(b, u):
                dve.wait_ge(S.x_hi, b + 1 + BASE)
                dve.tensor_tensor(xl[:, u], psT[:, :, :], xh[:, u], ALU.subtract).then_inc(S.x_lo, 1)

            def body(b, u):
                if not is_last(b, NB):
                    norm_block(b + 1, 1 - u)
                    rest_x(b + 1, 1 - u)
                for j in range(2):
                    t = b * 2 + j
                    dve.wait_ge(S.y2_hi, t + 1 + BASE)
                    dve.tensor_tensor(token_tile(G.Y2l, t), psY[1][j][:, :], token_tile(G.Y2h, t),
                                      ALU.subtract).then_inc(S.y2_lo, 1)
            norm_block(0, 0)
            rest_x(0, 0)
            for k in range(2):
                dve.wait_ge(S.w_hi, k + 1 + BASE)
                dve.tensor_tensor(wl[:, k], raw[k], wh[:, k], ALU.subtract).then_inc(S.w_lo, 1)
            loop(dve, NB, body, peel=1)

        @block.scalar
        def _(act):
            def split_w(k):
                act.wait_ge(w_in[k], 16 + BASE)
                act.activation(wh[:, k], raw[k], ACT.Copy).then_inc(S.w_hi, 1)

            def split_x(b, u):
                act.wait_ge(S.t_done, done(b) + BASE)
                act.activation(xh[:, u], psT[:, :, :], ACT.Copy).then_inc(S.x_hi, 1)

            def body(b, u):
                if not is_last(b, NB):
                    split_x(b + 1, 1 - u)
                for j in range(2):
                    t = b * 2 + j
                    act.wait_ge(S.y1_done, t + 1 + BASE)
                    act.activation(token_tile(G.Y1, t), psY[0][j][:, :], ACT.Copy).then_inc(S.y1_ready, 1)
                    act.wait_ge(S.y2_done, t + 1 + BASE)
                    act.activation(token_tile(G.Y2h, t), psY[1][j][:, :], ACT.Copy).then_inc(S.y2_hi, 1)
            split_x(0, 0)
            split_w(0)
            split_w(1)
            loop(act, NB, body, peel=1)

        @block.tensor
        def _(pe):
            lead(pe, S.t_done)

            def transposes(b, u):
                pe.wait_ge(S.xn_ready, b * 2 + 2 + BASE)
                pe.wait_ge(S.x_lo, b + BASE)
                for c in range(DC):
                    for j in range(2):
                        mm = pe.transpose(psT[:, c, j * P:(j + 1) * P], xn[:, u, j, c * P:(c + 1) * P], G.ident[:, :])
                mm.then_inc(S.t_done, 1)

            def body(b, u):
                if not is_last(b, NB):
                    transposes(b + 1, 1 - u)
                pe.wait_ge(S.x_lo, b + 1 + BASE)
                for j in range(2):
                    n = slice(j * P, (j + 1) * P)
                    for k, (free, sem) in enumerate(((S.y1_ready, S.y1_done), (S.y2_lo, S.y2_done))):
                        if isinstance(b, int) and b + j == 0:
                            pe.wait_ge(S.w_lo, k + 1 + BASE)
                        pe.wait_ge(free, b * 2 + BASE)
                        for c in range(DC):
                            for i, (x, wt) in enumerate(((xh, wh), (xh, wl), (xl, wh))):
                                mm = pe.matmul(psY[k][j][:, :], x[:, u, c, n], wt[:, k, c],
                                               start=(c + i == 0), stop=(c == DC - 1 and i == 2))
                        mm.then_inc(sem, 1)
            transposes(0, 0)
            loop(pe, NB, body, peel=1, head=2)


def neighbour_mean(nc, G):
    TCOLS = BUCKETS * 32
    with Phase(nc, "nmean") as ph:
        adj = ph.sb("adj", [P, 2, TCOLS], U16)
        ch, cl = (ph.sb(n, [P, 2, NT, P], F32R) for n in ("ch", "cl"))
        total = ph.sb("total", [P, 2, P])
        rdeg = ph.sb("rdeg", [P, 2])
        z = ph.sb("z", [P, 2, D])
        psZ = [ph.ps(f"psZ{i}", [P, D]) for i in range(2)]
        psD = [ph.ps(f"psD{i}", [P, 2]) for i in range(2)]
        names = "adj_in0 adj_in1 c_hi c_lo summed z_done deg_ready rdeg_ready z_ready x_ready".split()
        S = type("Sems", (), dict(zip(names, ph.sems(*names))))
        adj_in = (S.adj_in0, S.adj_in1)
        block = ph.block()

        def counts(u, g):
            return adj[:, u].rearrange("p (s q c) -> p s q c", q=4, c=32)[:, :, :, g * 16:(g + 1) * 16]

        def part(c, u, g):
            return c[:, u, :, g * GRAPH:(g + 1) * GRAPH].rearrange("p s (q r) -> p s q r", q=4)

        @block.sync
        def _(sp):
            def load(t, u):
                sp.wait_ge(S.summed, reuse(t) + BASE)
                sp.dma_start(adj[:, u], G.adj_dram[:, bass.ds(t * TCOLS, TCOLS)]).then_inc(adj_in[u], 16)
            loop(sp, NT, load)

        @block.scalar
        def _(act):
            def split(t, u):
                act.wait_ge(adj_in[u], (t - u) * 8 + 16 + BASE)
                act.wait_ge(S.z_done, reuse(t) + BASE)
                for g in range(2):
                    act.activation(part(ch, u, g), counts(u, g), ACT.Copy).then_inc(S.c_hi, 1)
            loop(act, NT, split)

        @block.vector
        def _(dve):
            lead(dve, S.summed)
            lead(dve, S.z_ready)

            def rest(t, u):
                for g in range(2):
                    dve.wait_ge(S.c_hi, t * 2 + g + 1 + BASE)
                    dve.tensor_tensor(part(cl, u, g), counts(u, g), part(ch, u, g), ALU.subtract).then_inc(S.c_lo, 1)
                dve.tensor_reduce(total[:, u].rearrange("p (g q r) -> p g q r", g=2, q=4),
                                  adj[:, u].rearrange("p (s q g r) -> p g q r s", q=4, g=2, r=16), AX.X,
                                  ALU.add).then_inc(S.summed, 1)

            def body(t, u):
                if not is_last(t, NT):
                    rest(t + 1, 1 - u)
                dve.wait_ge(S.z_done, done(t) + BASE)
                dve.tensor_scalar(rdeg[:, 0:1], psD[u][:, 0:1], 1.0, None, ALU.max).then_inc(S.deg_ready, 1)
                dve.wait_ge(S.deg_ready, t + 1 + BASE)
                dve.reciprocal(rdeg[:, 1:2], rdeg[:, 0:1]).then_inc(S.rdeg_ready, 1)
                dve.wait_ge(S.rdeg_ready, t + 1 + BASE)
                dve.scalar_tensor_tensor(out=z[:, u], in0=psZ[u][:, :], scalar=rdeg[:, 1:2], in1=token_tile(G.Y1, t),
                                         op0=ALU.mult, op1=ALU.add).then_inc(S.z_ready, 1)
                dve.wait_ge(S.z_ready, done(t) + BASE)
                dve.scalar_tensor_tensor(out=token_tile(G.X, t), in0=z[:, u], scalar=0.0, in1=token_tile(G.X, t),
                                         op0=ALU.max, op1=ALU.add).then_inc(S.x_ready, 1)
            rest(0, 0)
            loop(dve, NT, body, peel=2)

        @block.tensor
        def _(pe):
            lead(pe, S.z_done)

            def body(t, u):
                pe.wait_ge(S.c_lo, t * 2 + 2 + BASE)
                pe.wait_ge(S.z_ready, reuse(t) + BASE)
                for s in range(NT):
                    for i, (c, y) in enumerate(((ch, G.Y2h), (ch, G.Y2l), (cl, G.Y2h))):
                        pe.matmul(psZ[u][:, :], c[:, u, s], y[:, s], start=(s + i == 0), stop=(s == NT - 1 and i == 2))
                pe.wait_ge(S.summed, done(t) + BASE)
                pe.matmul(psD[u][:, :], total[:, u], G.ones[:, 0:2], start=True, stop=True).then_inc(S.z_done, 1)
            loop(pe, NT, body)


def flow_projections(nc, G, w):
    with Phase(nc, "fproj") as ph:
        wq, wk, wv = (ph.sb(n, [P, DC, D]) for n in ("wq", "wk", "wv"))
        bq, bk, g1, be1 = (ph.sb(n, [P, DC]) for n in ("bq", "bk", "g1", "be1"))
        bv = ph.sb("bv", [P, D])
        ln = ln_stats_buffers(ph)
        xin = ph.sb("xin", [P, 2, 2, D])
        xn = ph.sb("xn", [P, 2, 2, D])
        xnT = ph.sb("xnT", [P, 2, DC, BLK])
        part = ph.sb("part", [P, 2, DC, NB])
        psT = ph.ps("psT", [P, DC, BLK])
        psQ = [ph.ps(f"psQ{i}", [P, DC, BLK]) for i in range(2)]
        psV = [ph.ps(f"psV{i}", [P, D]) for i in range(2)]
        names = ("w_in wq_in wk_in wv_in x_in0 x_in1 xn_ready t_done xnT_ready q_done q_ready v_done v_ready "
                 "sums_ready").split()
        S = type("Sems", (), dict(zip(names, ph.sems(*names))))
        x_in = (S.x_in0, S.x_in1)
        block = ph.block()

        @block.sync
        def _(sp):
            for dst, name in ((bq, "F_bq"), (bk, "F_bk"), (g1, "g1"), (be1, "be1")):
                sp.dma_start(dst[:, :], w[name]).then_inc(S.w_in, 16)
            sp.dma_start(bv[:, :], w["F_bv"].partition_broadcast(P)).then_inc(S.w_in, 16)
            def load(b, u):
                sp.wait_ge(S.xn_ready, reuse(b, 2) + BASE)
                sp.dma_start(xin[:, u].rearrange("p j d -> p (j d)"),
                             G.xn_dram[:, bass.ds(b * 2 * D, 2 * D)]).then_inc(x_in[u], 16)
            load(0, 0)
            for dst, name, sem in ((wq, "F_Wq", S.wq_in), (wk, "F_Wk", S.wk_in), (wv, "F_Wv", S.wv_in)):
                sp.dma_start(dst[:, :, :], w[name].rearrange("(c p) n -> p c n", p=P)).then_inc(sem, 16)
            loop(sp, NB, load, head=2, done_steps=1)

        @block.gpsimd
        def _(pool):
            ln_stats_pool(pool, ln, G)

        @block.vector
        def _(dve):
            ln_stats_vector(dve, ln, G.bn)
            dve.wait_ge(S.w_in, 16 * 5 + BASE)
            lead(dve, S.xn_ready, 2)

            def norm_block(b, u):
                dve.wait_ge(x_in[u], (b - u) * 8 + 16 + BASE)
                dve.wait_ge(S.t_done, reuse(b) + BASE)
                for j in range(2):
                    t = b * 2 + j
                    dve.tensor_scalar(xn[:, u, j], xin[:, u, j], col(ln.rstd, t), col(ln.shift, t),
                                      ALU.mult, ALU.add).then_inc(S.xn_ready, 1)

            def body(b, u):
                if not is_last(b, NB):
                    norm_block(b + 1, 1 - u)
                for j in range(2):
                    t = b * 2 + j
                    dve.wait_ge(S.v_done, t + 1 + BASE)
                    dve.tensor_tensor(token_tile(G.V, t), psV[j][:, :], bv[:, :], ALU.add).then_inc(S.v_ready, 1)
            norm_block(0, 0)
            loop(dve, NB, body, peel=1)
            dve.wait_ge(S.q_ready, NB * 2 * DC + BASE)
            dve.tensor_reduce(G.qksum[:, :, :], part[:, :, :, :], AX.X, ALU.add).then_inc(S.sums_ready, 1)

        @block.scalar
        def _(act):
            act.wait_ge(S.w_in, 16 * 5 + BASE)

            def body(b, u):
                act.wait_ge(S.t_done, done(b) + BASE)
                for c in range(DC):
                    act.activation(xnT[:, u, c], psT[:, c], ACT.Identity, bias=be1[:, c:c + 1],
                                   scale=g1[:, c:c + 1]).then_inc(S.xnT_ready, 1)
                for k, (dst, bias) in enumerate(((G.Q, bq), (G.K, bk))):
                    for c in range(DC):
                        if c % 2 == 0:
                            act.wait_ge(S.q_done, b * 4 + k * 2 + c // 2 + 1 + BASE)
                        act.activation(dst[:, c, bass.ds(b * BLK, BLK)], psQ[k][:, c], ACT.Sigmoid,
                                       bias=bias[:, c:c + 1], accum_out=part[:, k, c, bass.ds(b, 1)]
                                       ).then_inc(S.q_ready, 1)
            loop(act, NB, body)

        @block.tensor
        def _(pe):
            lead(pe, S.t_done)

            def transposes(b, u):
                pe.wait_ge(S.xn_ready, (b + 1 + LEAD) * 2 + BASE)
                pe.wait_ge(S.xnT_ready, b * DC + BASE)
                for c in range(DC):
                    for j in range(2):
                        mm = pe.transpose(psT[:, c, j * P:(j + 1) * P], xn[:, u, j, c * P:(c + 1) * P], G.ident[:, :])
                mm.then_inc(S.t_done, 1)

            def body(b, u):
                pe.wait_ge(S.xnT_ready, b * DC + DC + BASE)
                for k, (wt, wt_in) in enumerate(((wq, S.wq_in), (wk, S.wk_in))):
                    if isinstance(b, int) and b == 0:
                        pe.wait_ge(wt_in, 16 + BASE)
                    pe.wait_ge(S.q_ready, b * 2 * DC + BASE)
                    for c in range(DC):
                        for d in range(DC):
                            mm = pe.matmul(psQ[k][:, c], wt[:, d, c * P:(c + 1) * P], xnT[:, u, d],
                                           start=(d == 0), stop=(d == DC - 1))
                        if c % 2:
                            mm.then_inc(S.q_done, 1)
                    if k == 0 and not is_last(b, NB):
                        transposes(b + 1, 1 - u)
                if isinstance(b, int) and b == 0:
                    pe.wait_ge(S.wv_in, 16 + BASE)
                for j in range(2):
                    pe.wait_ge(S.v_ready, b * 2 + j + BASE)
                    for d in range(DC):
                        mm = pe.matmul(psV[j][:, :], xnT[:, u, d, j * P:(j + 1) * P], wv[:, d], start=(d == 0),
                                       stop=(d == DC - 1))
                    mm.then_inc(S.v_done, 1)
            transposes(0, 0)
            loop(pe, NB, body, peel=1, head=2)


def flow_scan(nc, G, w):
    NBIG = N_TOK // D
    NX = NBIG * DC
    with Phase(nc, "fscan") as ph:
        wo = ph.sb("wo", [P, DC, D])
        sums = ph.sb("sums", [P, 4, DC])
        masked = ph.sb("masked", [P, 4, DC, HEADS])
        eps = ph.sb("eps", [P, 2])
        const = ph.sb("const", [HEADS, 4])
        rows = ph.sb("rows", [HEADS, 4, N_TOK])
        part = ph.sb("part", [P, 2, NBIG, DC])
        prod = ph.sb("prod", [P, 2, D])
        junk = ph.sb("junk", [P, D])
        stat = ph.sb("stat", [HEADS, 4])
        ke = ph.sb("ke", [P, DC, D])
        kt = prod
        kv = junk[:, :].rearrange("p (c n) -> p c n", c=PAIRS)
        kvT = ke[:, 0].rearrange("p (c n) -> p c n", c=PAIRS)
        psC = ph.ps("psC", [HEADS, 4, 2])
        psR = [ph.ps(f"psR{i}", [HEADS, D]) for i in range(2)]
        psX = [ph.ps(f"psX{i}", [P, D]) for i in range(2)]
        psT = [ph.ps(f"psT{i}", [P, D]) for i in range(2)]
        psK = ph.ps("psK", [P, PAIRS, P])
        names = ("w_in eps_ready kv_zero sum_step masked_ready c_done c_ready r_done r_ready rec_ready x_done x_used "
                 "summed step sig_ready exp_ready t_done kt_ready kv_done kv_ready kvT_done kvT_ready "
                 "m_done m_ready flow_ready passed passed_dve").split()
        S = type("Sems", (), dict(zip(names, ph.sems(*names))))
        block = ph.block()
        X_of = (G.Q, G.K, G.Q, G.K)

        @block.sync
        def _(sp):
            sp.dma_start(wo[:, :, :], w["F_Wo"].rearrange("(c p) n -> p c n", p=P)).then_inc(S.w_in, 16)

        @block.gpsimd
        def _(pool):
            pool.memset(eps[:, :], FLOW_EPS).then_inc(S.eps_ready, 1)
            pool.wait_ge(S.summed, done(2 * NX - 1) + BASE)
            pool.memset(junk[:, :], 0.0).then_inc(S.kv_zero, 1)

        @block.tensor
        def _(pe):
            pe.wait_ge(S.eps_ready, 1 + BASE)
            lead(pe, S.kv_done)

            def head_sums(i):
                pe.wait_ge(S.masked_ready, i + 1 + BASE)
                pe.wait_ge(S.c_ready, i + BASE)
                for c in range(DC):
                    mm = pe.matmul(psC[:, i], masked[:, i, c], eps[:, :], start=(c == 0), stop=(c == DC - 1))
                mm.then_inc(S.c_done, 1)

                def body(n, u):
                    pe.wait_ge(S.r_ready, reuse(n + i * NBIG) + BASE)
                    for c in range(DC):
                        mm = pe.matmul(psR[u][:, :], masked[:, i, c], X_of[i][:, c, bass.ds(n * D, D)],
                                       start=(c == 0), stop=(c == DC - 1))
                    mm.then_inc(S.r_done, 1)
                loop(pe, NBIG, body)

            def spread(k, row, n):
                for c in range(DC):
                    gate(pe, S.x_used, reuse(n * DC + c + k * NX), S.passed)
                    pe.matmul(psX[c % 2][:, :], G.rep[:, c], rows[:, row, bass.ds(n * D, D)], start=True,
                              stop=True).then_inc(S.x_done, 1)
            head_sums(0)
            head_sums(1)
            for row in range(2):
                pe.wait_ge(S.rec_ready, (row + 1) * NBIG + BASE)
                loop(pe, NBIG, lambda n, u: spread(row, row, n))
            head_sums(2)
            head_sums(3)
            pe.wait_ge(S.step, STEPS + BASE)

            def context(n, u):
                spread(2, 3, n)
                pe.wait_ge(S.x_used, done(n * DC + DC - 1 + 2 * NX) + BASE)
                for j in range(5):
                    t = n * 4 + j
                    if j < 4:
                        pe.wait_ge(S.kt_ready, reuse(t) + BASE)
                        for c in range(DC):
                            mm = pe.transpose(psT[j % 2][:, c * P:(c + 1) * P], ke[:, c, j * P:(j + 1) * P],
                                              G.ident[:, :])
                        mm.then_inc(S.t_done, 1)
                    if j:
                        pe.wait_ge(S.kt_ready, done(t - 1) + BASE)
                        for c in range(PAIRS):
                            mm = pe.matmul(psK[:, c], kt[:, (j - 1) % 2, c * P:(c + 1) * P],
                                           G.V[:, bass.ds(t - 1, 1), c * P:(c + 1) * P].rearrange("p a m -> p (a m)"),
                                           start=(isinstance(t, int) and t == 1 and c == 0),
                                           stop=is_last(t - 1, NT), skip_group_check=True)
                        mm.then_inc(S.kv_done, 1)
            for n in range(NBIG):
                context(n, n % 2)
            pe.wait_ge(S.kv_ready, 2 + BASE)
            for c in range(PAIRS):
                mm = pe.transpose(psT[0][:, c * P:(c + 1) * P], kv[:, c], G.ident[:, :])
            mm.then_inc(S.kvT_done, 1)
            pe.wait_ge(S.kvT_ready, 1 + BASE)
            pe.wait_ge(S.w_in, 16 + BASE)
            for c in range(PAIRS):
                if c >= 2:
                    pe.wait_ge(S.m_ready, c - 1 + BASE)
                pe.matmul(psX[c % 2][:, :], kvT[:, c], wo[:, c], start=True, stop=True).then_inc(S.m_done, 1)

        @block.vector
        def _(dve):
            lead(dve, S.r_ready)
            lead(dve, S.x_used)
            ss = Step(dve, S.sum_step, 0, 8)
            ss.did(dve.tensor_scalar(sums[:, 0], G.qksum[:, 1], FLOW_EPS, None, ALU.add))
            ss.do(dve.tensor_scalar(sums[:, 1], G.qksum[:, 0], FLOW_EPS, None, ALU.add))

            def mask(i):
                dve.tensor_tensor(masked[:, i], G.sel[:, :, :], sums[:, i].unsqueeze(2).to_broadcast([P, DC, HEADS]),
                                  ALU.mult).then_inc(S.masked_ready, 1)

            def take(i, invert):
                dve.wait_ge(S.c_done, i + 1 + BASE)
                dve.tensor_copy(const[:, i:i + 1], psC[:, i, 0:1]).then_inc(S.c_ready, 1)
                dve.wait_ge(S.c_ready, i + 1 + BASE)

                def body(n, u):
                    m = n + i * NBIG
                    r = rows[:, i, bass.ds(n * D, D)]
                    dve.wait_ge(S.r_done, m + 1 + BASE)
                    dve.tensor_scalar(r, psR[u][:, :], const[:, i:i + 1], None, ALU.add).then_inc(S.r_ready, 1)
                    if invert:
                        gate(dve, S.r_ready, done(m), S.passed_dve)
                        dve.reciprocal(r, r).then_inc(S.rec_ready, 1)
                loop(dve, NBIG, body)

            def weigh(row, X):
                def body(n, u):
                    for c in range(DC):
                        m = n * DC + c + row * NX
                        dve.wait_ge(S.x_done, m + 1 + BASE)
                        dve.wait_ge(S.summed, reuse(m) + BASE)
                        dve.tensor_tensor(prod[:, c % 2], X[:, c, bass.ds(n * D, D)], psX[c % 2][:, :],
                                          ALU.mult).then_inc(S.x_used, 1)
                loop(dve, NBIG, body)
            mask(0)
            mask(1)
            take(0, True)
            take(1, True)
            weigh(0, G.Q)
            weigh(1, G.K)
            dve.wait_ge(S.summed, done(2 * NX - 1) + BASE)
            for i, k in ((2, 1), (3, 0)):
                ss.do(dve.tensor_reduce(sums[:, i], part[:, k].rearrange("p n c -> p c n"), AX.X, ALU.add))
                ss.do(dve.tensor_scalar(sums[:, i], sums[:, i], FLOW_EPS, None, ALU.add))
                mask(i)
            take(2, False)
            take(3, False)
            st = Step(dve, S.step, 0, STEPS)
            dve.wait_ge(S.r_ready, done(4 * NBIG - 1) + BASE)
            st.do(dve.tensor_scalar(rows[:, 3], rows[:, 3], -1.0, 1.0, ALU.max, ALU.min))
            st.do(dve.tensor_reduce(stat[:, 0:1], rows[:, 3], AX.X, ALU.max))
            st.do(dve.tensor_scalar(stat[:, 1:2], stat[:, 0:1], -1.0, None, ALU.mult))
            dve.wait_ge(S.exp_ready, 1 + BASE)
            st.do(dve.reciprocal(stat[:, 3:4], stat[:, 2:3]))
            st.do(dve.tensor_scalar(rows[:, 3], rows[:, 3], stat[:, 3:4], float(N_TOK), ALU.mult, ALU.mult))
            dve.wait_ge(S.sig_ready, 1 + BASE)
            dve.tensor_tensor(G.flow[:, :], rows[:, 0], rows[:, 2], ALU.mult).then_inc(S.flow_ready, 1)

            def compete(n, u):
                for c in range(DC):
                    m = n * DC + c + 2 * NX
                    dve.wait_ge(S.x_done, m + 1 + BASE)
                    if c == 0:
                        dve.wait_ge(S.t_done, n * 4 + BASE)
                    dve.tensor_tensor(ke[:, c], G.K[:, c, bass.ds(n * D, D)], psX[c % 2][:, :], ALU.mult)\
                        .then_inc(S.x_used, 1)
            loop(dve, NBIG, compete)
            dve.wait_ge(S.kv_done, done(NT - 1) + BASE)
            dve.wait_ge(S.kv_zero, 1 + BASE)
            for h in (slice(0, DH), slice(DH, P)):
                dve.tensor_copy(kv[h, :, h], psK[h, :, h]).then_inc(S.kv_ready, 1)

        @block.scalar
        def _(act):
            lead(act, S.summed)
            lead(act, S.kt_ready)
            for k in range(2):
                def body(n, u):
                    for c in range(DC):
                        m = n * DC + c + k * NX
                        act.wait_ge(S.x_used, done(m) + BASE)
                        act.wait_ge(S.summed, m + LEAD + BASE)
                        act.activation(junk[:, :], prod[:, c % 2], ACT.Copy,
                                       accum_out=part[:, k, bass.ds(n, 1), c]).then_inc(S.summed, 1)
                loop(act, NBIG, body)
            act.wait_ge(S.r_ready, done(3 * NBIG - 1) + BASE)
            act.activation(rows[:, 2], rows[:, 2], ACT.Sigmoid).then_inc(S.sig_ready, 1)
            act.wait_ge(S.step, 3 + BASE)
            act.activation(rows[:, 3], rows[:, 3], ACT.Exp, bias=stat[:, 1:2],
                           accum_out=stat[:, 2:3]).then_inc(S.exp_ready, 1)

            def turn(n, u):
                for j in range(4):
                    t = n * 4 + j
                    act.wait_ge(S.t_done, t + 1 + BASE)
                    act.wait_ge(S.kv_done, reuse(t) + BASE)
                    act.activation(kt[:, j % 2], psT[j % 2][:, :], ACT.Copy).then_inc(S.kt_ready, 1)
            loop(act, NBIG, turn)
            act.wait_ge(S.kvT_done, 1 + BASE)
            act.activation(ke[:, 0], psT[0][:, :], ACT.Copy).then_inc(S.kvT_ready, 1)
            for c in range(PAIRS):
                act.wait_ge(S.m_done, c + 1 + BASE)
                act.activation(G.M[:, c], psX[c % 2][:, :], ACT.Copy).then_inc(S.m_ready, 1)


STEPS = 5


def flow_output(nc, G, w):
    FM = 2
    with Phase(nc, "fout") as ph:
        w1 = ph.sb("w1", [P, DC, FM * P])
        w2 = ph.sb("w2", [P, FM, D])
        b1 = ph.sb("b1", [P, FM])
        g2, be2 = (ph.sb(n, [P, DC]) for n in ("g2", "be2"))
        bo, b2 = (ph.sb(n, [P, D]) for n in ("bo", "b2"))
        qf = ph.sb("qf", [P, 2, DC, BLK])
        xin = ph.sb("xin", [P, 2, 2, D])
        x1 = ph.sb("x1", [P, 2, 2, D])
        bn = ph.sb("bn", [P, 2, 6])
        mv = ph.sb("mv", [P, 2, 2])
        rstd = ph.sb("rstd", [P, 2])
        hn = ph.sb("hn", [P, 2, 2, D])
        hT = ph.sb("hT", [P, DC, BLK])
        hid = ph.sb("hid", [P, 2, FM, BLK])
        psX = ph.ps("psX", [P, DC, BLK])
        psO = [ph.ps(f"psO{i}", [P, D]) for i in range(2)]
        psT = ph.ps("psT", [P, DC, BLK])
        psH = ph.ps("psH", [P, FM, BLK])
        psY = (ph.ps("psY", [P, D])[:, :], psH[:, :, :].rearrange("p f n -> p (f n)"))
        names = ("w_in x_in0 x_in1 x_done qf_ready o_done xo_ready x1_ready bn_ready mv_ready rstd_ready hn_ready "
                 "t_done hT_ready hid_done hid_ready y_done y1_ready y2_ready xr_ready passed passed_pe "
                 "passed_pool stats").split()
        S = type("Sems", (), dict(zip(names, ph.sems(*names))))
        x_in = (S.x_in0, S.x_in1)
        block = ph.block()

        @block.sync
        def _(sp):
            sp.dma_start(w1[:, :, :], w["F_W1"].rearrange("(c p) n -> p c n", p=P)).then_inc(S.w_in, 16)
            sp.dma_start(w2[:, :, :], w["F_W2"].rearrange("(c p) n -> p c n", p=P)).then_inc(S.w_in, 16)
            for dst, name in ((b1, "F_b1"), (g2, "g2"), (be2, "be2")):
                sp.dma_start(dst[:, :], w[name]).then_inc(S.w_in, 16)
            for dst, name in ((bo, "F_bo"), (b2, "F_b2")):
                sp.dma_start(dst[:, :], w[name].partition_broadcast(P)).then_inc(S.w_in, 16)

            def load(b, u):
                sp.wait_ge(S.xo_ready, reuse(b, 2) + BASE)
                sp.dma_start(xin[:, u].rearrange("p j d -> p (j d)"),
                             G.xn_dram[:, bass.ds(b * 2 * D, 2 * D)]).then_inc(x_in[u], 16)
            loop(sp, NB, load)

        @block.gpsimd
        def _(pool):
            def power(t, u):
                gate(pool, S.mv_ready, t + 1, S.passed_pool)
                pool.tensor_tensor(rstd[:, u:u + 1], mv[:, u, 1:2], G.minus_half[:, 0:1],
                                   ALU.pow).then_inc(S.rstd_ready, 1)
            loop(pool, NT, power)

        @block.vector
        def _(dve):
            dve.wait_ge(S.w_in, 16 * 7 + BASE)
            lead(dve, S.xo_ready, 2)
            lead(dve, S.xr_ready, 2)

            def first(b, u):
                dve.wait_ge(S.x_done, b + 1 + BASE)
                dve.wait_ge(S.o_done, reuse(b, 2) + BASE)
                dve.tensor_tensor(qf[:, u], G.Q[:, :, bass.ds(b * BLK, BLK)], psX[:, :, :],
                                  ALU.mult).then_inc(S.qf_ready, 1)
                dve.wait_ge(x_in[u], (b - u) * 8 + 16 + BASE)
                dve.wait_ge(S.xr_ready, reuse(b, 2) + BASE)
                for j in range(2):
                    t = b * 2 + j
                    x = x1[:, u, j]
                    dve.wait_ge(S.o_done, t + 1 + 2 * LEAD + BASE)
                    dve.tensor_tensor(x, xin[:, u, j], psO[j][:, :], ALU.add).then_inc(S.xo_ready, 1)
                    dve.wait_ge(S.xo_ready, t + 1 + 2 * LEAD + BASE)
                    dve.tensor_tensor(x, x, bo[:, :], ALU.add).then_inc(S.x1_ready, 1)
                    dve.wait_ge(S.x1_ready, t + 1 + BASE)
                    dve.bn_stats(bn[:, j], x).then_inc(S.bn_ready, 1)
                    gate(dve, S.bn_ready, t + 1, S.passed)
                    dve.bn_aggr(mv[:, j], bn[:, j]).then_inc(S.passed, 1)
                    dve.wait_ge(S.passed, t * 2 + 2 + BASE)
                    dve.tensor_scalar(mv[:, j, 1:2], mv[:, j, 1:2], LN_EPS, None, ALU.add).then_inc(S.mv_ready, 1)
                for j in range(2):
                    t = b * 2 + j
                    dve.wait_ge(S.rstd_ready, t + 1 + BASE)
                    dve.tensor_scalar(hn[:, u, j], x1[:, u, j], mv[:, j, 0:1], rstd[:, j:j + 1], ALU.subtract,
                                      ALU.mult).then_inc(S.hn_ready, 1)

            def second(b, u):
                for j in range(2):
                    t = b * 2 + j
                    x = x1[:, u, j]
                    dve.tensor_tensor(x, x, b2[:, :], ALU.add).then_inc(S.y1_ready, 1)
                    dve.wait_ge(S.y_done, t + 1 + BASE)
                    dve.wait_ge(S.y1_ready, t + 1 + BASE)
                    dve.tensor_tensor(x, x, psY[j], ALU.add).then_inc(S.y2_ready, 1)
                    dve.wait_ge(S.y2_ready, t + 1 + BASE)
                    dve.tensor_tensor(token_tile(G.X, t), token_tile(G.X, t), x, ALU.add).then_inc(S.xr_ready, 1)
                    dve.wait_ge(S.xr_ready, t + 1 + 2 * LEAD + BASE)
                    tile_stats(dve, G, t).then_inc(S.stats, 1)

            def body(b, u):
                if not is_last(b, NB):
                    first(b + 1, 1 - u)
                second(b, u)
            first(0, 0)
            loop(dve, NB, body, peel=1)

        @block.scalar
        def _(act):
            act.wait_ge(S.w_in, 16 * 7 + BASE)

            def body(b, u):
                act.wait_ge(S.t_done, done(b) + BASE)
                act.wait_ge(S.hid_done, b + BASE)
                for c in range(DC):
                    act.activation(hT[:, c], psT[:, c], ACT.Identity, bias=be2[:, c:c + 1],
                                   scale=g2[:, c:c + 1]).then_inc(S.hT_ready, 1)
                act.wait_ge(S.hid_done, b + 1 + BASE)
                for f in range(FM):
                    act.activation(hid[:, u, f], psH[:, f], ACT.Gelu, bias=b1[:, f:f + 1]).then_inc(S.hid_ready, 1)
            loop(act, NB, body)

        @block.tensor
        def _(pe):
            pe.wait_ge(S.w_in, 16 * 7 + BASE)
            lead(pe, S.o_done, 2)
            lead(pe, S.t_done)

            def spread(b, u):
                gate(pe, S.qf_ready, b, S.passed_pe)
                for c in range(DC):
                    mm = pe.matmul(psX[:, c], G.rep[:, c], G.flow[:, bass.ds(b * BLK, BLK)], start=True, stop=True)
                mm.then_inc(S.x_done, 1)

            def attended(b, u):
                pe.wait_ge(S.qf_ready, b + 1 + BASE)
                for j in range(2):
                    pe.wait_ge(S.xo_ready, b * 2 + j - 1 + 2 * LEAD + BASE)
                    for c in range(DC):
                        mm = pe.matmul(psO[j][:, :], qf[:, u, c, j * P:(j + 1) * P], G.M[:, c], start=(c == 0),
                                       stop=(c == DC - 1))
                    mm.then_inc(S.o_done, 1)

            def transposes(b, u):
                pe.wait_ge(S.hn_ready, b * 2 + 2 + BASE)
                pe.wait_ge(S.hT_ready, b * DC + BASE)
                for c in range(DC):
                    for j in range(2):
                        mm = pe.transpose(psT[:, c, j * P:(j + 1) * P], hn[:, u, j, c * P:(c + 1) * P], G.ident[:, :])
                mm.then_inc(S.t_done, 1)

            def hidden(b, u):
                pe.wait_ge(S.hT_ready, b * DC + DC + BASE)
                pe.wait_ge(S.y2_ready, b * 2 + BASE)
                for f in range(FM):
                    for c in range(DC):
                        mm = pe.matmul(psH[:, f], w1[:, c, f * P:(f + 1) * P], hT[:, c], start=(c == 0),
                                       stop=(c == DC - 1))
                mm.then_inc(S.hid_done, 1)

            def outputs(b, u):
                pe.wait_ge(S.hid_ready, b * FM + FM + BASE)
                pe.wait_ge(S.y2_ready, b * 2 + BASE)
                for j in range(2):
                    for f in range(FM):
                        mm = pe.matmul(psY[j], hid[:, u, f, j * P:(j + 1) * P], w2[:, f], start=(f == 0),
                                       stop=(f == FM - 1))
                    mm.then_inc(S.y_done, 1)

            def body(b, u):
                transposes(b, u)
                if not is_last(b, NB):
                    spread(b + 1, 1 - u)
                hidden(b, u)
                if not is_last(b, NB):
                    attended(b + 1, 1 - u)
                outputs(b, u)
            spread(0, 0)
            attended(0, 0)
            loop(pe, NB, body, peel=1)


def program(nc, w, out):
    G = type("Shared", (), {})()

    def scratch(name, shape, dt=F32):
        return nc.dram_tensor(name, shape, dt, kind="Internal").ap()

    with ExitStack() as ctx:
        def sb(name, shape, dt=F32):
            return ctx.enter_context(nc.sbuf_tensor(name, shape, dt))

        G.X = sb("X", [P, NT, D])
        G.ident = sb("ident", [P, P])
        G.upper = sb("upper", [P, P])
        G.ones = sb("ones", [P, P])
        G.headmask = sb("headmask", [P, P])
        G.iota512 = sb("iota512", [P, ACOLS])
        G.part = sb("part", [P, 1])
        G.minus_half = sb("minus_half", [P, NT])
        G.edge_bucket = sb("edge_bucket", [P, NG], I32)
        G.edge_end = sb("edge_end", [P, BUCKETS])
        G.bn = sb("bn", [P, NT, 6])
        G.place = sb("place", [P, TOPK * NT], I32)
        G.wrow = sb("wrow", [P, NST], I32)
        G.wnew = sb("wnew", [P, NST], I32)
        G.gate = sb("gate", [P, NT, TOPK])
        G.comb = sb("comb", [P, NT, EXPERTS])
        G.rec_dram = scratch("rec_dram", [P * NCH, REC])
        G.adj_dram = scratch("adj_dram", [P, BUCKETS * ACOLS], U16)
        G.xnT_dram = scratch("xnT_dram", [P, NB * DC * BLK])
        G.q_dram = scratch("q_dram", [P, NB * DC * BLK])
        G.m_dram = scratch("m_dram", [P, PAIRS * D])
        G.xn_dram = scratch("xn_dram", [P, NT * D])
        G.xs_dram = scratch("xs_dram", [SLOTS, D])
        G.ys_dram = scratch("ys_dram", [SLOTS, D])
        constants(nc, G)
        with ExitStack() as layer:
            with nc.sbuf_tensor("rec", [P, EJ, REC], F32) as G.rec, \
                    nc.sbuf_tensor("rec_place", [P, EJ], I32) as G.rec_place:
                sort_edges(nc, G, w)
                linear_attention_scan(nc, G, w)
            G.BIAS = layer.enter_context(nc.sbuf_tensor("BIAS", [P, BUCKETS * BCOLS], F32))
            W = AttentionWeights(nc, layer)
            build_graph(nc, G, w, W)
            graph_attention(nc, G, W)
        with ExitStack() as moe:
            E = ExpertWeights(nc, moe, "A_", 1024)
            route(nc, G, w, "A_", False, E)
            experts(nc, G, w, "A_", E)
        combine(nc, G, w, "A_", None)
        with nc.sbuf_tensor("Y1", [P, NT, D], F32) as G.Y1, nc.sbuf_tensor("Y2h", [P, NT, D], F32R) as G.Y2h, \
                nc.sbuf_tensor("Y2l", [P, NT, D], F32R) as G.Y2l:
            neighbour_products(nc, G, w)
            neighbour_mean(nc, G)
        with nc.sbuf_tensor("M1", [P, PAIRS, D], F32) as G.M, nc.sbuf_tensor("Q1", [P, DC, N_TOK], F32) as G.Q, \
                nc.sbuf_tensor("flow", [HEADS, N_TOK], F32) as G.flow, \
                nc.sbuf_tensor("sel", [P, DC, HEADS], F32) as G.sel, \
                nc.sbuf_tensor("rep", [HEADS, DC, P], F32) as G.rep:
            head_rows(nc, G)
            with nc.sbuf_tensor("K", [P, DC, N_TOK], F32) as G.K, nc.sbuf_tensor("V", [P, NT, D], F32) as G.V, \
                    nc.sbuf_tensor("qksum", [P, 2, DC], F32) as G.qksum:
                flow_projections(nc, G, w)
                flow_scan(nc, G, w)
            flow_output(nc, G, w)
        with ExitStack() as moe:
            E = ExpertWeights(nc, moe, "B_", 256)
            route(nc, G, w, "B_", True, E)
            experts(nc, G, w, "B_", E)
        combine(nc, G, w, "B_", out)


def layouts(inputs):
    import numpy as np

    def chunks(b):
        return b.reshape(-1, P).T

    a = {k: np.asarray(v) for k, v in inputs.items()}
    wqkv = a["L0_mix_w_qkv"]
    out = {"x": a["x"], "src": a["src"], "dst": a["dst"], "edge_attr": a["edge_attr_16"],
           "We": a["L0_gnn_We"], "be": a["L0_gnn_be"],
           "mix_wq": wqkv[:D].T, "mix_wk": wqkv[D:2 * D].T, "mix_wv": wqkv[2 * D:].T,
           "mix_wo": a["L0_mix_w_out"].T, "b_out": a["L0_mix_b_out"],
           "bq": chunks(a["L0_gnn_bq"]), "bk": chunks(a["L0_gnn_bk"]), "gw": a["L1_gnn_w"].T}
    for n in ("Wq", "Wk", "Wv", "Wo", "bv", "bo"):
        out[n] = a["L0_gnn_" + n]
    for n in ("Wq", "Wk", "Wv", "Wo", "W1", "W2", "bv", "bo", "b2"):
        out["F_" + n] = a["L1_mix_" + n]
    for n in ("bq", "bk", "b1"):
        out["F_" + n] = chunks(a["L1_mix_" + n])
    for n in ("g1", "be1", "g2", "be2"):
        out[n] = chunks(a["L1_mix_" + n])

    def moe(pre, w1, b1, w2, b2, wr, br):
        E, _, F = w1.shape
        out[pre + "W1"] = w1.reshape(E, DC, P, F).transpose(0, 2, 1, 3).reshape(E * P, DC * F)
        out[pre + "W2"] = w2.reshape(E, F // P, P, D).transpose(0, 2, 1, 3).reshape(E * P, F // P * D)
        out[pre + "b1"] = b1.reshape(E, F // P, P).transpose(0, 2, 1).reshape(E * P, F // P)
        out[pre + "b2"], out[pre + "Wr"], out[pre + "br"] = b2, wr.T, br

    moe("A_", *(a["L0_ffn_" + n] for n in ("W1", "b1", "W2", "b2", "Wr", "br")))
    moe("B_", a["L1_ffn_rw1"].transpose(0, 2, 1), a["L1_ffn_rb1"], a["L1_ffn_rw2"].transpose(0, 2, 1),
        a["L1_ffn_rb2"], a["L1_ffn_gate_w"], a["L1_ffn_gate_b"])
    out["sw1"] = a["L1_ffn_sw1"].transpose(2, 0, 1).reshape(D, -1)
    out["sw2"] = a["L1_ffn_sw2"].transpose(0, 2, 1).reshape(-1, D)
    out["sb1"], out["sb2"] = chunks(a["L1_ffn_sb1"].reshape(-1)), a["L1_ffn_sb2"]
    return {k: np.ascontiguousarray(v) for k, v in out.items()}


def kernel(**inputs):
    import concourse.bacc as _bacc
    from concourse.bass_utils import run_bass_kernel_spmd as _run

    nc = _bacc.Bacc("TRN2", target_bir_lowering=False, num_devices=1)
    arrays = layouts(inputs)
    w = {k: nc.dram_tensor("in_" + k, v.shape, mybir.dt.from_np(v.dtype), kind="ExternalInput").ap()
         for k, v in arrays.items()}
    out = nc.dram_tensor("out", (N_TOK, D), F32, kind="ExternalOutput").ap()
    program(nc, w, out)
    r = _run(nc, [{"in_" + k: v for k, v in arrays.items()}], core_ids=[0])
    return r.results[0]["out"]
```
